# Optimizing a Trainium2 kernel written in Bass

```python
import numpy as np
import jax
import jax.numpy as jnp

def _softmax(x, axis=-1):
    return jax.nn.softmax(x, axis=axis)

def _gelu(x):
    return jax.nn.gelu(x, approximate=True)

def _silu(x):
    return jax.nn.silu(x)

def _sigmoid(x):
    return jax.nn.sigmoid(x)

def _layernorm(x, axis=-1, eps=1e-05):
    m = jnp.mean(x, axis=axis, keepdims=True)
    v = jnp.var(x, axis=axis, keepdims=True)
    return (x - m) / jnp.sqrt(v + eps)

def _scatter_add(tgt, idx, src, axis=0):
    return tgt.at[idx].add(src)

def _segment_sum(src, seg, n):
    return jax.ops.segment_sum(src, seg, n)
kernel_name = 'mk_vit_tower_d2_tok_img1024_r4_b74220'

def setup_inputs(seed: int=0):
    np.random.seed(seed)
    _w = jnp.asarray

    def _rec_inputs():
        import jax
        import jax.numpy as jnp
        _rk = jax.random.key(seed)
        x = -0.000222058 + 0.999998 * jax.random.normal(jax.random.fold_in(_rk, 1), (16, 3, 96, 96), jnp.float32)
        return x
    x = _rec_inputs()

    def _L0_tok_setup():
        import jax, jax.numpy as jnp
        import numpy as np
        P = 16
        C = 3
        D = 256

        def _patchify(x, p):
            B, Cc, H, W = x.shape
            gh, gw = (H // p, W // p)
            x = x.reshape(B, Cc, gh, p, gw, p)
            x = x.transpose(0, 2, 4, 1, 3, 5)
            return x.reshape(B, gh * gw, Cc * p * p)
        key = jax.random.key(seed)
        k1, k2, k3, k4, k5 = jax.random.split(key, 5)
        patch_dim = C * P * P
        s1 = 1.0 / np.sqrt(patch_dim)
        s2 = 1.0 / np.sqrt(D)
        return {'x': jax.random.normal(k1, (32, C, 128, 128), dtype=jnp.float32), 'W1': jax.random.uniform(k2, (patch_dim, D), jnp.float32, -s1, s1), 'b1': jax.random.uniform(k3, (D,), jnp.float32, -s1, s1), 'W2': jax.random.uniform(k4, (D, D), jnp.float32, -s2, s2), 'b2': jax.random.uniform(k5, (D,), jnp.float32, -s2, s2)}
    _L0_tok_all = _L0_tok_setup()
    _L0_tok_in = {k: v for k, v in _L0_tok_all.items() if k in ('W1', 'b1', 'W2', 'b2')}
    del _L0_tok_all

    def _L0_attn_setup():
        import jax, jax.numpy as jnp
        import numpy as np
        D_MODEL = 256
        N_HEAD = 16
        HEAD_D = D_MODEL // N_HEAD
        D_FF = 1024
        LN_EPS = 1e-05
        ATTN_EPS = 1e-06

        def _layer_norm(x, g, b, eps=LN_EPS):
            mu = jnp.mean(x, axis=-1, keepdims=True)
            var = jnp.var(x, axis=-1, keepdims=True)
            return (x - mu) * jax.lax.rsqrt(var + eps) * g + b

        def _linear_attention(x, qkv_w, qkv_b, out_w, out_b):
            B, N, C = x.shape
            qkv = (x @ qkv_w + qkv_b).reshape(B, N, 3, N_HEAD, HEAD_D)
            qkv = jnp.transpose(qkv, (2, 0, 3, 1, 4))
            q, k, v = (qkv[0], qkv[1], qkv[2])
            qf = jax.nn.elu(q) + 1.0
            kf = jax.nn.elu(k) + 1.0
            kv = jnp.einsum('bhnd,bhne->bhde', kf.astype(jnp.float32), v.astype(jnp.float32)).astype(v.dtype)
            y_num = jnp.einsum('bhnd,bhde->bhne', qf, kv)
            z = jnp.sum(kf.astype(jnp.float32), axis=2)
            y_den = jnp.einsum('bhnd,bhd->bhn', qf, z.astype(qf.dtype))
            y_den = jnp.maximum(y_den, ATTN_EPS)[..., None]
            y = (y_num / y_den).transpose(0, 2, 1, 3).reshape(B, N, C)
            return y @ out_w + out_b
        key = jax.random.key(seed)
        ks = jax.random.split(key, 16)
        s = 0.02
        return {'src': jax.random.normal(ks[0], (4, 1024, D_MODEL), dtype=jnp.float32), 'qkv_w': jax.random.normal(ks[1], (D_MODEL, 3 * D_MODEL), dtype=jnp.float32) * s, 'qkv_b': jax.random.normal(ks[2], (3 * D_MODEL,), dtype=jnp.float32) * s, 'out_w': jax.random.normal(ks[3], (D_MODEL, D_MODEL), dtype=jnp.float32) * s, 'out_b': jax.random.normal(ks[4], (D_MODEL,), dtype=jnp.float32) * s, 'w1': jax.random.normal(ks[5], (D_MODEL, D_FF), dtype=jnp.float32) * s, 'b1': jax.random.normal(ks[6], (D_FF,), dtype=jnp.float32) * s, 'w2': jax.random.normal(ks[7], (D_FF, D_MODEL), dtype=jnp.float32) * s, 'b2': jax.random.normal(ks[8], (D_MODEL,), dtype=jnp.float32) * s, 'g1': jnp.ones((D_MODEL,), dtype=jnp.float32), 'be1': jnp.zeros((D_MODEL,), dtype=jnp.float32), 'g2': jnp.ones((D_MODEL,), dtype=jnp.float32), 'be2': jnp.zeros((D_MODEL,), dtype=jnp.float32)}
    _L0_attn_all = _L0_attn_setup()
    _L0_attn_in = {k: v for k, v in _L0_attn_all.items() if k in ('qkv_w', 'qkv_b', 'out_w', 'out_b', 'w1', 'b1', 'w2', 'b2', 'g1', 'be1', 'g2', 'be2')}
    del _L0_attn_all

    def _L0_ffn_setup():
        import jax, jax.numpy as jnp
        import numpy as np
        H_DIM, E_DIM = (256, 128)
        N_SHARED, N_ROUTED, TOP_K = (2, 16, 4)
        B, S = (4, 512)
        key = jax.random.key(seed)
        ks = jax.random.split(key, 6)
        sc = 1.0 / np.sqrt(H_DIM)
        ec = 1.0 / np.sqrt(E_DIM)
        return {'x': jax.random.normal(ks[0], (B, S, H_DIM), dtype=jnp.float32), 'shared_up': jax.random.uniform(ks[1], (N_SHARED, E_DIM, H_DIM), jnp.float32, -sc, sc), 'shared_down': jax.random.uniform(ks[2], (N_SHARED, H_DIM, E_DIM), jnp.float32, -ec, ec), 'routed_up': jax.random.uniform(ks[3], (N_ROUTED, E_DIM, H_DIM), jnp.float32, -sc, sc), 'routed_down': jax.random.uniform(ks[4], (N_ROUTED, H_DIM, E_DIM), jnp.float32, -ec, ec), 'router_w': jax.random.uniform(ks[5], (N_ROUTED, H_DIM), jnp.float32, -sc, sc)}
    _L0_ffn_all = _L0_ffn_setup()
    _L0_ffn_in = {k: v for k, v in _L0_ffn_all.items() if k in ('shared_up', 'shared_down', 'routed_up', 'routed_down', 'router_w')}
    del _L0_ffn_all

    def _L1_attn_setup():
        import jax, jax.numpy as jnp
        import numpy as np
        import math
        N, S, E, H = (4, 1024, 256, 16)
        D = E // H
        key = jax.random.key(seed)
        ks = jax.random.split(key, 9)
        w = 1.0 / math.sqrt(E)
        mk = lambda k, shape: jax.random.normal(k, shape, jnp.float32) * w
        return {'x': jax.random.normal(ks[0], (N, S, E), jnp.float32), 'Wq': mk(ks[1], (E, E)), 'bq': mk(ks[2], (E,)), 'Wk': mk(ks[3], (E, E)), 'bk': mk(ks[4], (E,)), 'Wv': mk(ks[5], (E, E)), 'bv': mk(ks[6], (E,)), 'Wo': mk(ks[7], (E, E)), 'bo': mk(ks[8], (E,))}
    _L1_attn_all = _L1_attn_setup()
    _L1_attn_in = {k: v for k, v in _L1_attn_all.items() if k in ('Wq', 'bq', 'Wk', 'bk', 'Wv', 'bv', 'Wo', 'bo')}
    del _L1_attn_all

    def _L1_ffn_setup():
        import jax, jax.numpy as jnp
        import numpy as np
        B, S, D = (8, 128, 256)
        H = 16
        DFF = 1024
        E = 4
        K = 2
        EPS = 1e-05

        def _layernorm(x, w, b):
            m = x.mean(-1, keepdims=True)
            v = ((x - m) ** 2).mean(-1, keepdims=True)
            return (x - m) / jnp.sqrt(v + EPS) * w + b

        def _encoder_layer(x, iw, ib, ow, ob, l1w, l1b, l2w, l2b, n1w, n1b, n2w, n2b):
            b, s, d = x.shape
            hd = d // H
            qkv = x @ iw.T + ib
            q, k, v = jnp.split(qkv, 3, axis=-1)
            rs = lambda t: t.reshape(b, s, H, hd).transpose(0, 2, 1, 3)
            q, k, v = (rs(q), rs(k), rs(v))
            scale = jnp.asarray(hd, x.dtype) ** 0.5
            scores = jnp.einsum('bhqd,bhkd->bhqk', q, k) / scale
            attn = jax.nn.softmax(scores, axis=-1)
            o = jnp.einsum('bhqk,bhkd->bhqd', attn, v).transpose(0, 2, 1, 3).reshape(b, s, d)
            o = o @ ow.T + ob
            x = _layernorm(x + o, n1w, n1b)
            ff = jax.nn.relu(x @ l1w.T + l1b) @ l2w.T + l2b
            return _layernorm(x + ff, n2w, n2b)
        key = jax.random.key(seed)
        ks = jax.random.split(key, 12)
        g = lambda k, shape: jax.random.normal(k, shape, dtype=jnp.float32) * 0.02
        return {'x': jax.random.normal(ks[0], (B, S, D), dtype=jnp.float32), 'in_proj_w': g(ks[1], (E, 3 * D, D)), 'in_proj_b': g(ks[2], (E, 3 * D)), 'out_proj_w': g(ks[3], (E, D, D)), 'out_proj_b': g(ks[4], (E, D)), 'ln1_w': jnp.ones((E, D), jnp.float32), 'ln1_b': jnp.zeros((E, D), jnp.float32), 'lin1_w': g(ks[5], (E, DFF, D)), 'lin1_b': g(ks[6], (E, DFF)), 'lin2_w': g(ks[7], (E, D, DFF)), 'lin2_b': g(ks[8], (E, D)), 'ln2_w': jnp.ones((E, D), jnp.float32), 'ln2_b': jnp.zeros((E, D), jnp.float32), 'gate_w': g(ks[9], (E, D)), 'gate_b': g(ks[10], (E,))}
    _L1_ffn_all = _L1_ffn_setup()
    _L1_ffn_in = {k: v for k, v in _L1_ffn_all.items() if k in ('in_proj_w', 'in_proj_b', 'out_proj_w', 'out_proj_b', 'ln1_w', 'ln1_b', 'lin1_w', 'lin1_b', 'lin2_w', 'lin2_b', 'ln2_w', 'ln2_b', 'gate_w', 'gate_b')}
    del _L1_ffn_all
    return {'x': x, 'L0_tok_W1': _L0_tok_in['W1'], 'L0_tok_b1': _L0_tok_in['b1'], 'L0_tok_W2': _L0_tok_in['W2'], 'L0_tok_b2': _L0_tok_in['b2'], 'L0_attn_qkv_w': _L0_attn_in['qkv_w'], 'L0_attn_qkv_b': _L0_attn_in['qkv_b'], 'L0_attn_out_w': _L0_attn_in['out_w'], 'L0_attn_out_b': _L0_attn_in['out_b'], 'L0_attn_w1': _L0_attn_in['w1'], 'L0_attn_b1': _L0_attn_in['b1'], 'L0_attn_w2': _L0_attn_in['w2'], 'L0_attn_b2': _L0_attn_in['b2'], 'L0_attn_g1': _L0_attn_in['g1'], 'L0_attn_be1': _L0_attn_in['be1'], 'L0_attn_g2': _L0_attn_in['g2'], 'L0_attn_be2': _L0_attn_in['be2'], 'L0_ffn_shared_up': _L0_ffn_in['shared_up'], 'L0_ffn_shared_down': _L0_ffn_in['shared_down'], 'L0_ffn_routed_up': _L0_ffn_in['routed_up'], 'L0_ffn_routed_down': _L0_ffn_in['routed_down'], 'L0_ffn_router_w': _L0_ffn_in['router_w'], 'L1_attn_Wq': _L1_attn_in['Wq'], 'L1_attn_bq': _L1_attn_in['bq'], 'L1_attn_Wk': _L1_attn_in['Wk'], 'L1_attn_bk': _L1_attn_in['bk'], 'L1_attn_Wv': _L1_attn_in['Wv'], 'L1_attn_bv': _L1_attn_in['bv'], 'L1_attn_Wo': _L1_attn_in['Wo'], 'L1_attn_bo': _L1_attn_in['bo'], 'L1_ffn_in_proj_w': _L1_ffn_in['in_proj_w'], 'L1_ffn_in_proj_b': _L1_ffn_in['in_proj_b'], 'L1_ffn_out_proj_w': _L1_ffn_in['out_proj_w'], 'L1_ffn_out_proj_b': _L1_ffn_in['out_proj_b'], 'L1_ffn_ln1_w': _L1_ffn_in['ln1_w'], 'L1_ffn_ln1_b': _L1_ffn_in['ln1_b'], 'L1_ffn_lin1_w': _L1_ffn_in['lin1_w'], 'L1_ffn_lin1_b': _L1_ffn_in['lin1_b'], 'L1_ffn_lin2_w': _L1_ffn_in['lin2_w'], 'L1_ffn_lin2_b': _L1_ffn_in['lin2_b'], 'L1_ffn_ln2_w': _L1_ffn_in['ln2_w'], 'L1_ffn_ln2_b': _L1_ffn_in['ln2_b'], 'L1_ffn_gate_w': _L1_ffn_in['gate_w'], 'L1_ffn_gate_b': _L1_ffn_in['gate_b']}

def reference(x, L0_tok_W1, L0_tok_b1, L0_tok_W2, L0_tok_b2, L0_attn_qkv_w, L0_attn_qkv_b, L0_attn_out_w, L0_attn_out_b, L0_attn_w1, L0_attn_b1, L0_attn_w2, L0_attn_b2, L0_attn_g1, L0_attn_be1, L0_attn_g2, L0_attn_be2, L0_ffn_shared_up, L0_ffn_shared_down, L0_ffn_routed_up, L0_ffn_routed_down, L0_ffn_router_w, L1_attn_Wq, L1_attn_bq, L1_attn_Wk, L1_attn_bk, L1_attn_Wv, L1_attn_bv, L1_attn_Wo, L1_attn_bo, L1_ffn_in_proj_w, L1_ffn_in_proj_b, L1_ffn_out_proj_w, L1_ffn_out_proj_b, L1_ffn_ln1_w, L1_ffn_ln1_b, L1_ffn_lin1_w, L1_ffn_lin1_b, L1_ffn_lin2_w, L1_ffn_lin2_b, L1_ffn_ln2_w, L1_ffn_ln2_b, L1_ffn_gate_w, L1_ffn_gate_b):
    import jax
    import jax.numpy as jnp

    def _L0_tok_ref(x, W1, b1, W2, b2):
        import jax, jax.numpy as jnp
        import numpy as np
        P = 16
        C = 3
        D = 256

        def _patchify(x, p):
            B, Cc, H, W = x.shape
            gh, gw = (H // p, W // p)
            x = x.reshape(B, Cc, gh, p, gw, p)
            x = x.transpose(0, 2, 4, 1, 3, 5)
            return x.reshape(B, gh * gw, Cc * p * p)
        patches = _patchify(x, P)
        h = jax.nn.silu(jnp.einsum('blk,kd->bld', patches, W1) + b1)
        return jnp.einsum('bld,de->ble', h, W2) + b2

    def _L0_attn_ref(src, qkv_w, qkv_b, out_w, out_b, w1, b1, w2, b2, g1, be1, g2, be2):
        import jax, jax.numpy as jnp
        import numpy as np
        D_MODEL = 256
        N_HEAD = 16
        HEAD_D = D_MODEL // N_HEAD
        D_FF = 1024
        LN_EPS = 1e-05
        ATTN_EPS = 1e-06

        def _layer_norm(x, g, b, eps=LN_EPS):
            mu = jnp.mean(x, axis=-1, keepdims=True)
            var = jnp.var(x, axis=-1, keepdims=True)
            return (x - mu) * jax.lax.rsqrt(var + eps) * g + b

        def _linear_attention(x, qkv_w, qkv_b, out_w, out_b):
            B, N, C = x.shape
            qkv = (x @ qkv_w + qkv_b).reshape(B, N, 3, N_HEAD, HEAD_D)
            qkv = jnp.transpose(qkv, (2, 0, 3, 1, 4))
            q, k, v = (qkv[0], qkv[1], qkv[2])
            qf = jax.nn.elu(q) + 1.0
            kf = jax.nn.elu(k) + 1.0
            kv = jnp.einsum('bhnd,bhne->bhde', kf.astype(jnp.float32), v.astype(jnp.float32)).astype(v.dtype)
            y_num = jnp.einsum('bhnd,bhde->bhne', qf, kv)
            z = jnp.sum(kf.astype(jnp.float32), axis=2)
            y_den = jnp.einsum('bhnd,bhd->bhn', qf, z.astype(qf.dtype))
            y_den = jnp.maximum(y_den, ATTN_EPS)[..., None]
            y = (y_num / y_den).transpose(0, 2, 1, 3).reshape(B, N, C)
            return y @ out_w + out_b
        attn_out = _linear_attention(_layer_norm(src, g1, be1), qkv_w, qkv_b, out_w, out_b)
        x = src + attn_out
        h = jax.nn.gelu(_layer_norm(x, g2, be2) @ w1 + b1, approximate=False)
        return x + h @ w2 + b2

    def _L0_ffn_ref(x, shared_up, shared_down, routed_up, routed_down, router_w):
        import jax, jax.numpy as jnp
        import numpy as np
        H_DIM, E_DIM = (256, 128)
        N_SHARED, N_ROUTED, TOP_K = (2, 16, 4)
        B, S = (4, 512)
        b, s, h = x.shape
        xt = x.reshape(-1, h)
        up_s = jnp.einsum('th,seh->tse', xt, shared_up)
        shared = jnp.einsum('tse,she->th', jax.nn.gelu(up_s, approximate=False), shared_down)
        probs = jax.nn.softmax(xt @ router_w.T, axis=-1)
        topk_p, topk_i = jax.lax.top_k(probs, TOP_K)
        gate = jnp.zeros_like(probs).at[jnp.arange(xt.shape[0])[:, None], topk_i].add(topk_p)
        up_r = jnp.einsum('th,reh->tre', xt, routed_up)
        act = jax.nn.gelu(up_r, approximate=False) * gate[:, :, None]
        routed = jnp.einsum('tre,rhe->th', act, routed_down)
        return (shared + routed).reshape(b, s, h)

    def _L1_attn_ref(x, Wq, bq, Wk, bk, Wv, bv, Wo, bo):
        import jax, jax.numpy as jnp
        import numpy as np
        import math
        N, S, E, H = (4, 1024, 256, 16)
        D = E // H
        n, s, e = x.shape
        h, d = (H, D)
        scale = 1.0 / math.sqrt(d)

        def proj(W, b):
            y = jnp.einsum('nse,fe->nsf', x, W) + b
            return y.reshape(n, s, h, d).transpose(0, 2, 1, 3)
        Q = proj(Wq, bq)
        K = proj(Wk, bk)
        V = proj(Wv, bv)
        scores = jnp.einsum('nqhd,nkhd->nhqk', Q, K) * scale
        attn = jax.nn.softmax(scores, axis=-1)
        out = jnp.einsum('nhql,nlhd->nqhd', attn, V)
        out = out.reshape(n, s, e)
        return jnp.einsum('nse,fe->nsf', out, Wo) + bo

    def _L1_ffn_ref(x, in_proj_w, in_proj_b, out_proj_w, out_proj_b, ln1_w, ln1_b, lin1_w, lin1_b, lin2_w, lin2_b, ln2_w, ln2_b, gate_w, gate_b):
        import jax, jax.numpy as jnp
        import numpy as np
        B, S, D = (8, 128, 256)
        H = 16
        DFF = 1024
        E = 4
        K = 2
        EPS = 1e-05

        def _layernorm(x, w, b):
            m = x.mean(-1, keepdims=True)
            v = ((x - m) ** 2).mean(-1, keepdims=True)
            return (x - m) / jnp.sqrt(v + EPS) * w + b

        def _encoder_layer(x, iw, ib, ow, ob, l1w, l1b, l2w, l2b, n1w, n1b, n2w, n2b):
            b, s, d = x.shape
            hd = d // H
            qkv = x @ iw.T + ib
            q, k, v = jnp.split(qkv, 3, axis=-1)
            rs = lambda t: t.reshape(b, s, H, hd).transpose(0, 2, 1, 3)
            q, k, v = (rs(q), rs(k), rs(v))
            scale = jnp.asarray(hd, x.dtype) ** 0.5
            scores = jnp.einsum('bhqd,bhkd->bhqk', q, k) / scale
            attn = jax.nn.softmax(scores, axis=-1)
            o = jnp.einsum('bhqk,bhkd->bhqd', attn, v).transpose(0, 2, 1, 3).reshape(b, s, d)
            o = o @ ow.T + ob
            x = _layernorm(x + o, n1w, n1b)
            ff = jax.nn.relu(x @ l1w.T + l1b) @ l2w.T + l2b
            return _layernorm(x + ff, n2w, n2b)
        gate_logits = x.mean(axis=1) @ gate_w.T + gate_b
        _, top_idx = jax.lax.top_k(gate_logits, K)
        gate_weights = jax.nn.softmax(gate_logits, axis=-1)
        mask = jnp.zeros_like(gate_weights).at[jnp.arange(x.shape[0])[:, None], top_idx].set(1.0)
        expert_outs = jax.vmap(_encoder_layer, in_axes=(None, 0, 0, 0, 0, 0, 0, 0, 0, 0, 0, 0, 0))(x, in_proj_w, in_proj_b, out_proj_w, out_proj_b, lin1_w, lin1_b, lin2_w, lin2_b, ln1_w, ln1_b, ln2_w, ln2_b)
        return jnp.einsum('be,ebsd->bsd', gate_weights * mask, expert_outs)
    h = _L0_tok_ref(x, L0_tok_W1, L0_tok_b1, L0_tok_W2, L0_tok_b2)
    h = h + _L0_attn_ref(_layernorm(h, axis=-1), L0_attn_qkv_w, L0_attn_qkv_b, L0_attn_out_w, L0_attn_out_b, L0_attn_w1, L0_attn_b1, L0_attn_w2, L0_attn_b2, L0_attn_g1, L0_attn_be1, L0_attn_g2, L0_attn_be2)
    h = h + _L0_ffn_ref(_layernorm(h, axis=-1), L0_ffn_shared_up, L0_ffn_shared_down, L0_ffn_routed_up, L0_ffn_routed_down, L0_ffn_router_w)
    h = h + _L1_attn_ref(_layernorm(h, axis=-1), L1_attn_Wq, L1_attn_bq, L1_attn_Wk, L1_attn_bk, L1_attn_Wv, L1_attn_bv, L1_attn_Wo, L1_attn_bo)
    h = h + _L1_ffn_ref(_layernorm(h, axis=-1), L1_ffn_in_proj_w, L1_ffn_in_proj_b, L1_ffn_out_proj_w, L1_ffn_out_proj_b, L1_ffn_ln1_w, L1_ffn_ln1_b, L1_ffn_lin1_w, L1_ffn_lin1_b, L1_ffn_lin2_w, L1_ffn_lin2_b, L1_ffn_ln2_w, L1_ffn_ln2_b, L1_ffn_gate_w, L1_ffn_gate_b)
    return h

_drawn_inputs = setup_inputs


def setup_inputs(seed=0):
    import zlib

    import numpy as np

    out = dict(_drawn_inputs(seed))
    spreads = {'L0_attn_g1': (1.0, 0.6),
     'L0_attn_be1': (0.0, 0.764),
     'L0_attn_g2': (1.0, 0.6),
     'L0_attn_be2': (0.0, 0.693),
     'L1_ffn_ln1_w': (1.0, 0.2),
     'L1_ffn_ln1_b': (0.0, 0.384),
     'L1_ffn_ln2_w': (1.0, 0.2),
     'L1_ffn_ln2_b': (0.0, 0.367)}
    factors = {'L0_attn_qkv_b': 7.614,
     'L0_attn_b1': 8.0,
     'L1_attn_bq': 2.695,
     'L1_attn_bk': 3.636,
     'L1_ffn_in_proj_w': 7.115,
     'L1_ffn_in_proj_b': 8.0,
     'L1_ffn_out_proj_w': 6.904,
     'L1_ffn_out_proj_b': 53.876,
     'L1_ffn_lin1_b': 30.401,
     'L1_ffn_lin2_b': 8.0,
     'L1_ffn_gate_b': 3.2}
    for name, (base, spread) in spreads.items():
        noise = np.random.default_rng([zlib.crc32(name.encode()), seed]).standard_normal(out[name].shape)
        drawn = base * np.exp(spread * noise) if base else spread * noise
        out[name] = jnp.asarray(drawn.astype(out[name].dtype))
    for name, factor in factors.items():
        out[name] = (out[name] * factor).astype(out[name].dtype)
    return out
```

```python
from collections import Counter
from contextlib import ExitStack

import numpy as np

import concourse.bass as bass
from concourse import mybir

F32 = mybir.dt.float32
F32R = mybir.dt.float32r
ALU = mybir.AluOpType
ACT = mybir.ActivationFunctionType
AX = mybir.AxisListType

P = 128
D = 256
C = D // P
IMAGES = 16
TOK = 36
HALVES = 2
HI = IMAGES // HALVES
NT = HI * TOK
HD = 16
HC = P // HD
PATCH = 768
KP = PATCH // P
FF = 1024
ROUTED, SHARED, TOPK = 16, 2, 4
EXPERTS, TOP2 = 4, 2
LN_EPS = 1e-5
ATTN_EPS = 1e-6
GROUPS = [(0, 3), (3, 3), (6, 2)]
SLOTS = 3
PITCH = SLOTS * TOK
LEAD = (SLOTS - 1) * TOK
PADDED = LEAD + HI * PITCH
TILE = 512
RING = 5
STAGES = 2
RT = 96
RB = NT // RT
UB = 4
WB = 4
HID = 8


def bias_columns():
    names = [("tok_b1", 2), ("tok_b2", 2), ("l0_qk_b", 4), ("l0_out_b", 2), ("l0_b1", 8), ("l0_b2", 2),
             ("g1", 2), ("be1", 2), ("g2", 2), ("be2", 2), ("l1_out_b", 2)]
    for e in range(EXPERTS):
        names += [(f"e{e}_qk_b", 4), (f"e{e}_out_b", 2), (f"e{e}_b1", 8), (f"e{e}_b2", 2),
                  (f"e{e}_g1", 2), (f"e{e}_be1", 2), (f"e{e}_g2", 2), (f"e{e}_be2", 2)]
    at, out = 0, {}
    for name, n in names:
        out[name] = (at, n)
        at += n
    return out, at


K_MEAN = 0
K_BLOCK = K_MEAN + P
K_DELTA = K_BLOCK + PITCH
K_IDENT = K_DELTA + TOK
K_FIRST = K_IDENT + P
K_EYE8 = K_FIRST + RB * ROUTED
K_ONES = K_EYE8 + HI
K_SHAPE = K_ONES + P


def shape_constants():
    k = np.zeros((P, K_SHAPE), np.float32)
    k[:, K_MEAN:K_MEAN + P] = 1.0 / D
    r = np.arange(PITCH)
    k[:PITCH, K_BLOCK:K_BLOCK + PITCH] = r[:, None] // TOK == r[None] // TOK
    k[:PITCH, K_DELTA:K_DELTA + TOK] = r[:, None] % TOK == np.arange(TOK)[None]
    k[:, K_IDENT:K_IDENT + P] = np.eye(P)
    k[:, K_FIRST:K_FIRST + RB * ROUTED] = np.arange(RB * ROUTED) % ROUTED != 0
    k[:HI, K_EYE8:K_EYE8 + HI] = np.eye(HI)
    k[:, K_ONES:K_ONES + P] = 1.0
    return k


def build_tower(nc, patches, weights, biases, vbias, hbias, router, gate, gate_b, constants, out, mixed):
    bcol, nbias = bias_columns()
    tiles = weights.shape[1] // TILE

    with ExitStack() as ctx:
        def sb(name, shape, dt=F32):
            return ctx.enter_context(nc.sbuf_tensor(name, shape, dt))

        def sem(name):
            return ctx.enter_context(nc.semaphore(name))

        u_ring = [ctx.enter_context(nc.psum_tensor(f"u_ring{i}", [P, TILE], F32)) for i in range(UB)]
        w_ring = [ctx.enter_context(nc.psum_tensor(f"w_ring{i}", [P, TILE], F32)) for i in range(WB)]

        kshape = sb("kshape", [P, K_SHAPE])
        mean_w = sb("mean_w", [P, P], F32R)
        block_w = sb("block_w", [PITCH, PITCH], F32R)
        eye_w = sb("eye_w", [ROUTED, ROUTED], F32R)
        bias = sb("bias", [P, nbias])
        vb = sb("vb", [P, 2, D])
        rt_raw = sb("rt_raw", [P, C * ROUTED])
        rt = sb("rt", [P, 2, C * ROUTED], F32R)
        gt = sb("gt", [P, C * EXPERTS])
        gtb = sb("gtb", [P, EXPERTS])
        stage = sb("stage", [P, STAGES, TILE])
        wh = sb("wh", [P, RING, TILE], F32R)
        wl = sb("wl", [P, RING, TILE], F32R)

        h = sb("h", [P, HALVES, C, NT])
        x = sb("x", [P, HALVES, C, NT])
        xr = sb("xr", [P, HALVES, C, NT])
        t1 = sb("t1", [P, HALVES, C, NT])
        t2 = sb("t2", [P, HALVES, C, NT])
        ah = sb("ah", [P, HALVES, C, NT], F32R)
        al = sb("al", [P, HALVES, C, NT], F32R)
        rstd = sb("rstd", [P, 2, NT])

        qpad = sb("qpad", [P, C, PADDED], F32R)
        kpad = sb("kpad", [P, 2, C, PADDED], F32R)
        vs = sb("vs", [PITCH, 3, 2 * D], F32R)
        vm = sb("vm", [PITCH, SLOTS, 3, 2 * D], F32R)
        vf = sb("vf", [PITCH, D])
        shift = sb("shift", [PITCH, 2, HC])
        mx = sb("mx", [PITCH, 2, HC, TOK], F32R)
        e_t = sb("e_t", [PITCH, 2, HC * TOK])
        eh = sb("eh", [PITCH, 3, HC * TOK], F32R)
        el = sb("el", [PITCH, 3, HC * TOK], F32R)
        rs = sb("rs", [PITCH, 2, HC * TOK])

        hf = sb("hf", [P, 2, NT])
        lg = sb("lg", [RT, RB * ROUTED])
        pr = sb("pr", [RT, RB * ROUTED])
        gw = sb("gw", [RT, HALVES, RB * ROUTED])
        eps_t = sb("eps_t", [P, 1])
        sm = sb("sm", [RT, 2 * ROUTED * RB])
        sel_n = sb("sel_n", [RT, 4])
        sel_c = sb("sel_c", [RT, RB * ROUTED])
        top = sb("top", [RT, RB, 8])
        xm = sb("xm", [P, C, HI])
        lg1 = sb("lg1", [HI, 8])
        wx = sb("wx", [HI, EXPERTS, HI])
        wimg = sb("wimg", [P, HALVES, EXPERTS, HI])

        with nc.sbuf_tensor("gb", [P, 2, NT], F32) as gb, \
                nc.sbuf_tensor("gth", [ROUTED, HALVES, NT], F32R) as gth, \
                nc.sbuf_tensor("gtl", [ROUTED, HALVES, NT], F32R) as gtl:
            pass
        qks = sb("qks", [P, C, 3, NT], F32R)
        with nc.sbuf_tensor("patch_raw", [P, KP, NT], F32) as patch_raw, \
                nc.sbuf_tensor("patch_h", [P, HALVES, KP, NT], F32R) as patch_h, \
                nc.sbuf_tensor("patch_l", [P, HALVES, KP, NT], F32R) as patch_l:
            pass
        qkx = sb("qkx", [P, HC, C, 3, NT], F32R)
        with nc.sbuf_tensor("av", [P, C, HC, NT], F32) as av:
            pass
        hid = sb("hid", [P, HID, 2, NT], F32R)

        k_dma = sem("k_dma")
        patch_dma = sem("patch_dma")
        stage_dma = [sem(f"stage_dma{i}") for i in range(STAGES)]
        w_ready = sem("w_ready")
        w_used = sem("w_used")
        k_ready = sem("k_ready")
        zeroed = sem("zeroed")
        patch_split = sem("patch_split")
        u_full, u_taken = sem("u_full"), sem("u_taken")
        d_full, d_taken = sem("d_full"), sem("d_taken")
        a_split = sem("a_split")
        act_out = sem("act_out")
        dve_in = sem("dve_in")
        dve_step = sem("dve_step")
        qk_split = sem("qk_split")
        hb_dma = sem("hb_dma")
        ho_ready = sem("ho_ready")
        mixed_dma = sem("mixed_dma")
        back_dma = [sem(f"back_dma{i}") for i in range(2)]
        vb_dma = sem("vb_dma")
        qk_dma = sem("qk_dma")
        v_split = sem("v_split")
        v_dma = sem("v_dma")
        mx_ready = sem("mx_ready")
        r_ready = sem("r_ready")
        es_ready = sem("es_ready")
        ps_ready = sem("ps_ready")
        av_dma = sem("av_dma")
        hid_ready = sem("hid_ready")
        hid_used = sem("hid_used")
        gate_ready = sem("gate_ready")
        xm_ready = sem("xm_ready")
        wx_ready = sem("wx_ready")
        out_ready = sem("out_ready")
        out_dma = sem("out_dma")

        flat = "p h c n -> p (h c n)"
        hb = xr[:].rearrange(flat)[:, 0:3 * D]
        hq = t2[0:PITCH].rearrange(flat)[:, 0:3 * D]
        hp = av[0:PITCH].rearrange("p c s n -> p (c s n)")[:, 0:HD ** 3]
        h_s = e_t[:].rearrange("p i n -> p (i n)")[:, 0:D]

        block = ctx.enter_context(nc.Block())

        def bc(name, i):
            return bias[:, bcol[name][0] + i:bcol[name][0] + i + 1]

        class Tally:

            def __init__(self, eng):
                self.eng, self.n = eng, Counter()

            def up(self, s, by=1):
                self.n[s.name] += by
                return s, by

            def more(self, s, by=1):
                self.n[s.name] += by
                self.eng.wait_ge(s, self.n[s.name])

            def own(self, s):
                self.eng.wait_ge(s, self.n[s.name])

            def room(self, s, used, size):
                if used >= size:
                    self.eng.wait_ge(s, used - size + 1)

        steps = [(g, c) for g in range(len(GROUPS)) for c in range(C)]

        def u_banks(softmax):
            return 2 * C + len(steps) * (1 + softmax) + C * HI

        norm_u, ff_u = HALVES, HALVES * FF // P
        U_BEFORE = [HALVES * C + 2 * norm_u]
        U_BEFORE.append(U_BEFORE[0] + HALVES * u_banks(False) + norm_u + ff_u + norm_u
                        + HALVES * (SHARED + 2 * ROUTED) + 2 * norm_u)
        for _e in range(1, EXPERTS):
            U_BEFORE.append(U_BEFORE[-1] + HALVES * u_banks(True) + norm_u + ff_u + norm_u)

        @block.gpsimd
        def _(pool):
            def load(i):
                pool.dma_start(stage[:, i % STAGES], weights[:, TILE * i:TILE * (i + 1)]
                               ).then_inc(stage_dma[i % STAGES], 16)

            load(0)
            load(1)
            for z in (qpad, kpad, vm):
                last = nc.gpsimd.memset(z[:].bitcast(F32), 0.0)
            last.then_inc(zeroed, 1)
            for i in range(tiles):
                if i == 4:
                    pool.wait_ge(u_full, HALVES * C)
                    nc.gpsimd.memset(qkx[:].bitcast(F32), 0.0).then_inc(zeroed, 1)
                raw = stage[:, i % STAGES]
                pool.wait_ge(stage_dma[i % STAGES], 16 * (i // STAGES + 1))
                if i >= RING:
                    pool.wait_ge(w_used, i - RING + 1)
                nc.gpsimd.tensor_copy(wh[:, i % RING], raw).then_inc(w_ready, 1)
                pool.wait_ge(w_ready, 2 * i + 1)
                nc.gpsimd.tensor_tensor(wl[:, i % RING], raw, wh[:, i % RING].bitcast(F32),
                                        ALU.subtract).then_inc(w_ready, 1)
                if i + STAGES < tiles:
                    pool.wait_ge(w_ready, 2 * (i + 1))
                    load(i + STAGES)

        @block.sync
        def _(sp):
            t = Tally(sp)
            for dst, src in ((kshape, constants), (bias, biases), (rt_raw, router), (gt, gate)):
                sp.dma_start(dst[:], src).then_inc(k_dma, 16)
            sp.dma_start(gtb[:], gate_b.partition_broadcast(P)).then_inc(k_dma, 16)
            for hv in range(HALVES):
                if hv:
                    sp.wait_ge(patch_split, hv)
                sp.dma_start(patch_raw[:], patches[hv]).then_inc(patch_dma, 16)

            banks = U_BEFORE[0]
            for n in range(1 + EXPERTS):
                banks = U_BEFORE[n]
                if n == 1:
                    sp.wait_ge(gate_ready, 1)
                    sp.dma_start(hb[:], hbias.partition_broadcast(P)).then_inc(hb_dma, 16)
                    for hv in range(HALVES):
                        for g, (i0, ni) in enumerate(GROUPS):
                            t.more(ho_ready)
                            for i in range(ni):
                                sp.dma_start(mixed[HI * hv + i0 + i].rearrange("a t d -> t a d"),
                                             vf[TOK * i:TOK * (i + 1)].rearrange("t (a d) -> t a d", d=HD)
                                             ).then_inc(mixed_dma, 16)
                            t.more(mixed_dma, 16 * ni)
                            sp.dma_start(rs[0:ni * TOK, (hv * len(GROUPS) + g) % 2, 0:D],
                                         mixed[HI * hv + i0:HI * hv + i0 + ni].rearrange("i a t d -> (i a t d)")
                                         .rearrange("(r f) -> r f", f=D)
                                         ).then_inc(back_dma[(hv * len(GROUPS) + g) % 2], 16)
                if n > 1:
                    sp.wait_ge(v_split, HALVES * (n - 1))
                sp.dma_start(vb[:, n % 2], vbias[n].partition_broadcast(P)).then_inc(vb_dma, 16)
                for hv in range(HALVES):
                    t.more(qk_split)
                    for s in range(HC):
                        r = slice(HD * s, HD * (s + 1))
                        sp.dma_start(qkx[r, s].bitcast(F32), qks[r].bitcast(F32)).then_inc(qk_dma, 16)
                    t.more(v_split)
                    for s in range(SLOTS):
                        r = slice(TOK * s, TOK * (s + 1))
                        g = 3 if s < 2 else 2
                        sp.dma_start(vm[r, s, 0:g].bitcast(F32), vs[r, 0:g].bitcast(F32)).then_inc(v_dma, 16)
                    banks += u_banks(n > 0)
                    sp.wait_ge(u_taken, banks)
                    for s in range(HC):
                        r = slice(HD * s, HD * (s + 1))
                        sp.dma_start(t1[r, hv], av[r, :, s]).then_inc(av_dma, 16)
            for hv in range(HALVES):
                t.more(out_ready)
                sp.dma_start(out[hv], h[:, hv]).then_inc(out_dma, 16)
            sp.wait_ge(out_dma, 16 * HALVES)

        @block.tensor
        def _(pe):
            t = Tally(pe)
            n = Counter()

            def u_bank():
                t.room(u_taken, n["u"], UB)
                n["u"] += 1
                return u_ring[(n["u"] - 1) % UB]

            def d_bank():
                t.room(d_taken, n["d"], WB)
                n["d"] += 1
                return w_ring[(n["d"] - 1) % WB]

            def product(o, lhs, rhs, start, stop):
                first = nc.tensor.matmul(o, lhs[0], rhs[0], start=start, stop=False)
                second = nc.tensor.matmul(o, lhs[0], rhs[1], start=False, stop=False)
                if n["tiles_done"]:
                    first.then_inc(w_used, n["tiles_done"])
                    n["tiles_done"] = 0
                if n["hid_done"]:
                    second.then_inc(hid_used, n["hid_done"])
                    n["hid_done"] = 0
                return nc.tensor.matmul(o, lhs[1], rhs[0], start=False, stop=stop)

            def tile(i):
                pe.wait_ge(w_ready, 2 * (n["tile"] + i + 1))
                return (n["tile"] + i) % RING

            def done(k):
                n["tile"] += k
                n["tiles_done"] += k

            def w(s, col, width=P):
                return wh[:, s, col:col + width], wl[:, s, col:col + width]

            def a(hv, k, cols=slice(0, NT)):
                return ah[:, hv, k, cols], al[:, hv, k, cols]

            def stats(hv, u):
                t.more(a_split)
                o = (u_bank() if u else d_bank())[:, 0:NT]
                for i, v in enumerate((ah[:, hv, 0], al[:, hv, 0], ah[:, hv, 1], al[:, hv, 1])):
                    last = nc.tensor.matmul(o, mean_w[:], v, start=(i == 0), stop=(i == 3))
                last.then_inc(u_full if u else d_full, 1)

            def norms():
                for u in (False, True):
                    for hv in range(HALVES):
                        stats(hv, u)

            def linear2(hv, s, bank, full):
                for m in range(2):
                    o = bank()[:, 0:NT]
                    for k in range(C):
                        last = product(o, w(s, P * (2 * m + k)), a(hv, k), k == 0, k == C - 1)
                    last.then_inc(full, 1)
                return last

            def attention(softmax):
                for hv in range(HALVES):
                    t.more(a_split)
                    for i in range(2):
                        linear2(hv, tile(i), u_bank, u_full)
                    s = tile(2)
                    for i0, ni in GROUPS:
                        o = d_bank()[0:ni * TOK, 0:D]
                        for k in range(C):
                            last = product(o, a(hv, k, slice(TOK * i0, TOK * (i0 + ni))),
                                           w(s, D * k, D), k == 0, k == C - 1)
                        last.then_inc(d_full, 1)
                    t.more(qk_dma, 16 * HC)
                    J = len(steps)
                    for j in range(-2, J + 1):
                        if softmax and j + 2 < J:
                            (g, c) = steps[j + 2]
                            i0, ni = GROUPS[g]
                            o = d_bank()[0:ni * TOK, 0:HC * TOK]
                            for i in range(ni):
                                at = PITCH * (i0 + i) + LEAD - TOK * i
                                q = slice(TOK * (i0 + i), TOK * (i0 + i + 1))
                                last = nc.tensor.matmul(o, qpad[:, c, at:at + ni * TOK], qkx[:, :, c, 2, q],
                                                        start=(i == 0), stop=(i == ni - 1))
                            last.then_inc(d_full, 1)
                        if 0 <= j + 1 < J:
                            (g, c) = steps[j + 1]
                            i0, ni = GROUPS[g]
                            o = u_bank()[0:ni * TOK, 0:HC * TOK]
                            for i in range(ni):
                                at = PITCH * (i0 + i) + LEAD - TOK * i
                                q = slice(TOK * (i0 + i), TOK * (i0 + i + 1))
                                last = product(o, (kpad[:, 0, c, at:at + ni * TOK], kpad[:, 1, c, at:at + ni * TOK]),
                                               (qkx[:, :, c, 0, q], qkx[:, :, c, 1, q]),
                                               i == 0, i == ni - 1 and not softmax)
                            if softmax:
                                t.more(mx_ready)
                                last = nc.tensor.matmul(o, block_w[0:ni * TOK, 0:ni * TOK],
                                                        mx[0:ni * TOK, (j + 1) % 2], start=False, stop=True)
                            last.then_inc(u_full, 1)
                        if 0 <= j < J:
                            (g, c) = steps[j]
                            r = slice(0, GROUPS[g][1] * TOK)
                            t.more(es_ready)
                            o = (u_bank() if softmax else d_bank())[r, 0:HC * TOK]
                            nc.tensor.matmul(o, block_w[r, r], eh[r, j % 3], start=True, stop=False)
                            nc.tensor.matmul(o, block_w[r, r], el[r, j % 3], start=False, stop=True
                                             ).then_inc(u_full if softmax else d_full, 1)
                        if j == 0:
                            t.more(v_dma, 16 * SLOTS)
                        if 0 <= j - 1 < J:
                            (g, c) = steps[j - 1]
                            i0, ni = GROUPS[g]
                            r = slice(0, ni * TOK)
                            t.more(ps_ready)
                            for i in range(ni):
                                o = u_bank()[:, 0:HC * TOK]
                                product(o, (vm[r, i, g, P * c:P * (c + 1)], vm[r, i, g, D + P * c:D + P * (c + 1)]),
                                        (eh[r, (j - 1) % 3], el[r, (j - 1) % 3]), True, True
                                        ).then_inc(u_full, 1)
                done(3)
                s = tile(0)
                for hv in range(HALVES):
                    t.more(a_split)
                    last = linear2(hv, s, d_bank, d_full)
                done(1)

            def feed_forward():
                acc = [[d_bank() for _ in range(C)] for _ in range(HALVES)]
                t.more(a_split, HALVES)
                pairs = FF // P // 2
                for p in range(pairs + 1):
                    if p < pairs:
                        s = tile(0)
                        for hv in range(HALVES):
                            linear2(hv, s, u_bank, u_full)
                        done(1)
                    if p:
                        s = tile(0)
                        for hv in range(HALVES):
                            for i in range(2):
                                t.more(hid_ready)
                                slot = n["hid"] % HID
                                n["hid"] += 1
                                for m in range(C):
                                    last = product(acc[hv][m][:, 0:NT], w(s, P * (2 * i + m)),
                                                   (hid[:, slot, 0], hid[:, slot, 1]),
                                                   p == 1 and i == 0, p == pairs and i == 1)
                                    if p == pairs and i == 1:
                                        last.then_inc(d_full, 1)
                                n["hid_done"] += 1
                        done(1)

            def back(hv, g):
                if g >= 0:
                    ni = GROUPS[g][1]
                    t.more(back_dma[(hv * len(GROUPS) + g) % 2], 16)
                    for c in range(C):
                        nc.tensor.transpose(d_bank()[:, 0:ni * TOK], rs[0:ni * TOK, (hv * len(GROUPS) + g) % 2, P * c:P * (c + 1)],
                                            kshape[0:ni * TOK, K_IDENT:K_IDENT + ni * TOK]).then_inc(d_full, 1)

            pe.wait_ge(k_ready, 1)
            t.more(patch_split, HALVES)
            for hv in range(HALVES):
                for m in range(C):
                    o = u_bank()[:, 0:NT]
                    for k in range(KP):
                        b = KP * m + k
                        s = tile(b // 4)
                        last = product(o, w(s, P * (b % 4)), (patch_h[:, hv, k], patch_l[:, hv, k]),
                                       k == 0, k == KP - 1)
                    last.then_inc(u_full, 1)
            done(3)
            s = tile(0)
            for hv in range(HALVES):
                t.more(a_split)
                linear2(hv, s, d_bank, d_full)
            done(1)

            norms()
            norms()
            pe.wait_ge(zeroed, 2)
            attention(False)
            norms()
            feed_forward()

            norms()
            acc = None
            for hv in range(HALVES):
                t.more(a_split)
                o = d_bank()
                for b in range(RB):
                    for k in range(C):
                        last = product(o[0:RT, ROUTED * b:ROUTED * (b + 1)], a(hv, k, slice(RT * b, RT * (b + 1))),
                                       (rt[:, 0, ROUTED * k:ROUTED * (k + 1)], rt[:, 1, ROUTED * k:ROUTED * (k + 1)]),
                                       k == 0, k == C - 1)
                last.then_inc(d_full, 1)
            for hv in range(HALVES):
                t.more(gate_ready)
                o = d_bank()
                for b in range(RB):
                    last = nc.tensor.transpose(o[0:ROUTED, RT * b:RT * (b + 1)], gw[:, hv, ROUTED * b:ROUTED * (b + 1)],
                                               kshape[0:RT, K_IDENT:K_IDENT + RT])
                last.then_inc(d_full, 1)
            gates = n["d"]
            acc = [[d_bank() for _ in range(C)] for _ in range(HALVES)]
            E = SHARED + ROUTED
            for e in range(E + 1):
                if e < E:
                    s = tile(1 if e else 0)
                    for hv in range(HALVES):
                        o = u_bank()[:, 0:NT]
                        for k in range(C):
                            last = product(o, w(s, P * k), a(hv, k), k == 0, k == C - 1)
                        last.then_inc(u_full, 1)
                        if e >= SHARED:
                            if e == SHARED and hv == 0:
                                pe.wait_ge(d_taken, gates)
                            r = e - SHARED
                            o = u_bank()[:, 0:NT]
                            pick = eye_w[:, r:r + 1].to_broadcast([ROUTED, P])
                            nc.tensor.matmul(o, pick, gth[:, hv], start=True, stop=False)
                            nc.tensor.matmul(o, pick, gtl[:, hv], start=False, stop=True
                                             ).then_inc(u_full, 1)
                if e:
                    s = tile(0)
                    for hv in range(HALVES):
                        t.more(hid_ready)
                        slot = n["hid"] % HID
                        n["hid"] += 1
                        for m in range(C):
                            last = product(acc[hv][m][:, 0:NT], w(s, P * (2 + m)), (hid[:, slot, 0], hid[:, slot, 1]),
                                           e == 1, e == E)
                            if e == E:
                                last.then_inc(d_full, 1)
                        n["hid_done"] += 1
                    done(1)

            norms()
            t.more(a_split, HALVES)
            for hv in range(HALVES):
                for g, (i0, ni) in enumerate(GROUPS):
                    for i in range(3):
                        s = tile(i)
                        o = d_bank()[0:ni * TOK, 0:D]
                        for k in range(C):
                            last = product(o, a(hv, k, slice(TOK * i0, TOK * (i0 + ni))), w(s, D * k, D),
                                           k == 0, k == C - 1)
                        last.then_inc(d_full, 1)
                    back(hv, g - 1)
                back(hv, len(GROUPS) - 1)
            done(3)
            s = tile(0)
            for hv in range(HALVES):
                t.more(a_split)
                linear2(hv, s, d_bank, d_full)
            done(1)

            norms()
            for hv in range(HALVES):
                t.more(xm_ready)
                o = d_bank()[0:HI, 0:EXPERTS]
                for k in range(C):
                    last = nc.tensor.matmul(o, xm[:, k], gt[:, EXPERTS * k:EXPERTS * (k + 1)],
                                            start=(k == 0), stop=(k == C - 1))
                last.then_inc(d_full, 1)
                t.more(wx_ready)
                o = d_bank()[:, 0:EXPERTS * HI]
                nc.tensor.matmul(o, kshape[0:HI, K_ONES:K_ONES + P], wx[:].rearrange("i e j -> i (e j)"), start=True, stop=True).then_inc(d_full, 1)
            for e in range(EXPERTS):
                attention(True)
                norms()
                feed_forward()
                norms()

        @block.scalar
        def _(act):
            t = Tally(act)
            n = Counter()

            def bank():
                t.more(u_full)
                n["u"] += 1
                return u_ring[(n["u"] - 1) % UB]

            def rsqrt(hv):
                o = bank()[:, 0:NT]
                nc.scalar.activation(rstd[:, hv], o, ACT.Ln, bias=eps_t[:, 0:1]).then_inc(*t.up(u_taken))
                t.own(u_taken)
                nc.scalar.activation(rstd[:, hv], rstd[:, hv], ACT.Exp, scale=-0.5).then_inc(*t.up(r_ready))

            def norms():
                for hv in range(HALVES):
                    rsqrt(hv)

            def attention(softmax, qk_bias):
                for hv in range(HALVES):
                    for i, dst in ((0, t1), (1, t2)):
                        for c in range(C):
                            o = bank()[:, 0:NT]
                            nc.scalar.activation(dst[:, hv, c], o, ACT.Identity, bias=bc(qk_bias, 2 * i + c)
                                                 ).then_inc(*t.up(u_taken))
                    if not softmax:
                        for _m in range(2):
                            t.more(dve_in)
                            nc.scalar.activation(xr[:, hv], xr[:, hv], ACT.Exp).then_inc(*t.up(act_out))
                    J = len(steps)
                    for j in range(-2, J + 1):
                        if 0 <= j + 1 < J:
                            r = slice(0, GROUPS[steps[j + 1][0]][1] * TOK)
                            o = bank()[r, 0:HC * TOK]
                            t.room(ps_ready, n["e"], 2)
                            n["e"] += 1
                            f, sc = (ACT.Exp, HD ** -0.5) if softmax else (ACT.Identity, 1.0)
                            nc.scalar.activation(e_t[r, (j + 1) % 2], o, f, scale=sc).then_inc(*t.up(u_taken))
                        if softmax and 0 <= j < J:
                            r = slice(0, GROUPS[steps[j][0]][1] * TOK)
                            o = bank()[r, 0:HC * TOK]
                            nc.scalar.activation(rs[r, j % 2], o, ACT.Ln).then_inc(*t.up(u_taken))
                            t.own(u_taken)
                            nc.scalar.activation(rs[r, j % 2], rs[r, j % 2], ACT.Exp, scale=-1.0
                                                 ).then_inc(*t.up(r_ready))
                        if 0 <= j - 1 < J:
                            (g, c) = steps[j - 1]
                            i0, ni = GROUPS[g]
                            if j == 1 and n["av"]:
                                act.wait_ge(av_dma, 16 * HC * n["av"])
                            for i in range(ni):
                                o = bank()[:, 0:HC * TOK].rearrange("p (s q) -> p s q", q=TOK)
                                at = TOK * (i0 + i)
                                nc.scalar.activation(av[:, c, :, at:at + TOK], o, ACT.Copy
                                                     ).then_inc(*t.up(u_taken))
                    n["av"] += 1

            def hidden(f, b):
                o = bank()[:, 0:NT]
                t.room(hid_ready, n["hf"], 2)
                nc.scalar.activation(hf[:, n["hf"] % 2], o, f, **({"bias": b} if b is not None else {})
                                     ).then_inc(*t.up(u_taken))
                n["hf"] += 1

            def feed_forward(f, b1):
                for p in range(FF // P // 2):
                    for hv in range(HALVES):
                        for m in range(2):
                            hidden(f, bc(b1, 2 * p + m))

            act.wait_ge(k_ready, 1)
            for hv in range(HALVES):
                for m in range(C):
                    o = bank()[:, 0:NT]
                    nc.scalar.activation(t1[:, hv, m], o, ACT.Silu, bias=bc("tok_b1", m)).then_inc(*t.up(u_taken))
            nc.scalar.preload_act_table_set("natural_log_exp_and_others")
            norms()
            norms()
            attention(False, "l0_qk_b")
            norms()
            feed_forward(ACT.Gelu, "l0_b1")
            nc.scalar.preload_act_table_set("natural_log_exp_and_others")
            norms()
            for hv in range(HALVES):
                t.more(dve_in)
                nc.scalar.activation(pr[:], lg[:], ACT.Exp).then_inc(*t.up(act_out))
            for e in range(SHARED + ROUTED):
                for hv in range(HALVES):
                    hidden(ACT.Gelu, None)
                    if e >= SHARED:
                        o = bank()[:, 0:NT]
                        nc.scalar.activation(gb[:, n["gb"] % 2], o, ACT.Copy).then_inc(*t.up(u_taken))
                        n["gb"] += 1
            nc.scalar.preload_act_table_set("natural_log_exp_and_others")
            norms()
            for _ in range(HALVES * len(GROUPS)):
                ni = GROUPS[_ % len(GROUPS)][1]
                t.more(dve_in)
                nc.scalar.activation(h_s[0:ni * TOK], h_s[0:ni * TOK], ACT.Exp, scale=HD ** -0.5
                                     ).then_inc(*t.up(act_out))
            norms()
            for hv in range(HALVES):
                t.more(dve_in)
                nc.scalar.activation(sm[0:HI, 8:8 + EXPERTS], sm[0:HI, 0:EXPERTS], ACT.Exp).then_inc(*t.up(act_out))
            for e in range(EXPERTS):
                attention(True, f"e{e}_qk_b")
                norms()
                feed_forward(ACT.Relu, f"e{e}_b1")
                norms()

        @block.vector
        def _(dve):
            t = Tally(dve)
            n = Counter()
            v = nc.vector

            def step(ins):
                ins.then_inc(*t.up(dve_step))
                t.own(dve_step)

            def tell(ins, s):
                ins.then_inc(*t.up(s))
                t.own(s)

            def banks(k=1):
                n["u"] += k

            def taken():
                n["u"] += 1
                dve.wait_ge(u_taken, n["u"])

            def bank():
                t.more(d_full)
                n["d"] += 1
                return w_ring[(n["d"] - 1) % WB]

            def take(ins):
                ins.then_inc(*t.up(d_taken))
                t.own(d_taken)

            def split(src, hv):
                step(v.tensor_copy(ah[:, hv], src))
                tell(v.tensor_tensor(al[:, hv], src, ah[:, hv].bitcast(F32), ALU.subtract), a_split)

            def norms(src, dst, g=None, b=None):
                for hv in range(HALVES):
                    split(src[:, hv], hv)
                for hv in range(HALVES):
                    o = bank()[:, 0:NT]
                    take(v.tensor_tensor(t1[:, hv], src[:, hv], o.unsqueeze(1).to_broadcast([P, C, NT]), ALU.subtract))
                    step(v.tensor_tensor(t2[:, hv], t1[:, hv], t1[:, hv], ALU.mult))
                    split(t2[:, hv], hv)
                banks(HALVES)
                for hv in range(HALVES):
                    t.more(r_ready)
                    step(v.tensor_tensor(dst[:, hv], t1[:, hv], rstd[:, hv].unsqueeze(1).to_broadcast([P, C, NT]),
                                         ALU.mult))
                    if g:
                        for c in range(C):
                            step(v.tensor_scalar(dst[:, hv, c], dst[:, hv, c], bc(g, c), bc(b, c), ALU.mult, ALU.add))

            def residual(dst, src, b):
                for hv in range(HALVES):
                    for c in range(C):
                        o = bank()[:, 0:NT]
                        if b:
                            take(v.scalar_tensor_tensor(dst[:, hv, c], o, bc(b, c), src[:, hv, c], ALU.add, ALU.add))
                        else:
                            take(v.tensor_tensor(dst[:, hv, c], o, src[:, hv, c], ALU.add))

            def images(ap):
                return ap[:, :, LEAD:PADDED].rearrange("p c (i w) -> p c i w", w=PITCH)[:, :, :, 0:TOK]

            def by_image(ap):
                return ap.rearrange("p c (i q) -> p c i q", q=TOK)

            def attention(softmax, src, vcol, dst, res, out_b):
                for hv in range(HALVES):
                    split(src[:, hv], hv)
                for hv in range(HALVES):
                    banks(2 * C)
                    dve.wait_ge(u_taken, n["u"])
                    if not softmax:
                        for m in (t1, t2):
                            tell(v.tensor_scalar(xr[:, hv], m[:, hv], 0.0, None, ALU.min), dve_in)
                            t.more(act_out)
                            step(v.scalar_tensor_tensor(m[:, hv], m[:, hv], 0.0, xr[:, hv], ALU.max, ALU.add))
                    if n["att"]:
                        dve.wait_ge(qk_dma, 16 * HC * n["att"])
                    step(v.tensor_copy(qks[:, :, 0], t1[:, hv]))
                    step(v.tensor_copy(qks[:, :, 2], t2[:, hv]))
                    if softmax:
                        v.tensor_copy(images(qpad), by_image(t1[:, hv]))
                    for c in range(C):
                        v.tensor_copy(images(kpad[:, 0])[:, c], by_image(t2[:, hv])[:, c])
                    for c in range(C):
                        v.tensor_tensor(images(kpad[:, 1])[:, c], by_image(t2[:, hv])[:, c],
                                        by_image(qks[:, :, 2].bitcast(F32))[:, c], ALU.subtract)
                    tell(v.tensor_tensor(qks[:, :, 1], t1[:, hv], qks[:, :, 0].bitcast(F32), ALU.subtract), qk_split)
                    dve.wait_ge(vb_dma, 16 * (vcol + 1))
                    if n["att"]:
                        dve.wait_ge(v_dma, 16 * SLOTS * n["att"])
                    for g, (i0, ni) in enumerate(GROUPS):
                        r = slice(0, ni * TOK)
                        o = bank()[r, 0:D]
                        take(v.tensor_tensor(vf[r], o, vb[r, vcol % 2], ALU.add))
                        step(v.tensor_copy(vs[r, g, 0:D], vf[r]))
                        last = v.tensor_tensor(vs[r, g, D:2 * D], vf[r], vs[r, g, 0:D].bitcast(F32), ALU.subtract)
                        if g < len(GROUPS) - 1:
                            step(last)
                    tell(last, v_split)
                    n["att"] += 1
                    J = len(steps)
                    for j in range(-2, J + 1):
                        if softmax and j + 2 < J:
                            r = slice(0, GROUPS[steps[j + 2][0]][1] * TOK)
                            ni = r.stop
                            o = bank()[r, 0:HC * TOK].rearrange("p (s k) -> p s k", k=TOK)
                            take(v.tensor_reduce(shift[r, j % 2], o, AX.X, ALU.max, negate=True))
                            tell(v.tensor_tensor(mx[r, j % 2],
                                            kshape[r, K_DELTA:K_DELTA + TOK].unsqueeze(1).to_broadcast([ni, HC, TOK]),
                                            shift[r, j % 2].unsqueeze(2).to_broadcast([ni, HC, TOK]),
                                            ALU.mult), mx_ready)
                        if 0 <= j + 1 < J:
                            r = slice(0, GROUPS[steps[j + 1][0]][1] * TOK)
                            i, i3 = (j + 1) % 2, (j + 1) % 3
                            taken()
                            step(v.tensor_copy(eh[r, i3], e_t[r, i]))
                            tell(v.tensor_tensor(el[r, i3], e_t[r, i], eh[r, i3].bitcast(F32), ALU.subtract), es_ready)
                        if 0 <= j < J:
                            r = slice(0, GROUPS[steps[j][0]][1] * TOK)
                            i = j % 2
                            if softmax:
                                banks()
                                t.more(r_ready)
                            else:
                                o = bank()[r, 0:HC * TOK]
                                take(v.tensor_scalar(rs[r, i], o, ATTN_EPS, None, ALU.max))
                                step(v.reciprocal(rs[r, i], rs[r, i]))
                            step(v.tensor_tensor(e_t[r, i], e_t[r, i], rs[r, i], ALU.mult))
                            step(v.tensor_copy(eh[r, j % 3], e_t[r, i]))
                            tell(v.tensor_tensor(el[r, j % 3], e_t[r, i], eh[r, j % 3].bitcast(F32), ALU.subtract), ps_ready)
                        if 0 <= j - 1 < J:
                            banks(GROUPS[steps[j - 1][0]][1])
                for hv in range(HALVES):
                    t.more(av_dma, 16 * HC)
                    split(t1[:, hv], hv)
                residual(dst, res, out_b)

            def hidden(gated):
                taken()
                i = n["hid"] % 2
                if gated:
                    taken()
                    step(v.tensor_tensor(hf[:, i], hf[:, i], gb[:, n["gb"] % 2], ALU.mult))
                    n["gb"] += 1
                t.room(hid_used, n["hid"], HID)
                slot = n["hid"] % HID
                n["hid"] += 1
                step(v.tensor_copy(hid[:, slot, 0], hf[:, i]))
                tell(v.tensor_tensor(hid[:, slot, 1], hf[:, i], hid[:, slot, 0].bitcast(F32), ALU.subtract), hid_ready)

            def feed_forward(src, dst, b2):
                for hv in range(HALVES):
                    split(src[:, hv], hv)
                for _ in range(HALVES * FF // P):
                    hidden(False)
                residual(dst, xr, b2)

            def select(values, least, first, count, m, nb, ne, work):
                view = values.rearrange("p (b e) -> p b e", e=ne)
                lim = least.to_broadcast([m, nb, ne])
                w3 = [work[:, i].rearrange("p (b e) -> p b e", e=ne) for i in range(2)]
                step(v.tensor_tensor(w3[0], view, lim, ALU.is_gt))
                step(v.tensor_tensor(w3[1], view, lim, ALU.is_equal))
                step(v.tensor_reduce(sel_n[0:m, 0:nb], w3[0], AX.X, ALU.add))
                step(v.tensor_tensor_scan(sel_c[0:m, 0:nb * ne], first, work[:, 1], 0.0, ALU.mult, ALU.add))
                c3 = sel_c[0:m, 0:nb * ne].rearrange("p (b e) -> p b e", e=ne)
                step(v.tensor_tensor(c3, c3, sel_n[0:m, 0:nb].unsqueeze(2).to_broadcast([m, nb, ne]), ALU.add))
                step(v.scalar_tensor_tensor(work[:, 1], sel_c[0:m, 0:nb * ne], float(count), work[:, 1],
                                            ALU.is_le, ALU.mult))
                step(v.tensor_tensor(work[:, 0], work[:, 0], work[:, 1], ALU.add))
                return work[:, 0]

            def over_heads(hv, g):
                m = GROUPS[g][1] * TOK
                for i in range(3):
                    take(v.tensor_tensor(hq[0:m, D * i:D * (i + 1)], bank()[0:m, 0:D], hb[0:m, D * i:D * (i + 1)],
                                         ALU.add))
                q, k, val = (hq[0:m, D * i:D * (i + 1)].rearrange("p (a d) -> p a d", d=HD) for i in range(3))
                p4 = hp[0:m].rearrange("p (a b d) -> p a b d", a=HD, b=HD)
                s3 = h_s[0:m].rearrange("p (a b) -> p a b", b=HD)
                full = [m, HD, HD, HD]
                lim = shift[0:m].rearrange("p i s -> p (i s)")
                step(v.tensor_tensor(p4, q.unsqueeze(2).to_broadcast(full), k.unsqueeze(1).to_broadcast(full), ALU.mult))
                step(v.tensor_reduce(s3, p4, AX.X, ALU.add))
                step(v.tensor_reduce(lim, s3, AX.X, ALU.max))
                tell(v.tensor_tensor(s3, s3, lim.unsqueeze(2).to_broadcast([m, HD, HD]), ALU.subtract), dve_in)
                t.more(act_out)
                step(v.tensor_reduce(lim, s3, AX.X, ALU.add))
                step(v.reciprocal(lim, lim))
                step(v.tensor_tensor(s3, s3, lim.unsqueeze(2).to_broadcast([m, HD, HD]), ALU.mult))
                step(v.tensor_tensor(p4, s3.unsqueeze(2).to_broadcast(full),
                                     val.rearrange("p b d -> p d b").unsqueeze(1).to_broadcast(full), ALU.mult))
                n["groups"] += 1
                if n["groups"] > 1:
                    dve.wait_ge(mixed_dma, 16 * n["images"])
                n["images"] += GROUPS[g][1]
                tell(v.tensor_reduce(vf[0:m].rearrange("p (a d) -> p a d", d=HD), p4, AX.X, ALU.add), ho_ready)

            def heads_back(hv, g):
                if g >= 0:
                    i0, ni = GROUPS[g]
                    for c in range(C):
                        take(v.tensor_copy(t1[:, hv, c, TOK * i0:TOK * (i0 + ni)], bank()[:, 0:ni * TOK]))

            dve.wait_ge(k_dma, 16 * 5)
            step(v.memset(eps_t[:], LN_EPS))
            step(v.tensor_copy(mean_w[:], kshape[:, K_MEAN:K_MEAN + P]))
            step(v.tensor_copy(block_w[:], kshape[0:PITCH, K_BLOCK:K_BLOCK + PITCH]))
            step(v.tensor_copy(eye_w[:], kshape[0:ROUTED, K_IDENT:K_IDENT + ROUTED]))
            step(v.tensor_copy(rt[:, 0], rt_raw[:]))
            tell(v.tensor_tensor(rt[:, 1], rt_raw[:], rt[:, 0].bitcast(F32), ALU.subtract), k_ready)
            for hv in range(HALVES):
                t.more(patch_dma, 16)
                step(v.tensor_copy(patch_h[:, hv], patch_raw[:]))
                tell(v.tensor_tensor(patch_l[:, hv], patch_raw[:], patch_h[:, hv].bitcast(F32), ALU.subtract), patch_split)

            for hv in range(HALVES):
                banks(C)
                dve.wait_ge(u_taken, n["u"])
                split(t1[:, hv], hv)
            for hv in range(HALVES):
                for c in range(C):
                    take(v.tensor_scalar(h[:, hv, c], bank()[:, 0:NT], bc("tok_b2", c), None, ALU.add))
            dve.wait_ge(zeroed, 2)

            norms(h, x)
            norms(x, t1, "g1", "be1")
            attention(False, t1, 0, xr, x, "l0_out_b")
            norms(xr, t1, "g2", "be2")
            feed_forward(t1, t2, "l0_b2")
            for hv in range(HALVES):
                step(v.tensor_tensor(h[:, hv], h[:, hv], t2[:, hv], ALU.add))

            norms(h, x)
            for hv in range(HALVES):
                split(x[:, hv], hv)
            for hv in range(HALVES):
                o = bank()[0:RT, 0:RB * ROUTED]
                o3 = o.rearrange("p (b e) -> p b e", e=ROUTED)
                l3 = lg[:].rearrange("p (b e) -> p b e", e=ROUTED)
                p3 = pr[:].rearrange("p (b e) -> p b e", e=ROUTED)
                step(v.tensor_reduce(sel_n[:, 0:RB], o3, AX.X, ALU.max))
                tell(v.tensor_tensor(l3, o3, sel_n[:, 0:RB].unsqueeze(2).to_broadcast([RT, RB, ROUTED]), ALU.subtract), dve_in)
                t.more(act_out)
                tell(v.tensor_reduce(sel_n[:, 0:RB], p3, AX.X, ALU.add), d_taken)
                t.own(d_taken)
                step(v.reciprocal(sel_n[:, 0:RB], sel_n[:, 0:RB]))
                step(v.tensor_tensor(p3, p3, sel_n[:, 0:RB].unsqueeze(2).to_broadcast([RT, RB, ROUTED]), ALU.mult))
                for b in range(RB):
                    step(v.max(top[:, b], pr[:, ROUTED * b:ROUTED * (b + 1)]))
                keep = select(pr[:], top[:, :, TOPK - 1:TOPK], kshape[0:RT, K_FIRST:K_FIRST + RB * ROUTED],
                              TOPK, RT, RB, ROUTED, sm[:].rearrange("p (a n) -> p a n", a=2))
                tell(v.tensor_tensor(gw[:, hv], keep, pr[:], ALU.mult), gate_ready)
            for hv in range(HALVES):
                o = bank()[0:ROUTED, 0:NT]
                step(v.tensor_copy(gth[:, hv], o))
                take(v.tensor_tensor(gtl[:, hv], o, gth[:, hv].bitcast(F32), ALU.subtract))
            for e in range(SHARED + ROUTED):
                for hv in range(HALVES):
                    hidden(e >= SHARED)
            residual(h, h, None)

            norms(h, x)
            for hv in range(HALVES):
                split(x[:, hv], hv)
            dve.wait_ge(hb_dma, 16)
            for hv in range(HALVES):
                for g in range(len(GROUPS)):
                    over_heads(hv, g)
                    heads_back(hv, g - 1)
                heads_back(hv, len(GROUPS) - 1)
            for hv in range(HALVES):
                split(t1[:, hv], hv)
            residual(h, h, "l1_out_b")

            norms(h, x)
            for hv in range(HALVES):
                step(v.tensor_reduce(xm[:], by_image(x[:, hv]), AX.X, ALU.add))
                tell(v.tensor_scalar(xm[:], xm[:], 1.0 / TOK, None, ALU.mult), xm_ready)
                step(v.memset(lg1[:], -3e38))
                take(v.tensor_tensor(lg1[:, 0:EXPERTS], bank()[0:HI, 0:EXPERTS], gtb[0:HI], ALU.add))
                step(v.max(top[0:HI, 0], lg1[:]))
                tell(v.tensor_scalar(sm[0:HI, 0:EXPERTS], lg1[:, 0:EXPERTS], top[0:HI, 0, 0:1], None, ALU.subtract), dve_in)
                t.more(act_out)
                ex = sm[0:HI, 8:8 + EXPERTS]
                step(v.tensor_reduce(sel_n[0:HI, 0:1], ex, AX.X, ALU.add))
                step(v.reciprocal(sel_n[0:HI, 0:1], sel_n[0:HI, 0:1]))
                step(v.tensor_scalar(ex, ex, sel_n[0:HI, 0:1], None, ALU.mult))
                keep = select(lg1[:, 0:EXPERTS], top[0:HI, 0:1, TOP2 - 1:TOP2], kshape[0:HI, K_FIRST:K_FIRST + EXPERTS],
                              TOP2, HI, 1, EXPERTS, sm[0:HI, 16:16 + 2 * EXPERTS].rearrange("p (a n) -> p a n", a=2))
                step(v.tensor_tensor(keep, keep, ex, ALU.mult))
                tell(v.tensor_tensor(wx[:], keep.unsqueeze(2).to_broadcast([HI, EXPERTS, HI]),
                                kshape[0:HI, K_EYE8:K_EYE8 + HI].unsqueeze(1).to_broadcast([HI, EXPERTS, HI]),
                                ALU.mult), wx_ready)
                o = bank()[:, 0:EXPERTS * HI].rearrange("p (e i) -> p e i", i=HI)
                take(v.tensor_copy(wimg[:, hv], o))
            for e in range(EXPERTS):
                attention(True, x, 1 + e, xr, x, f"e{e}_out_b")
                norms(xr, xr, f"e{e}_g1", f"e{e}_be1")
                feed_forward(xr, xr, f"e{e}_b2")
                norms(xr, xr, f"e{e}_g2", f"e{e}_be2")
                for hv in range(HALVES):
                    for c in range(C):
                        step(v.tensor_tensor(by_image(t1[:, hv])[:, c], by_image(xr[:, hv])[:, c],
                                             wimg[:, hv, e].unsqueeze(2).to_broadcast([P, HI, TOK]), ALU.mult))
                    last = v.tensor_tensor(h[:, hv], h[:, hv], t1[:, hv], ALU.add)
                    if e == EXPERTS - 1:
                        tell(last, out_ready)
                    else:
                        step(last)


def blocks(w, order):
    k, m = w.shape[0] // P, w.shape[1] // P
    b = w.reshape(k, P, m, P)
    return b.transpose((1, 2, 0, 3) if order == "mk" else (1, 0, 2, 3)).reshape(P, -1)


def expert_pairs(w1, w2):
    a, b = blocks(w1, "mk"), blocks(w2, "km")
    n = a.shape[1] // TILE
    parts = []
    for p in range(n + 1):
        if p < n:
            parts.append(a[:, TILE * p:TILE * (p + 1)])
        if p:
            parts.append(b[:, TILE * (p - 1):TILE * p])
    return parts


def attention_weights(wq, wk, wv, wo):
    return [blocks(wq, "mk"), blocks(wk, "mk"), blocks(wv, "km"), blocks(wo, "mk")]


def kernel(**inputs):
    import concourse.bacc as bacc
    from concourse.bass_utils import run_bass_kernel_spmd

    a = {k: np.asarray(v) for k, v in inputs.items()}
    patches = a["x"].reshape(HALVES, HI, 3, 6, 16, 6, 16).transpose(0, 2, 4, 6, 1, 3, 5)
    patches = patches.reshape(HALVES, KP, P, NT).transpose(0, 2, 1, 3)

    parts = [blocks(a["L0_tok_W1"], "mk"), blocks(a["L0_tok_W2"], "mk")]
    qkv = a["L0_attn_qkv_w"]
    parts += attention_weights(qkv[:, 0:D], qkv[:, D:2 * D], qkv[:, 2 * D:], a["L0_attn_out_w"])
    parts += expert_pairs(a["L0_attn_w1"], a["L0_attn_w2"])
    ups = list(a["L0_ffn_shared_up"]) + list(a["L0_ffn_routed_up"])
    downs = list(a["L0_ffn_shared_down"]) + list(a["L0_ffn_routed_down"])
    for up, down in zip(ups, downs):
        parts += [blocks(up.T, "mk"), blocks(down.T, "mk")]
    parts += [blocks(a[f"L1_attn_W{n}"].T, "km") for n in "qkv"] + [blocks(a["L1_attn_Wo"].T, "mk")]
    for e in range(EXPERTS):
        qkv = a["L1_ffn_in_proj_w"][e]
        parts += attention_weights(qkv[0:D].T, qkv[D:2 * D].T, qkv[2 * D:].T, a["L1_ffn_out_proj_w"][e].T)
        parts += expert_pairs(a["L1_ffn_lin1_w"][e].T, a["L1_ffn_lin2_w"][e].T)

    vectors = {"tok_b1": a["L0_tok_b1"], "tok_b2": a["L0_tok_b2"], "l0_qk_b": a["L0_attn_qkv_b"][0:2 * D],
               "l0_out_b": a["L0_attn_out_b"], "l0_b1": a["L0_attn_b1"], "l0_b2": a["L0_attn_b2"],
               "g1": a["L0_attn_g1"], "be1": a["L0_attn_be1"], "g2": a["L0_attn_g2"], "be2": a["L0_attn_be2"],
               "l1_out_b": a["L1_attn_bo"]}
    vbias = [a["L0_attn_qkv_b"][2 * D:]]
    for e in range(EXPERTS):
        f = {n: a[f"L1_ffn_{n}"][e] for n in ("in_proj_b", "out_proj_b", "lin1_b", "lin2_b", "ln1_w", "ln1_b",
                                              "ln2_w", "ln2_b")}
        vectors |= {f"e{e}_qk_b": f["in_proj_b"][0:2 * D], f"e{e}_out_b": f["out_proj_b"], f"e{e}_b1": f["lin1_b"],
                    f"e{e}_b2": f["lin2_b"], f"e{e}_g1": f["ln1_w"], f"e{e}_be1": f["ln1_b"],
                    f"e{e}_g2": f["ln2_w"], f"e{e}_be2": f["ln2_b"]}
        vbias.append(f["in_proj_b"][2 * D:])
    bcol, _ = bias_columns()
    biases = np.concatenate([vectors[n].reshape(k, P).T for n, (_, k) in bcol.items()], axis=1)

    arrays = {
        "patches": patches,
        "weights": np.concatenate(parts, axis=1),
        "biases": biases,
        "vbias": np.stack(vbias),
        "hbias": np.concatenate([a["L1_attn_bq"], a["L1_attn_bk"], a["L1_attn_bv"]]),
        "router": blocks_narrow(a["L0_ffn_router_w"].T),
        "gate": blocks_narrow(a["L1_ffn_gate_w"].T),
        "gate_b": a["L1_ffn_gate_b"],
        "constants": shape_constants(),
    }
    arrays = {f"in_{k}": np.ascontiguousarray(v) for k, v in arrays.items()}

    nc = bacc.Bacc("TRN2", target_bir_lowering=False, num_devices=1)
    args = [nc.dram_tensor(k, v.shape, mybir.dt.from_np(v.dtype), kind="ExternalInput").ap()
            for k, v in arrays.items()]
    out = nc.dram_tensor("out", (HALVES, P, C, NT), F32, kind="ExternalOutput").ap()
    mixed = nc.dram_tensor("mixed", (IMAGES, HD, TOK, HD), F32, kind="Internal").ap()
    build_tower(nc, *args, out, mixed)
    r = run_bass_kernel_spmd(nc, [arrays], core_ids=[0])
    got = r.results[0]["out"]
    return got.transpose(0, 3, 2, 1).reshape(IMAGES, TOK, D)


def blocks_narrow(w):
    return w.reshape(C, P, -1).transpose(1, 0, 2).reshape(P, -1)
```

```python
from collections import Counter
from contextlib import ExitStack

import numpy as np

import concourse.bass as bass
from concourse import mybir

F32 = mybir.dt.float32
F32R = mybir.dt.float32r
ALU = mybir.AluOpType
ACT = mybir.ActivationFunctionType
AX = mybir.AxisListType

P = 128
D = 256
C = D // P
IMAGES = 16
TOK = 36
HALVES = 2
HI = IMAGES // HALVES
NT = HI * TOK
HD = 16
HC = P // HD
PATCH = 768
KP = PATCH // P
FF = 1024
ROUTED, SHARED, TOPK = 16, 2, 4
EXPERTS, TOP2 = 4, 2
LN_EPS = 1e-5
ATTN_EPS = 1e-6
GROUPS = [(0, 3), (3, 3), (6, 2)]
SLOTS = 3
PITCH = SLOTS * TOK
LEAD = (SLOTS - 1) * TOK
PADDED = LEAD + HI * PITCH
TILE = 512
RING = 5
STAGES = 2
RT = 96
RB = NT // RT
UB = 4
WB = 4
HID = 8


def bias_columns():
    names = [("tok_b1", 2), ("tok_b2", 2), ("l0_qk_b", 4), ("l0_out_b", 2), ("l0_b1", 8), ("l0_b2", 2),
             ("g1", 2), ("be1", 2), ("g2", 2), ("be2", 2), ("l1_out_b", 2)]
    for e in range(EXPERTS):
        names += [(f"e{e}_qk_b", 4), (f"e{e}_out_b", 2), (f"e{e}_b1", 8), (f"e{e}_b2", 2),
                  (f"e{e}_g1", 2), (f"e{e}_be1", 2), (f"e{e}_g2", 2), (f"e{e}_be2", 2)]
    at, out = 0, {}
    for name, n in names:
        out[name] = (at, n)
        at += n
    return out, at


TOK_TILES = (PATCH + D) * D // (P * TILE)
ATT_ALONE = 4 * D * D // (P * TILE)
BLOCK_TILES = ATT_ALONE + 2 * D * FF // (P * TILE)
MOE_TILES = SHARED + ROUTED
ATT_TILES = [TOK_TILES] + [TOK_TILES + BLOCK_TILES + MOE_TILES + ATT_ALONE + e * BLOCK_TILES for e in range(EXPERTS)]

K_MEAN = 0
K_BLOCK = K_MEAN + P
K_DELTA = K_BLOCK + PITCH
K_IDENT = K_DELTA + TOK
K_FIRST = K_IDENT + P
K_EYE8 = K_FIRST + RB * ROUTED
K_ONES = K_EYE8 + HI
K_SHAPE = K_ONES + P


def shape_constants():
    k = np.zeros((P, K_SHAPE), np.float32)
    k[:, K_MEAN:K_MEAN + P] = 1.0 / D
    r = np.arange(PITCH)
    k[:PITCH, K_BLOCK:K_BLOCK + PITCH] = r[:, None] // TOK == r[None] // TOK
    k[:PITCH, K_DELTA:K_DELTA + TOK] = r[:, None] % TOK == np.arange(TOK)[None]
    k[:, K_IDENT:K_IDENT + P] = np.eye(P)
    k[:, K_FIRST:K_FIRST + RB * ROUTED] = np.arange(RB * ROUTED) % ROUTED != 0
    k[:HI, K_EYE8:K_EYE8 + HI] = np.eye(HI)
    k[:, K_ONES:K_ONES + P] = 1.0
    return k


def build_tower(nc, patches, weights, biases, vbias, hbias, router, gate, gate_b, constants, out, mixed):
    bcol, nbias = bias_columns()
    tiles = weights.shape[1] // TILE

    with ExitStack() as ctx:
        def sb(name, shape, dt=F32):
            return ctx.enter_context(nc.sbuf_tensor(name, shape, dt))

        def sem(name):
            return ctx.enter_context(nc.semaphore(name))

        u_ring = [ctx.enter_context(nc.psum_tensor(f"u_ring{i}", [P, TILE], F32)) for i in range(UB)]
        w_ring = [ctx.enter_context(nc.psum_tensor(f"w_ring{i}", [P, TILE], F32)) for i in range(WB)]

        kshape = sb("kshape", [P, K_SHAPE])
        block_w = sb("block_w", [PITCH, PITCH], F32R)
        eye_w = sb("eye_w", [ROUTED, ROUTED], F32R)
        bias = sb("bias", [P, nbias])
        vb = sb("vb", [P, 2, D])
        rt_raw = sb("rt_raw", [P, C * ROUTED])
        rt = sb("rt", [P, 2, C * ROUTED], F32R)
        gt = sb("gt", [P, C * EXPERTS])
        gtb = sb("gtb", [P, EXPERTS])
        stage = sb("stage", [P, STAGES, TILE])
        wh = sb("wh", [P, RING, TILE], F32R)
        wl = sb("wl", [P, RING, TILE], F32R)

        h = sb("h", [P, HALVES, C, NT])
        x = sb("x", [P, HALVES, C, NT])
        xr = sb("xr", [P, HALVES, C, NT])
        t1 = sb("t1", [P, HALVES, C, NT])
        t2 = sb("t2", [P, HALVES, C, NT])
        ah = sb("ah", [P, HALVES, C, NT], F32R)
        al = sb("al", [P, HALVES, C, NT], F32R)
        rstd = sb("rstd", [P, 2, NT])

        qpad = sb("qpad", [P, C, PADDED], F32R)
        kpad = sb("kpad", [P, 2, C, PADDED], F32R)
        vs = sb("vs", [PITCH, 3, 2 * D], F32R)
        vm = sb("vm", [PITCH, SLOTS, 3, 2 * D], F32R)
        vf = sb("vf", [PITCH, D])
        shift = sb("shift", [PITCH, 2, HC])
        mx = sb("mx", [PITCH, 2, HC, TOK], F32R)
        e_t = sb("e_t", [PITCH, 2, HC * TOK])
        eh = sb("eh", [PITCH, 3, HC * TOK], F32R)
        el = sb("el", [PITCH, 3, HC * TOK], F32R)
        rs = sb("rs", [PITCH, 2, HC * TOK])

        hf = sb("hf", [P, 2, NT])
        lg = sb("lg", [RT, RB * ROUTED])
        pr = sb("pr", [RT, RB * ROUTED])
        gw = sb("gw", [RT, HALVES, RB * ROUTED])
        eps_t = sb("eps_t", [P, 1])
        sm = sb("sm", [RT, 2 * ROUTED * RB])
        sel_n = sb("sel_n", [RT, 4])
        sel_c = sb("sel_c", [RT, RB * ROUTED])
        top = sb("top", [RT, RB, 8])
        xm = sb("xm", [P, C, HI])
        lg1 = sb("lg1", [HI, 8])
        wx = sb("wx", [HI, EXPERTS, HI])
        wimg = sb("wimg", [P, HALVES, EXPERTS, HI])

        with nc.sbuf_tensor("gb", [P, 2, NT], F32) as gb, \
                nc.sbuf_tensor("gth", [ROUTED, HALVES, NT], F32R) as gth, \
                nc.sbuf_tensor("gtl", [ROUTED, HALVES, NT], F32R) as gtl:
            pass
        qks = sb("qks", [P, C, 3, NT], F32R)
        with nc.sbuf_tensor("patch_raw", [P, KP, NT], F32) as patch_raw, \
                nc.sbuf_tensor("patch_h", [P, HALVES, KP, NT], F32R) as patch_h, \
                nc.sbuf_tensor("patch_l", [P, HALVES, KP, NT], F32R) as patch_l:
            pass
        with nc.sbuf_tensor("head_products", [PITCH, HD ** 3], F32) as head_products:
            pass
        qkx = sb("qkx", [P, HC, C, 3, NT], F32R)
        with nc.sbuf_tensor("av", [P, C, HC, NT], F32) as av:
            pass
        hid = sb("hid", [P, HID, 2, NT], F32R)

        k_dma = sem("k_dma")
        patch_dma = sem("patch_dma")
        stage_dma = [sem(f"stage_dma{i}") for i in range(STAGES)]
        w_ready = sem("w_ready")
        w_used = sem("w_used")
        k_ready = sem("k_ready")
        zeroed = sem("zeroed")
        patch_split = sem("patch_split")
        u_full, u_taken = sem("u_full"), sem("u_taken")
        d_full, d_taken = sem("d_full"), sem("d_taken")
        a_split = sem("a_split")
        norm_in = sem("norm_in")
        squared = sem("squared")
        act_out = sem("act_out")
        dve_in = sem("dve_in")
        dve_step = sem("dve_step")
        qk_split = sem("qk_split")
        hb_dma = sem("hb_dma")
        ho_ready = sem("ho_ready")
        h_soft = sem("h_soft")
        h_mixed = sem("h_mixed")
        mixed_dma = sem("mixed_dma")
        back_dma = [sem(f"back_dma{i}") for i in range(2)]
        vb_dma = sem("vb_dma")
        qk_dma = [sem(f"qk_dma{c}") for c in range(C)]
        v_split = sem("v_split")
        v_dma = [sem(f"v_dma{c}") for c in range(C)]
        mx_ready = sem("mx_ready")
        r_ready = sem("r_ready")
        ps_ready = sem("ps_ready")
        av_dma = [sem(f"av_dma{c}") for c in range(C)]
        hid_ready = sem("hid_ready")
        hid_used = sem("hid_used")
        gate_ready = sem("gate_ready")
        xm_ready = sem("xm_ready")
        wx_ready = sem("wx_ready")
        out_ready = sem("out_ready")
        out_dma = sem("out_dma")

        flat = "p h c n -> p (h c n)"
        hb = xr[:].rearrange(flat)[:, 0:3 * D]
        hq = t2[0:PITCH].rearrange(flat)[:, 0:4 * D]
        hp = av[0:PITCH].rearrange("p c s n -> p (c s n)")[:, 0:HD ** 3]
        hv_p = head_products[:]
        units = [(hv, g) for hv in range(HALVES) for g in range(len(GROUPS))]
        cube = [HD, HD, HD]

        def h_s(u):
            return e_t[0:GROUPS[units[u][1]][1] * TOK, u % 2, 0:D]

        block = ctx.enter_context(nc.Block())

        def bc(name, i):
            return bias[:, bcol[name][0] + i:bcol[name][0] + i + 1]

        class Tally:

            def __init__(self, eng):
                self.eng, self.n = eng, Counter()

            def up(self, s, by=1):
                self.n[s.name] += by
                return s, by

            def more(self, s, by=1):
                self.n[s.name] += by
                self.eng.wait_ge(s, self.n[s.name])

            def own(self, s):
                self.eng.wait_ge(s, self.n[s.name])

            def room(self, s, used, size):
                if used >= size:
                    self.eng.wait_ge(s, used - size + 1)

        steps = [(hv, c, g) for hv in range(HALVES) for c in range(C) for g in range(len(GROUPS))]
        J, G = len(steps), len(GROUPS)
        ROUNDS = range(-2, J + 1)
        PREPARE = {G - 2 + G * c: c for c in range(C)}
        N2_VAR = -1
        OUT_P = 2 * J // 3 + 1
        N1_VAR = OUT_P + 3

        def u_rounds(softmax, before, base):
            u, out = base + 2 * C, {}
            for j in ROUNDS:
                u += (0 <= j + 1 < J) + (softmax and 0 <= j < J)
                if 0 <= j - 1 < J:
                    hv, c, g = steps[j - 1]
                    u += GROUPS[g][1]
                    out[hv, c] = u
                u += 2 * (j in PREPARE) + HALVES * (before and j == N2_VAR) + (j == N1_VAR)
            return out, u + 1

        norm_u, ff_u = HALVES, HALVES * FF // P
        av_full = []
        banks_u = HALVES * C + 2 * norm_u
        for blk in range(1 + EXPERTS):
            products_at, banks_u = u_rounds(blk > 0, blk > 1, banks_u)
            av_full.append(products_at)
            banks_u += ff_u
            if blk == 0:
                banks_u += norm_u + HALVES * (SHARED + 2 * ROUTED) + 2 * norm_u

        @block.gpsimd
        def _(pool):
            def load(i):
                pool.dma_start(stage[:, i % STAGES], weights[:, TILE * i:TILE * (i + 1)]
                               ).then_inc(stage_dma[i % STAGES], 16)

            t = Tally(pool)

            def expand_v(c):
                for s in range(SLOTS):
                    r = slice(TOK * s, TOK * (s + 1))
                    g = sum(ni > s for _, ni in GROUPS)
                    to, come = (ap[:, 0:g].bitcast(F32).rearrange("p g (l d) -> p (g l) d", l=2)[:, :, P * c:P * (c + 1)]
                                for ap in (vm[r, s], vs[r]))
                    pool.dma_start(to, come).then_inc(v_dma[c], 16)

            first_tile = {}
            for blk in range(1 + EXPERTS):
                first_tile[ATT_TILES[blk] + RING] = (blk, 0)
                first_tile[ATT_TILES[blk] + RING + C + 1] = (blk, 1)

            load(0)
            load(1)
            for i in range(tiles):
                if i == 4:
                    for z in (qpad, kpad, vm):
                        last = nc.gpsimd.memset(z[:].bitcast(F32), 0.0)
                    last.then_inc(zeroed, 1)
                    pool.wait_ge(u_full, HALVES * C)
                    nc.gpsimd.memset(qkx[:].bitcast(F32), 0.0).then_inc(zeroed, 1)
                if i == ATT_TILES[1] - ATT_ALONE + RING:
                    for u, (hv, g) in enumerate(units):
                        m = GROUPS[g][1] * TOK
                        pool.wait_ge(h_soft, u + 1)
                        val = hq[0:m, D * (2 + u % 2):D * (3 + u % 2)].rearrange("p (b d) -> p d b", d=HD)
                        nc.gpsimd.tensor_tensor(hv_p[0:m].rearrange("p (a d b) -> p a d b", a=HD, b=HD),
                                                h_s(u).rearrange("p (a b) -> p a b", b=HD).unsqueeze(2)
                                                .to_broadcast([m] + cube),
                                                val.unsqueeze(1).to_broadcast([m] + cube), ALU.mult
                                                ).then_inc(h_mixed, 1)
                    pool.wait_ge(ho_ready, len(units))
                    nc.gpsimd.memset(qkx[:].bitcast(F32).rearrange("p s c i n -> p (s c i n)")[:, 0:HD ** 3], 0.0
                                     ).then_inc(zeroed, 1)
                if i in first_tile:
                    blk, part = first_tile[i]
                    if part == 0:
                        t.more(v_split)
                        for c in range(C):
                            expand_v(c)
                        t.more(v_split)
                        pool.wait_ge(u_taken, av_full[blk][0, 0])
                        expand_v(0)
                    else:
                        pool.wait_ge(u_taken, av_full[blk][0, 1])
                        expand_v(1)
                raw = stage[:, i % STAGES]
                pool.wait_ge(stage_dma[i % STAGES], 16 * (i // STAGES + 1))
                if i >= RING:
                    pool.wait_ge(w_used, i - RING + 1)
                nc.gpsimd.tensor_copy(wh[:, i % RING], raw).then_inc(w_ready, 1)
                pool.wait_ge(w_ready, 2 * i + 1)
                nc.gpsimd.tensor_tensor(wl[:, i % RING], raw, wh[:, i % RING].bitcast(F32),
                                        ALU.subtract).then_inc(w_ready, 1)
                if i + STAGES < tiles:
                    pool.wait_ge(w_ready, 2 * (i + 1))
                    load(i + STAGES)

        @block.sync
        def _(sp):
            t = Tally(sp)
            for dst, src in ((kshape, constants), (bias, biases), (rt_raw, router), (gt, gate)):
                sp.dma_start(dst[:], src).then_inc(k_dma, 16)
            sp.dma_start(gtb[:], gate_b.partition_broadcast(P)).then_inc(k_dma, 16)
            for hv in range(HALVES):
                if hv:
                    sp.wait_ge(patch_split, hv)
                sp.dma_start(patch_raw[:], patches[hv]).then_inc(patch_dma, 16)

            for n in range(1 + EXPERTS):
                if n == 1:
                    sp.wait_ge(gate_ready, 1)
                    sp.dma_start(hb[:], hbias.partition_broadcast(P)).then_inc(hb_dma, 16)
                    for u, (hv, g) in enumerate(units):
                        i0, ni = GROUPS[g]
                        t.more(ho_ready)
                        for i in range(ni):
                            sp.dma_start(mixed[HI * hv + i0 + i].rearrange("a t d -> t a d"),
                                         vf[TOK * i:TOK * (i + 1)].rearrange("t (a d) -> t a d", d=HD)
                                         ).then_inc(mixed_dma, 16)
                        t.more(mixed_dma, 16 * ni)
                        sp.dma_start(rs[0:ni * TOK, u % 2, 0:D],
                                     mixed[HI * hv + i0:HI * hv + i0 + ni].rearrange("i a t d -> (i a t d)")
                                     .rearrange("(r f) -> r f", f=D)
                                     ).then_inc(back_dma[u % 2], 16)
                if n > 1:
                    sp.wait_ge(v_split, HALVES * (n - 1))
                sp.dma_start(vb[:, n % 2], vbias[n].partition_broadcast(P)).then_inc(vb_dma, 16)

                if n == 1:
                    sp.wait_ge(zeroed, 3)

                def expand(c):
                    t.more(qk_split)
                    for s in range(HC):
                        r = slice(HD * s, HD * (s + 1))
                        sp.dma_start(qkx[r, s, c].bitcast(F32), qks[r, c].bitcast(F32)).then_inc(qk_dma[c], 16)

                def extract(hv, c):
                    sp.wait_ge(u_taken, av_full[n][hv, c])
                    for s in range(HC):
                        r = slice(HD * s, HD * (s + 1))
                        sp.dma_start(t1[r, hv, c], av[r, c, s]).then_inc(av_dma[c], 16)

                for c in range(C):
                    expand(c)
                for c in range(C):
                    expand(c)
                    extract(0, c)
                for c in range(C):
                    extract(1, c)
            for hv in range(HALVES):
                t.more(out_ready)
                sp.dma_start(out[hv], h[:, hv]).then_inc(out_dma, 16)
            sp.wait_ge(out_dma, 16 * HALVES)

        @block.tensor
        def _(pe):
            t = Tally(pe)
            n = Counter()

            def u_bank():
                t.room(u_taken, n["u"], UB)
                n["u"] += 1
                return u_ring[(n["u"] - 1) % UB]

            def d_bank():
                t.room(d_taken, n["d"], WB)
                n["d"] += 1
                return w_ring[(n["d"] - 1) % WB]

            def product(o, lhs, rhs, start, stop):
                first = nc.tensor.matmul(o, lhs[0], rhs[0], start=start, stop=False)
                second = nc.tensor.matmul(o, lhs[0], rhs[1], start=False, stop=False)
                if n["tiles_done"]:
                    first.then_inc(w_used, n["tiles_done"])
                    n["tiles_done"] = 0
                if n["hid_done"]:
                    second.then_inc(hid_used, n["hid_done"])
                    n["hid_done"] = 0
                return nc.tensor.matmul(o, lhs[1], rhs[0], start=False, stop=stop)

            def tile(i):
                pe.wait_ge(w_ready, 2 * (n["tile"] + i + 1))
                return (n["tile"] + i) % RING

            def done(k):
                n["tile"] += k
                n["tiles_done"] += k

            def w(s, col, width=P):
                return wh[:, s, col:col + width], wl[:, s, col:col + width]

            def a(hv, k, cols=slice(0, NT)):
                return ah[:, hv, k, cols], al[:, hv, k, cols]

            def feature_mean(o, src, full):
                for k in range(C):
                    last = nc.tensor.matmul(o[:, 0:NT], kshape[:, K_MEAN:K_MEAN + P], src[:, k],
                                            start=(k == 0), stop=(k == C - 1))
                last.then_inc(full, 1)

            def mean(src, hv, added=None):
                if added:
                    pe.wait_ge(d_taken, added)
                else:
                    t.more(norm_in)
                feature_mean(d_bank(), src[:, hv], d_full)

            def variance(hv):
                t.more(squared)
                feature_mean(u_bank(), t2[:, hv], u_full)

            def norms(src, residual):
                ends = [n["d"] - C * (HALVES - 1 - hv) if residual else None for hv in range(HALVES)]
                for hv in range(HALVES):
                    mean(src, hv, ends[hv])
                for hv in range(HALVES):
                    variance(hv)

            def linear2(hv, s, bank, full):
                for m in range(2):
                    o = bank()[:, 0:NT]
                    for k in range(C):
                        last = product(o, w(s, P * (2 * m + k)), a(hv, k), k == 0, k == C - 1)
                    last.then_inc(full, 1)
                return last

            def attention(softmax, before):
                first, xr_before = n["tile"], n["d"]
                scores = {}

                def out_proj(hv):
                    t.more(a_split)
                    n["tile"] = first + 3
                    linear2(hv, tile(0), d_bank, d_full)
                    n["tile"] = first
                    return n["d"]

                def prepare(hv, c):
                    if c == 0:
                        t.more(a_split)
                    for i in range(2):
                        s, o = tile(i), u_bank()[:, 0:NT]
                        for k in range(C):
                            last = product(o, w(s, P * (C * c + k)), a(hv, k), k == 0, k == C - 1)
                        last.then_inc(u_full, 1)
                    if c == 0:
                        s = tile(2)
                        for i0, ni in GROUPS:
                            o = d_bank()[0:ni * TOK, 0:D]
                            for k in range(C):
                                last = product(o, a(hv, k, slice(TOK * i0, TOK * (i0 + ni))),
                                               w(s, D * k, D), k == 0, k == C - 1)
                            last.then_inc(d_full, 1)

                def images(step):
                    hv, c, g = step
                    i0, ni = GROUPS[g]
                    for i in range(ni):
                        at = PITCH * (i0 + i) + LEAD - TOK * i
                        yield (slice(at, at + ni * TOK), slice(TOK * (i0 + i), TOK * (i0 + i + 1)),
                               i == 0, i == ni - 1)

                for c in range(C):
                    prepare(0, c)
                if before:
                    for hv in range(HALVES):
                        mean(xr, hv, xr_before - C * (HALVES - 1 - hv))
                for j in ROUNDS:
                    if j + 2 < J:
                        hv, c, g = steps[j + 2]
                        r = slice(0, GROUPS[g][1] * TOK)
                        if g == 0 and softmax:
                            t.more(qk_dma[c], 16 * HC)
                        if softmax:
                            o = d_bank()[r, 0:HC * TOK]
                            for padded, own, start, stop in images(steps[j + 2]):
                                last = nc.tensor.matmul(o, qpad[:, c, padded], qkx[:, :, c, 2, own], start=start, stop=stop)
                            last.then_inc(d_full, 1)
                    if 0 <= j + 1 < J:
                        hv, c, g = steps[j + 1]
                        r = slice(0, GROUPS[g][1] * TOK)
                        if g == 0 and not softmax:
                            t.more(qk_dma[c], 16 * HC)
                        o = u_bank()[r, 0:HC * TOK]
                        for padded, own, start, stop in images(steps[j + 1]):
                            last = product(o, (kpad[:, 0, c, padded], kpad[:, 1, c, padded]),
                                           (qkx[:, :, c, 0, own], qkx[:, :, c, 1, own]), start, stop and not softmax)
                        if softmax:
                            t.more(mx_ready)
                            last = nc.tensor.matmul(o, block_w[r, r], mx[r, (j + 1) % 2], start=False, stop=True)
                        last.then_inc(u_full, 1)
                        scores[j + 1] = n["u"]
                    if 0 <= j < J:
                        r = slice(0, GROUPS[steps[j][2]][1] * TOK)
                        pe.wait_ge(u_taken, scores[j])
                        o = (u_bank() if softmax else d_bank())[r, 0:HC * TOK]
                        nc.tensor.matmul(o, kshape[r, K_BLOCK:K_BLOCK + r.stop], e_t[r, j % 2], start=True, stop=True
                                         ).then_inc(u_full if softmax else d_full, 1)
                    if 0 <= j - 1 < J:
                        hv, c, g = steps[j - 1]
                        i0, ni = GROUPS[g]
                        r = slice(0, ni * TOK)
                        if g == 0:
                            t.more(v_dma[c], 16 * SLOTS)
                        t.more(ps_ready)
                        for i in range(ni):
                            o = u_bank()[:, 0:HC * TOK]
                            product(o, (vm[r, i, g, P * c:P * (c + 1)], vm[r, i, g, D + P * c:D + P * (c + 1)]),
                                    (eh[r, (j - 1) % 3], el[r, (j - 1) % 3]), True, True
                                    ).then_inc(u_full, 1)
                    if j in PREPARE:
                        prepare(1, PREPARE[j])
                        if PREPARE[j] == C - 1:
                            n["tiles_done"] += 3
                    if before and j == N2_VAR:
                        for hv in range(HALVES):
                            variance(hv)
                    if j == OUT_P:
                        residual = out_proj(0)
                    if j == OUT_P + 1:
                        mean(xr, 0, residual)
                    if j == N1_VAR:
                        variance(0)
                residual = out_proj(1)
                n["tile"] += 4
                n["tiles_done"] += 1
                t.more(a_split)
                mean(xr, 1, residual)
                variance(1)

            def feed_forward():
                acc = [[d_bank() for _ in range(C)] for _ in range(HALVES)]
                t.more(a_split)
                pairs = FF // P // 2
                for p in range(pairs + 1):
                    if p < pairs:
                        s = tile(0)
                        for hv in range(HALVES):
                            linear2(hv, s, u_bank, u_full)
                        done(1)
                    if p:
                        s = tile(0)
                        for hv in range(HALVES):
                            for i in range(2):
                                t.more(hid_ready)
                                slot = n["hid"] % HID
                                n["hid"] += 1
                                for m in range(C):
                                    last = product(acc[hv][m][:, 0:NT], w(s, P * (2 * i + m)),
                                                   (hid[:, slot, 0], hid[:, slot, 1]),
                                                   p == 1 and i == 0, p == pairs and i == 1)
                                    if p == pairs and i == 1:
                                        last.then_inc(d_full, 1)
                                n["hid_done"] += 1
                        done(1)

            def back(u):
                if u >= 0:
                    m = GROUPS[units[u][1]][1] * TOK
                    t.more(back_dma[u % 2], 16)
                    for c in range(C):
                        nc.tensor.transpose(d_bank()[:, 0:m], rs[0:m, u % 2, P * c:P * (c + 1)],
                                            kshape[0:m, K_IDENT:K_IDENT + m]).then_inc(d_full, 1)

            pe.wait_ge(k_ready, 1)
            t.more(patch_split, HALVES)
            for hv in range(HALVES):
                for m in range(C):
                    o = u_bank()[:, 0:NT]
                    for k in range(KP):
                        b = KP * m + k
                        s = tile(b // 4)
                        last = product(o, w(s, P * (b % 4)), (patch_h[:, hv, k], patch_l[:, hv, k]),
                                       k == 0, k == KP - 1)
                    last.then_inc(u_full, 1)
            done(3)
            s = tile(0)
            for hv in range(HALVES):
                t.more(a_split)
                linear2(hv, s, d_bank, d_full)
            done(1)

            norms(h, True)
            norms(x, False)
            pe.wait_ge(zeroed, 2)
            attention(False, False)
            feed_forward()

            norms(h, False)
            acc = None
            for hv in range(HALVES):
                t.more(a_split)
                o = d_bank()
                for b in range(RB):
                    for k in range(C):
                        last = product(o[0:RT, ROUTED * b:ROUTED * (b + 1)], a(hv, k, slice(RT * b, RT * (b + 1))),
                                       (rt[:, 0, ROUTED * k:ROUTED * (k + 1)], rt[:, 1, ROUTED * k:ROUTED * (k + 1)]),
                                       k == 0, k == C - 1)
                last.then_inc(d_full, 1)
            for hv in range(HALVES):
                t.more(gate_ready)
                o = d_bank()
                for b in range(RB):
                    last = nc.tensor.transpose(o[0:ROUTED, RT * b:RT * (b + 1)], gw[:, hv, ROUTED * b:ROUTED * (b + 1)],
                                               kshape[0:RT, K_IDENT:K_IDENT + RT])
                last.then_inc(d_full, 1)
            gates = n["d"]
            acc = [[d_bank() for _ in range(C)] for _ in range(HALVES)]
            E = SHARED + ROUTED
            for e in range(E + 1):
                if e < E:
                    s = tile(1 if e else 0)
                    for hv in range(HALVES):
                        o = u_bank()[:, 0:NT]
                        for k in range(C):
                            last = product(o, w(s, P * k), a(hv, k), k == 0, k == C - 1)
                        last.then_inc(u_full, 1)
                        if e >= SHARED:
                            if e == SHARED and hv == 0:
                                pe.wait_ge(d_taken, gates)
                            r = e - SHARED
                            o = u_bank()[:, 0:NT]
                            pick = eye_w[:, r:r + 1].to_broadcast([ROUTED, P])
                            nc.tensor.matmul(o, pick, gth[:, hv], start=True, stop=False)
                            nc.tensor.matmul(o, pick, gtl[:, hv], start=False, stop=True
                                             ).then_inc(u_full, 1)
                if e:
                    s = tile(0)
                    for hv in range(HALVES):
                        t.more(hid_ready)
                        slot = n["hid"] % HID
                        n["hid"] += 1
                        for m in range(C):
                            last = product(acc[hv][m][:, 0:NT], w(s, P * (2 + m)), (hid[:, slot, 0], hid[:, slot, 1]),
                                           e == 1, e == E)
                            if e == E:
                                last.then_inc(d_full, 1)
                        n["hid_done"] += 1
                    done(1)

            norms(h, True)
            t.more(a_split, HALVES)
            for u in range(len(units) + 2):
                if u < len(units):
                    hv, g = units[u]
                    i0, ni = GROUPS[g]
                    for i in range(3):
                        s = tile(i)
                        o = d_bank()[0:ni * TOK, 0:D]
                        for k in range(C):
                            last = product(o, a(hv, k, slice(TOK * i0, TOK * (i0 + ni))), w(s, D * k, D),
                                           k == 0, k == C - 1)
                        last.then_inc(d_full, 1)
                back(u - 2)
            done(3)
            s = tile(0)
            for hv in range(HALVES):
                t.more(a_split)
                linear2(hv, s, d_bank, d_full)
            done(1)

            norms(h, True)
            for hv in range(HALVES):
                t.more(xm_ready)
                o = d_bank()[0:HI, 0:EXPERTS]
                for k in range(C):
                    last = nc.tensor.matmul(o, xm[:, k], gt[:, EXPERTS * k:EXPERTS * (k + 1)],
                                            start=(k == 0), stop=(k == C - 1))
                last.then_inc(d_full, 1)
                t.more(wx_ready)
                o = d_bank()[:, 0:EXPERTS * HI]
                nc.tensor.matmul(o, kshape[0:HI, K_ONES:K_ONES + P], wx[:].rearrange("i e j -> i (e j)"), start=True, stop=True).then_inc(d_full, 1)
            for e in range(EXPERTS):
                attention(True, e > 0)
                feed_forward()
            norms(xr, True)

        @block.scalar
        def _(act):
            t = Tally(act)
            n = Counter()

            def bank():
                t.more(u_full)
                n["u"] += 1
                return u_ring[(n["u"] - 1) % UB]

            def rsqrt(hv):
                o = bank()[:, 0:NT]
                nc.scalar.activation(rstd[:, hv], o, ACT.Ln, bias=eps_t[:, 0:1]).then_inc(*t.up(u_taken))
                t.own(u_taken)
                nc.scalar.activation(rstd[:, hv], rstd[:, hv], ACT.Exp, scale=-0.5).then_inc(*t.up(r_ready))

            def squares(hv):
                t.more(dve_in)
                for c, s in enumerate((d_taken, squared)):
                    nc.scalar.activation(t2[:, hv, c], t1[:, hv, c], ACT.Square).then_inc(s, 1)

            def affine(hv, dst, g, b):
                t.more(dve_in)
                for to in (ah, dst):
                    for c in range(C):
                        last = nc.scalar.activation(to[:, hv, c], t2[:, hv, c], ACT.Identity,
                                                    scale=bc(g, c), bias=bc(b, c))
                last.then_inc(*t.up(act_out))

            def norms(dst=None, g=None, b=None):
                for hv in range(HALVES):
                    squares(hv)
                for hv in range(HALVES):
                    rsqrt(hv)
                if g:
                    for hv in range(HALVES):
                        affine(hv, dst, g, b)

            def attention(softmax, qk_bias, norm1, before):
                def prepare(hv, c):
                    for i, dst in ((0, t1), (1, t2)):
                        o = bank()[:, 0:NT]
                        nc.scalar.activation(dst[:, hv, c], o, ACT.Identity, bias=bc(qk_bias, 2 * i + c)
                                             ).then_inc(*t.up(u_taken))
                    if not softmax:
                        for _m in range(2):
                            t.more(dve_in)
                            nc.scalar.activation(xr[:, hv, c], xr[:, hv, c], ACT.Exp).then_inc(*t.up(act_out))

                for c in range(C):
                    prepare(0, c)
                for j in ROUNDS:
                    if 0 <= j + 1 < J:
                        r = slice(0, GROUPS[steps[j + 1][2]][1] * TOK)
                        o = bank()[r, 0:HC * TOK]
                        t.room(ps_ready, n["e"], 2)
                        n["e"] += 1
                        f, sc = (ACT.Exp, HD ** -0.5) if softmax else (ACT.Identity, 1.0)
                        nc.scalar.activation(e_t[r, (j + 1) % 2], o, f, scale=sc).then_inc(*t.up(u_taken))
                    if softmax and 0 <= j < J:
                        r = slice(0, GROUPS[steps[j][2]][1] * TOK)
                        o = bank()[r, 0:HC * TOK]
                        nc.scalar.activation(rs[r, j % 2], o, ACT.Ln).then_inc(*t.up(u_taken))
                        t.own(u_taken)
                        nc.scalar.activation(rs[r, j % 2], rs[r, j % 2], ACT.Exp, scale=-1.0
                                             ).then_inc(*t.up(r_ready))
                    if 0 <= j - 1 < J:
                        hv, c, g = steps[j - 1]
                        i0, ni = GROUPS[g]
                        if g == 0:
                            if n["av"] >= C:
                                act.wait_ge(av_dma[c], 16 * HC * (n["av"] // C))
                            n["av"] += 1
                        for i in range(ni):
                            o = bank()[:, 0:HC * TOK].rearrange("p (s q) -> p s q", q=TOK)
                            at = TOK * (i0 + i)
                            nc.scalar.activation(av[:, c, :, at:at + TOK], o, ACT.Copy
                                                 ).then_inc(*t.up(u_taken))
                    if before and j == N2_VAR - 1:
                        for hv in range(HALVES):
                            squares(hv)
                    if j in PREPARE:
                        prepare(1, PREPARE[j])
                    if before and j == N2_VAR:
                        for hv in range(HALVES):
                            rsqrt(hv)
                    if before and j == N2_VAR + 1:
                        for hv in range(HALVES):
                            affine(hv, *before)
                    if j == N1_VAR - 1:
                        squares(0)
                    if j == N1_VAR:
                        rsqrt(0)
                affine(0, *norm1)
                squares(1)
                rsqrt(1)
                affine(1, *norm1)

            def hidden(f, b):
                o = bank()[:, 0:NT]
                t.room(hid_ready, n["hf"], 2)
                nc.scalar.activation(hf[:, n["hf"] % 2], o, f, **({"bias": b} if b is not None else {})
                                     ).then_inc(*t.up(u_taken))
                n["hf"] += 1

            def feed_forward(f, b1):
                for p in range(FF // P // 2):
                    for hv in range(HALVES):
                        for m in range(2):
                            hidden(f, bc(b1, 2 * p + m))

            act.wait_ge(k_ready, 1)
            for hv in range(HALVES):
                for m in range(C):
                    o = bank()[:, 0:NT]
                    nc.scalar.activation(t1[:, hv, m], o, ACT.Silu, bias=bc("tok_b1", m)).then_inc(*t.up(u_taken))
            nc.scalar.preload_act_table_set("natural_log_exp_and_others")
            norms()
            norms(t1, "g1", "be1")
            attention(False, "l0_qk_b", (t1, "g2", "be2"), None)
            feed_forward(ACT.Gelu, "l0_b1")
            nc.scalar.preload_act_table_set("natural_log_exp_and_others")
            norms()
            for hv in range(HALVES):
                t.more(dve_in)
                nc.scalar.activation(pr[:], lg[:], ACT.Exp).then_inc(*t.up(act_out))
            for e in range(SHARED + ROUTED):
                for hv in range(HALVES):
                    hidden(ACT.Gelu, None)
                    if e >= SHARED:
                        o = bank()[:, 0:NT]
                        nc.scalar.activation(gb[:, n["gb"] % 2], o, ACT.Copy).then_inc(*t.up(u_taken))
                        n["gb"] += 1
            nc.scalar.preload_act_table_set("natural_log_exp_and_others")
            norms()
            for u in range(len(units)):
                t.more(dve_in)
                nc.scalar.activation(h_s(u), h_s(u), ACT.Exp, scale=HD ** -0.5).then_inc(*t.up(act_out))
            norms()
            for hv in range(HALVES):
                t.more(dve_in)
                nc.scalar.activation(sm[0:HI, 8:8 + EXPERTS], sm[0:HI, 0:EXPERTS], ACT.Exp).then_inc(*t.up(act_out))
            for e in range(EXPERTS):
                attention(True, f"e{e}_qk_b", (xr, f"e{e}_g1", f"e{e}_be1"),
                          (xr, f"e{e - 1}_g2", f"e{e - 1}_be2") if e else None)
                feed_forward(ACT.Relu, f"e{e}_b1")
            norms(xr, f"e{EXPERTS - 1}_g2", f"e{EXPERTS - 1}_be2")

        @block.vector
        def _(dve):
            t = Tally(dve)
            n = Counter()
            v = nc.vector

            def step(ins):
                ins.then_inc(*t.up(dve_step))
                t.own(dve_step)

            def tell(ins, s):
                ins.then_inc(*t.up(s))
                t.own(s)

            def banks(k=1):
                n["u"] += k

            def taken():
                n["u"] += 1
                dve.wait_ge(u_taken, n["u"])

            def bank():
                t.more(d_full)
                n["d"] += 1
                return w_ring[(n["d"] - 1) % WB]

            def take(ins):
                ins.then_inc(*t.up(d_taken))
                t.own(d_taken)

            def split(src, hv):
                step(v.tensor_copy(ah[:, hv], src))
                tell(v.tensor_tensor(al[:, hv], src, ah[:, hv].bitcast(F32), ALU.subtract), a_split)

            def low(src, hv):
                t.more(act_out)
                tell(v.tensor_tensor(al[:, hv], src[:, hv], ah[:, hv].bitcast(F32), ALU.subtract), a_split)

            def center(src, hv):
                o = bank()[:, 0:NT]
                tell(v.tensor_tensor(t1[:, hv], src[:, hv], o.unsqueeze(1).to_broadcast([P, C, NT]), ALU.subtract),
                     dve_in)
                t.up(d_taken)

            def normal(dst, hv, s=None):
                t.more(r_ready)
                ins = v.tensor_tensor(dst[:, hv], t1[:, hv], rstd[:, hv].unsqueeze(1).to_broadcast([P, C, NT]), ALU.mult)
                if s is not None:
                    tell(ins, s)
                else:
                    step(ins)

            def norms(src, dst, g=None, b=None, last=False, then=None):
                for hv in range(HALVES):
                    center(src, hv)
                banks(HALVES)
                for hv in range(HALVES):
                    normal(t2 if g else dst, hv, dve_in if g else then)
                if last:
                    for hv in range(HALVES):
                        t.more(act_out)
                elif g:
                    for hv in range(HALVES):
                        low(dst, hv)

            def residual(dst, src, b, halves=range(HALVES)):
                for hv in halves:
                    for c in range(C):
                        o = bank()[:, 0:NT]
                        if b:
                            take(v.scalar_tensor_tensor(dst[:, hv, c], o, bc(b, c), src[:, hv, c], ALU.add, ALU.add))
                        else:
                            take(v.tensor_tensor(dst[:, hv, c], o, src[:, hv, c], ALU.add))

            def gated(e, hv):
                for c in range(C):
                    step(v.tensor_tensor(by_image(t1[:, hv])[:, c], by_image(xr[:, hv])[:, c],
                                         wimg[:, hv, e].unsqueeze(2).to_broadcast([P, HI, TOK]), ALU.mult))
                last = v.tensor_tensor(h[:, hv], h[:, hv], t1[:, hv], ALU.add)
                if e == EXPERTS - 1:
                    tell(last, out_ready)
                else:
                    step(last)

            def images(ap):
                return ap[:, :, LEAD:PADDED].rearrange("p c (i w) -> p c i w", w=PITCH)[:, :, :, 0:TOK]

            def by_image(ap):
                return ap.rearrange("p c (i q) -> p c i q", q=TOK)

            def attention(softmax, src, blk, res, out_b, norm_dst):
                before = blk > 1

                def prepare(hv, c):
                    banks(2)
                    dve.wait_ge(u_taken, n["u"])
                    q, k, ex = t1[:, hv, c], t2[:, hv, c], xr[:, hv, c]
                    if not softmax:
                        for m in (q, k):
                            tell(v.tensor_scalar(ex, m, 0.0, None, ALU.min), dve_in)
                            t.more(act_out)
                            step(v.scalar_tensor_tensor(m, m, 0.0, ex, ALU.max, ALU.add))
                    if n["att", c]:
                        dve.wait_ge(qk_dma[c], 16 * HC * n["att", c])
                    n["att", c] += 1
                    step(v.tensor_copy(qks[:, c, 0], q))
                    step(v.tensor_copy(qks[:, c, 2], k))
                    row = lambda ap: ap.rearrange("p (i q) -> p i q", q=TOK)
                    if softmax:
                        v.tensor_copy(images(qpad)[:, c], row(q))
                    v.tensor_copy(images(kpad[:, 0])[:, c], row(k))
                    v.tensor_tensor(images(kpad[:, 1])[:, c], row(k), row(qks[:, c, 2].bitcast(F32)), ALU.subtract)
                    tell(v.tensor_tensor(qks[:, c, 1], q, qks[:, c, 0].bitcast(F32), ALU.subtract), qk_split)
                    if c:
                        return
                    dve.wait_ge(vb_dma, 16 * (blk + 1))
                    for d in range(C):
                        if n["vs"]:
                            dve.wait_ge(v_dma[d], 16 * SLOTS * n["vs"])
                    n["vs"] += 1
                    for g, (i0, ni) in enumerate(GROUPS):
                        r = slice(0, ni * TOK)
                        o = bank()[r, 0:D]
                        take(v.tensor_tensor(vf[r], o, vb[r, blk % 2], ALU.add))
                        step(v.tensor_copy(vs[r, g, 0:D], vf[r]))
                        last = v.tensor_tensor(vs[r, g, D:2 * D], vf[r], vs[r, g, 0:D].bitcast(F32), ALU.subtract)
                        if g < len(GROUPS) - 1:
                            step(last)
                    tell(last, v_split)

                def own_products(hv):
                    for c in range(C):
                        t.more(av_dma[c], 16 * HC)
                    split(t1[:, hv], hv)

                if softmax:
                    split(src[:, 0], 0)
                for c in range(C):
                    prepare(0, c)
                for j in ROUNDS:
                    if before and j == N2_VAR - 1:
                        for hv in range(HALVES):
                            center(xr, hv)
                    if before and j == N2_VAR + 1:
                        for hv in range(HALVES):
                            normal(t2, hv, dve_in)
                    if before and j == N2_VAR + 2:
                        for hv in range(HALVES):
                            t.more(act_out)
                            gated(blk - 2, hv)
                    if j == OUT_P:
                        own_products(0)
                    if j == OUT_P + 1:
                        residual(xr, res, out_b, [0])
                    if j == N1_VAR - 1:
                        center(xr, 0)
                    if softmax and j + 2 < J:
                        m = GROUPS[steps[j + 2][2]][1] * TOK
                        lim = shift[0:m, j % 2]
                        o = bank()[0:m, 0:HC * TOK].rearrange("p (s k) -> p s k", k=TOK)
                        v.tensor_reduce(lim, o, AX.X, ALU.max, negate=True).then_inc(*t.up(d_taken))
                    banks(0 <= j + 1 < J)
                    if 0 <= j < J:
                        r = slice(0, GROUPS[steps[j][2]][1] * TOK)
                        i = j % 2
                        if softmax:
                            banks()
                            t.more(r_ready)
                        else:
                            o = bank()[r, 0:HC * TOK]
                            take(v.tensor_scalar(rs[r, i], o, ATTN_EPS, None, ALU.max))
                            step(v.reciprocal(rs[r, i], rs[r, i]))
                        v.tensor_tensor(e_t[r, i], e_t[r, i], rs[r, i], ALU.mult).then_inc(*t.up(dve_step))
                    if softmax and j + 2 < J:
                        t.own(d_taken)
                        v.tensor_tensor(mx[0:m, j % 2],
                                        kshape[0:m, K_DELTA:K_DELTA + TOK].unsqueeze(1).to_broadcast([m, HC, TOK]),
                                        lim.unsqueeze(2).to_broadcast([m, HC, TOK]), ALU.mult
                                        ).then_inc(*t.up(mx_ready))
                    if 0 <= j < J:
                        t.own(dve_step)
                        step(v.tensor_copy(eh[r, j % 3], e_t[r, i]))
                        tell(v.tensor_tensor(el[r, j % 3], e_t[r, i], eh[r, j % 3].bitcast(F32), ALU.subtract), ps_ready)
                    if 0 <= j - 1 < J:
                        banks(GROUPS[steps[j - 1][2]][1])
                    if j in PREPARE:
                        if softmax and PREPARE[j] == 0:
                            split(src[:, 1], 1)
                        prepare(1, PREPARE[j])
                    if before and j == N2_VAR:
                        banks(HALVES)
                    if j == N1_VAR:
                        banks()
                normal(t2, 0, dve_in)
                own_products(1)
                low(norm_dst, 0)
                residual(xr, res, out_b, [1])
                center(xr, 1)
                banks()
                normal(t2, 1, dve_in)
                low(norm_dst, 1)

            def hidden(by_gate):
                taken()
                i = n["hid"] % 2
                if by_gate:
                    taken()
                    step(v.tensor_tensor(hf[:, i], hf[:, i], gb[:, n["gb"] % 2], ALU.mult))
                    n["gb"] += 1
                t.room(hid_used, n["hid"], HID)
                slot = n["hid"] % HID
                n["hid"] += 1
                step(v.tensor_copy(hid[:, slot, 0], hf[:, i]))
                tell(v.tensor_tensor(hid[:, slot, 1], hf[:, i], hid[:, slot, 0].bitcast(F32), ALU.subtract), hid_ready)

            def feed_forward(dst, b2):
                for _ in range(HALVES * FF // P):
                    hidden(False)
                residual(dst, xr, b2)

            def select(values, least, first, count, m, nb, ne, work):
                view = values.rearrange("p (b e) -> p b e", e=ne)
                lim = least.to_broadcast([m, nb, ne])
                w3 = [work[:, i].rearrange("p (b e) -> p b e", e=ne) for i in range(2)]
                step(v.tensor_tensor(w3[0], view, lim, ALU.is_gt))
                step(v.tensor_tensor(w3[1], view, lim, ALU.is_equal))
                step(v.tensor_reduce(sel_n[0:m, 0:nb], w3[0], AX.X, ALU.add))
                step(v.tensor_tensor_scan(sel_c[0:m, 0:nb * ne], first, work[:, 1], 0.0, ALU.mult, ALU.add))
                c3 = sel_c[0:m, 0:nb * ne].rearrange("p (b e) -> p b e", e=ne)
                step(v.tensor_tensor(c3, c3, sel_n[0:m, 0:nb].unsqueeze(2).to_broadcast([m, nb, ne]), ALU.add))
                step(v.scalar_tensor_tensor(work[:, 1], sel_c[0:m, 0:nb * ne], float(count), work[:, 1],
                                            ALU.is_le, ALU.mult))
                step(v.tensor_tensor(work[:, 0], work[:, 0], work[:, 1], ALU.add))
                return work[:, 0]

            def mixed_out(u):
                m = GROUPS[units[u][1]][1] * TOK
                n["groups"] += 1
                if n["groups"] > 1:
                    dve.wait_ge(mixed_dma, 16 * n["images"])
                n["images"] += GROUPS[units[u][1]][1]
                dve.wait_ge(h_mixed, u + 1)
                tell(v.tensor_reduce(vf[0:m].rearrange("p (a d) -> p a d", d=HD),
                                     hv_p[0:m].rearrange("p (a d b) -> p a d b", a=HD, b=HD), AX.X, ALU.add), ho_ready)

            def over_heads(u):
                m = GROUPS[units[u][1]][1] * TOK
                own = [0, D, D * (2 + u % 2)]
                for i, at in enumerate(own):
                    take(v.tensor_tensor(hq[0:m, at:at + D], bank()[0:m, 0:D], hb[0:m, D * i:D * (i + 1)], ALU.add))
                q, k = (hq[0:m, D * i:D * (i + 1)].rearrange("p (a d) -> p a d", d=HD) for i in range(2))
                p4 = hp[0:m].rearrange("p (a b d) -> p a b d", a=HD, b=HD)
                s3 = h_s(u).rearrange("p (a b) -> p a b", b=HD)
                lim = shift[0:m].rearrange("p i s -> p (i s)")
                step(v.tensor_tensor(p4, q.unsqueeze(2).to_broadcast([m] + cube),
                                     k.unsqueeze(1).to_broadcast([m] + cube), ALU.mult))
                step(v.tensor_reduce(s3, p4, AX.X, ALU.add))
                step(v.tensor_reduce(lim, s3, AX.X, ALU.max))
                tell(v.tensor_tensor(s3, s3, lim.unsqueeze(2).to_broadcast([m, HD, HD]), ALU.subtract), dve_in)
                if u:
                    mixed_out(u - 1)
                t.more(act_out)
                step(v.tensor_reduce(lim, s3, AX.X, ALU.add))
                step(v.reciprocal(lim, lim))
                tell(v.tensor_tensor(s3, s3, lim.unsqueeze(2).to_broadcast([m, HD, HD]), ALU.mult), h_soft)

            def heads_back(u):
                if u >= 0:
                    hv, g = units[u]
                    i0, ni = GROUPS[g]
                    for c in range(C):
                        take(v.tensor_copy(t1[:, hv, c, TOK * i0:TOK * (i0 + ni)], bank()[:, 0:ni * TOK]))

            dve.wait_ge(k_dma, 16 * 5)
            step(v.memset(eps_t[:], LN_EPS))
            step(v.tensor_copy(block_w[:], kshape[0:PITCH, K_BLOCK:K_BLOCK + PITCH]))
            step(v.tensor_copy(eye_w[:], kshape[0:ROUTED, K_IDENT:K_IDENT + ROUTED]))
            step(v.tensor_copy(rt[:, 0], rt_raw[:]))
            tell(v.tensor_tensor(rt[:, 1], rt_raw[:], rt[:, 0].bitcast(F32), ALU.subtract), k_ready)
            for hv in range(HALVES):
                t.more(patch_dma, 16)
                step(v.tensor_copy(patch_h[:, hv], patch_raw[:]))
                tell(v.tensor_tensor(patch_l[:, hv], patch_raw[:], patch_h[:, hv].bitcast(F32), ALU.subtract), patch_split)

            for hv in range(HALVES):
                banks(C)
                dve.wait_ge(u_taken, n["u"])
                split(t1[:, hv], hv)
            for hv in range(HALVES):
                for c in range(C):
                    take(v.tensor_scalar(h[:, hv, c], bank()[:, 0:NT], bc("tok_b2", c), None, ALU.add))
            dve.wait_ge(zeroed, 2)

            norms(h, x, then=norm_in)
            norms(x, t1, "g1", "be1")
            attention(False, t1, 0, x, "l0_out_b", t1)
            feed_forward(t2, "l0_b2")
            for hv in range(HALVES):
                tell(v.tensor_tensor(h[:, hv], h[:, hv], t2[:, hv], ALU.add), norm_in)

            norms(h, x)
            for hv in range(HALVES):
                split(x[:, hv], hv)
            for hv in range(HALVES):
                o = bank()[0:RT, 0:RB * ROUTED]
                o3 = o.rearrange("p (b e) -> p b e", e=ROUTED)
                l3 = lg[:].rearrange("p (b e) -> p b e", e=ROUTED)
                p3 = pr[:].rearrange("p (b e) -> p b e", e=ROUTED)
                step(v.tensor_reduce(sel_n[:, 0:RB], o3, AX.X, ALU.max))
                tell(v.tensor_tensor(l3, o3, sel_n[:, 0:RB].unsqueeze(2).to_broadcast([RT, RB, ROUTED]), ALU.subtract), dve_in)
                t.more(act_out)
                tell(v.tensor_reduce(sel_n[:, 0:RB], p3, AX.X, ALU.add), d_taken)
                t.own(d_taken)
                step(v.reciprocal(sel_n[:, 0:RB], sel_n[:, 0:RB]))
                step(v.tensor_tensor(p3, p3, sel_n[:, 0:RB].unsqueeze(2).to_broadcast([RT, RB, ROUTED]), ALU.mult))
                for b in range(RB):
                    step(v.max(top[:, b], pr[:, ROUTED * b:ROUTED * (b + 1)]))
                keep = select(pr[:], top[:, :, TOPK - 1:TOPK], kshape[0:RT, K_FIRST:K_FIRST + RB * ROUTED],
                              TOPK, RT, RB, ROUTED, sm[:].rearrange("p (a n) -> p a n", a=2))
                tell(v.tensor_tensor(gw[:, hv], keep, pr[:], ALU.mult), gate_ready)
            for hv in range(HALVES):
                o = bank()[0:ROUTED, 0:NT]
                step(v.tensor_copy(gth[:, hv], o))
                take(v.tensor_tensor(gtl[:, hv], o, gth[:, hv].bitcast(F32), ALU.subtract))
            for e in range(SHARED + ROUTED):
                for hv in range(HALVES):
                    hidden(e >= SHARED)
            residual(h, h, None)

            norms(h, x)
            for hv in range(HALVES):
                split(x[:, hv], hv)
            dve.wait_ge(hb_dma, 16)
            for u in range(len(units)):
                over_heads(u)
                heads_back(u - 2)
            mixed_out(len(units) - 1)
            for u in range(len(units) - 2, len(units)):
                heads_back(u)
            for hv in range(HALVES):
                split(t1[:, hv], hv)
            residual(h, h, "l1_out_b")

            norms(h, x)
            for hv in range(HALVES):
                step(v.tensor_reduce(xm[:], by_image(x[:, hv]), AX.X, ALU.add))
                tell(v.tensor_scalar(xm[:], xm[:], 1.0 / TOK, None, ALU.mult), xm_ready)
                step(v.memset(lg1[:], -3e38))
                take(v.tensor_tensor(lg1[:, 0:EXPERTS], bank()[0:HI, 0:EXPERTS], gtb[0:HI], ALU.add))
                step(v.max(top[0:HI, 0], lg1[:]))
                tell(v.tensor_scalar(sm[0:HI, 0:EXPERTS], lg1[:, 0:EXPERTS], top[0:HI, 0, 0:1], None, ALU.subtract), dve_in)
                t.more(act_out)
                ex = sm[0:HI, 8:8 + EXPERTS]
                step(v.tensor_reduce(sel_n[0:HI, 0:1], ex, AX.X, ALU.add))
                step(v.reciprocal(sel_n[0:HI, 0:1], sel_n[0:HI, 0:1]))
                step(v.tensor_scalar(ex, ex, sel_n[0:HI, 0:1], None, ALU.mult))
                keep = select(lg1[:, 0:EXPERTS], top[0:HI, 0:1, TOP2 - 1:TOP2], kshape[0:HI, K_FIRST:K_FIRST + EXPERTS],
                              TOP2, HI, 1, EXPERTS, sm[0:HI, 16:16 + 2 * EXPERTS].rearrange("p (a n) -> p a n", a=2))
                step(v.tensor_tensor(keep, keep, ex, ALU.mult))
                tell(v.tensor_tensor(wx[:], keep.unsqueeze(2).to_broadcast([HI, EXPERTS, HI]),
                                kshape[0:HI, K_EYE8:K_EYE8 + HI].unsqueeze(1).to_broadcast([HI, EXPERTS, HI]),
                                ALU.mult), wx_ready)
                o = bank()[:, 0:EXPERTS * HI].rearrange("p (e i) -> p e i", i=HI)
                take(v.tensor_copy(wimg[:, hv], o))
            for e in range(EXPERTS):
                attention(True, x, 1 + e, x, f"e{e}_out_b", xr)
                feed_forward(xr, f"e{e}_b2")
            e = EXPERTS - 1
            norms(xr, xr, f"e{e}_g2", f"e{e}_be2", last=True)
            for hv in range(HALVES):
                gated(e, hv)


def blocks(w, order):
    k, m = w.shape[0] // P, w.shape[1] // P
    b = w.reshape(k, P, m, P)
    return b.transpose((1, 2, 0, 3) if order == "mk" else (1, 0, 2, 3)).reshape(P, -1)


def expert_pairs(w1, w2):
    a, b = blocks(w1, "mk"), blocks(w2, "km")
    n = a.shape[1] // TILE
    parts = []
    for p in range(n + 1):
        if p < n:
            parts.append(a[:, TILE * p:TILE * (p + 1)])
        if p:
            parts.append(b[:, TILE * (p - 1):TILE * p])
    return parts


def attention_weights(wq, wk, wv, wo):
    return [blocks(wq, "mk"), blocks(wk, "mk"), blocks(wv, "km"), blocks(wo, "mk")]


def kernel(**inputs):
    import concourse.bacc as bacc
    from concourse.bass_utils import run_bass_kernel_spmd

    a = {k: np.asarray(v) for k, v in inputs.items()}
    patches = a["x"].reshape(HALVES, HI, 3, 6, 16, 6, 16).transpose(0, 2, 4, 6, 1, 3, 5)
    patches = patches.reshape(HALVES, KP, P, NT).transpose(0, 2, 1, 3)

    parts = [blocks(a["L0_tok_W1"], "mk"), blocks(a["L0_tok_W2"], "mk")]
    qkv = a["L0_attn_qkv_w"]
    parts += attention_weights(qkv[:, 0:D], qkv[:, D:2 * D], qkv[:, 2 * D:], a["L0_attn_out_w"])
    parts += expert_pairs(a["L0_attn_w1"], a["L0_attn_w2"])
    ups = list(a["L0_ffn_shared_up"]) + list(a["L0_ffn_routed_up"])
    downs = list(a["L0_ffn_shared_down"]) + list(a["L0_ffn_routed_down"])
    for up, down in zip(ups, downs):
        parts += [blocks(up.T, "mk"), blocks(down.T, "mk")]
    parts += [blocks(a[f"L1_attn_W{n}"].T, "km") for n in "qkv"] + [blocks(a["L1_attn_Wo"].T, "mk")]
    for e in range(EXPERTS):
        qkv = a["L1_ffn_in_proj_w"][e]
        parts += attention_weights(qkv[0:D].T, qkv[D:2 * D].T, qkv[2 * D:].T, a["L1_ffn_out_proj_w"][e].T)
        parts += expert_pairs(a["L1_ffn_lin1_w"][e].T, a["L1_ffn_lin2_w"][e].T)

    vectors = {"tok_b1": a["L0_tok_b1"], "tok_b2": a["L0_tok_b2"], "l0_qk_b": a["L0_attn_qkv_b"][0:2 * D],
               "l0_out_b": a["L0_attn_out_b"], "l0_b1": a["L0_attn_b1"], "l0_b2": a["L0_attn_b2"],
               "g1": a["L0_attn_g1"], "be1": a["L0_attn_be1"], "g2": a["L0_attn_g2"], "be2": a["L0_attn_be2"],
               "l1_out_b": a["L1_attn_bo"]}
    vbias = [a["L0_attn_qkv_b"][2 * D:]]
    for e in range(EXPERTS):
        f = {n: a[f"L1_ffn_{n}"][e] for n in ("in_proj_b", "out_proj_b", "lin1_b", "lin2_b", "ln1_w", "ln1_b",
                                              "ln2_w", "ln2_b")}
        vectors |= {f"e{e}_qk_b": f["in_proj_b"][0:2 * D], f"e{e}_out_b": f["out_proj_b"], f"e{e}_b1": f["lin1_b"],
                    f"e{e}_b2": f["lin2_b"], f"e{e}_g1": f["ln1_w"], f"e{e}_be1": f["ln1_b"],
                    f"e{e}_g2": f["ln2_w"], f"e{e}_be2": f["ln2_b"]}
        vbias.append(f["in_proj_b"][2 * D:])
    bcol, _ = bias_columns()
    biases = np.concatenate([vectors[n].reshape(k, P).T for n, (_, k) in bcol.items()], axis=1)

    arrays = {
        "patches": patches,
        "weights": np.concatenate(parts, axis=1),
        "biases": biases,
        "vbias": np.stack(vbias),
        "hbias": np.concatenate([a["L1_attn_bq"], a["L1_attn_bk"], a["L1_attn_bv"]]),
        "router": blocks_narrow(a["L0_ffn_router_w"].T),
        "gate": blocks_narrow(a["L1_ffn_gate_w"].T),
        "gate_b": a["L1_ffn_gate_b"],
        "constants": shape_constants(),
    }
    arrays = {f"in_{k}": np.ascontiguousarray(v) for k, v in arrays.items()}

    nc = bacc.Bacc("TRN2", target_bir_lowering=False, num_devices=1)
    args = [nc.dram_tensor(k, v.shape, mybir.dt.from_np(v.dtype), kind="ExternalInput").ap()
            for k, v in arrays.items()]
    out = nc.dram_tensor("out", (HALVES, P, C, NT), F32, kind="ExternalOutput").ap()
    mixed = nc.dram_tensor("mixed", (IMAGES, HD, TOK, HD), F32, kind="Internal").ap()
    build_tower(nc, *args, out, mixed)
    r = run_bass_kernel_spmd(nc, [arrays], core_ids=[0])
    got = r.results[0]["out"]
    return got.transpose(0, 3, 2, 1).reshape(IMAGES, TOK, D)


def blocks_narrow(w):
    return w.reshape(C, P, -1).transpose(1, 0, 2).reshape(P, -1)
```

```python
from collections import Counter
from contextlib import ExitStack

import numpy as np

import concourse.bass as bass
from concourse import mybir

F32 = mybir.dt.float32
F32R = mybir.dt.float32r
ALU = mybir.AluOpType
ACT = mybir.ActivationFunctionType
AX = mybir.AxisListType

P = 128
D = 256
C = D // P
IMAGES = 16
TOK = 36
HALVES = 2
HI = IMAGES // HALVES
NT = HI * TOK
HD = 16
HC = P // HD
PATCH = 768
KP = PATCH // P
FF = 1024
ROUTED, SHARED, TOPK = 16, 2, 4
EXPERTS, TOP2 = 4, 2
LN_EPS = 1e-5
ATTN_EPS = 1e-6
GROUPS = [(0, 3), (3, 3), (6, 2)]
SLOTS = 3
PITCH = SLOTS * TOK
MARGIN = (SLOTS - 1) * TOK
PADDED = MARGIN + HI * PITCH
TILE = 512
RING = 5
STAGES = 2
RT = 96
RB = NT // RT
UB = 4
WB = 4
HID = 8


def bias_columns():
    names = [("tok_b1", 2), ("tok_b2", 2), ("l0_qk_b", 4), ("l0_out_b", 2), ("l0_b1", 8), ("l0_b2", 2),
             ("g1", 2), ("be1", 2), ("g2", 2), ("be2", 2), ("l1_out_b", 2)]
    for e in range(EXPERTS):
        names += [(f"e{e}_qk_b", 4), (f"e{e}_out_b", 2), (f"e{e}_b1", 8), (f"e{e}_b2", 2),
                  (f"e{e}_g1", 2), (f"e{e}_be1", 2), (f"e{e}_g2", 2), (f"e{e}_be2", 2)]
    at, out = 0, {}
    for name, n in names:
        out[name] = (at, n)
        at += n
    return out, at


TOK_TILES = (PATCH + D) * D // (P * TILE)
ATT_ALONE = 4 * D * D // (P * TILE)
BLOCK_TILES = ATT_ALONE + 2 * D * FF // (P * TILE)
MOE_TILES = SHARED + ROUTED
ATT_TILES = [TOK_TILES] + [TOK_TILES + BLOCK_TILES + MOE_TILES + ATT_ALONE + e * BLOCK_TILES for e in range(EXPERTS)]

K_MEAN = 0
K_BLOCK = K_MEAN + P
K_DELTA = K_BLOCK + PITCH
K_IDENT = K_DELTA + TOK
K_FIRST = K_IDENT + P
K_EYE8 = K_FIRST + RB * ROUTED
K_ONES = K_EYE8 + HI
K_SHAPE = K_ONES + P


def shape_constants():
    k = np.zeros((P, K_SHAPE), np.float32)
    k[:, K_MEAN:K_MEAN + P] = 1.0 / D
    r = np.arange(PITCH)
    k[:PITCH, K_BLOCK:K_BLOCK + PITCH] = r[:, None] // TOK == r[None] // TOK
    k[:PITCH, K_DELTA:K_DELTA + TOK] = r[:, None] % TOK == np.arange(TOK)[None]
    k[:, K_IDENT:K_IDENT + P] = np.eye(P)
    k[:, K_FIRST:K_FIRST + RB * ROUTED] = np.arange(RB * ROUTED) % ROUTED != 0
    k[:HI, K_EYE8:K_EYE8 + HI] = np.eye(HI)
    k[:, K_ONES:K_ONES + P] = 1.0
    return k


def build_tower(nc, patches, weights, biases, vbias, hbias, router, gate, gate_b, constants, out, mixed):
    bcol, nbias = bias_columns()
    tiles = weights.shape[1] // TILE

    with ExitStack() as ctx:
        def sb(name, shape, dt=F32):
            return ctx.enter_context(nc.sbuf_tensor(name, shape, dt))

        def sem(name):
            return ctx.enter_context(nc.semaphore(name))

        u_ring = [ctx.enter_context(nc.psum_tensor(f"u_ring{i}", [P, TILE], F32)) for i in range(UB)]
        w_ring = [ctx.enter_context(nc.psum_tensor(f"w_ring{i}", [P, TILE], F32)) for i in range(WB)]

        kshape = sb("kshape", [P, K_SHAPE])
        block_w = sb("block_w", [PITCH, PITCH], F32R)
        eye_w = sb("eye_w", [ROUTED, ROUTED], F32R)
        bias = sb("bias", [P, nbias])
        vb = sb("vb", [P, 2, D])
        rt_raw = sb("rt_raw", [P, C * ROUTED])
        rt = sb("rt", [P, 2, C * ROUTED], F32R)
        gt = sb("gt", [P, C * EXPERTS])
        gtb = sb("gtb", [P, EXPERTS])
        stage = sb("stage", [P, STAGES, TILE])
        wh = sb("wh", [P, RING, TILE], F32R)
        wl = sb("wl", [P, RING, TILE], F32R)

        h = sb("h", [P, HALVES, C, NT])
        x = sb("x", [P, HALVES, C, NT])
        xr = sb("xr", [P, HALVES, C, NT])
        t1 = sb("t1", [P, HALVES, C, NT])
        t2 = sb("t2", [P, HALVES, C, NT])
        ah = sb("ah", [P, HALVES, C, NT], F32R)
        al = sb("al", [P, HALVES, C, NT], F32R)
        rstd = sb("rstd", [P, 2, NT])

        qpad = sb("qpad", [P, C, PADDED], F32R)
        kpad = sb("kpad", [P, 2, C, PADDED], F32R)
        vs = sb("vs", [PITCH, 3, 2 * D], F32R)
        vm = sb("vm", [PITCH, SLOTS, 3, 2 * D], F32R)
        vf = sb("vf", [PITCH, D])
        shift = sb("shift", [PITCH, 2, HC])
        mx = sb("mx", [PITCH, 2, HC, TOK], F32R)
        e_t = sb("e_t", [PITCH, 2, HC * TOK])
        eh = sb("eh", [PITCH, 3, HC * TOK], F32R)
        el = sb("el", [PITCH, 3, HC * TOK], F32R)
        rs = sb("rs", [PITCH, 2, HC * TOK])

        hf = sb("hf", [P, 2, NT])
        lg = sb("lg", [RT, RB * ROUTED])
        pr = sb("pr", [RT, RB * ROUTED])
        gw = sb("gw", [RT, HALVES, RB * ROUTED])
        eps_t = sb("eps_t", [P, 1])
        sm = sb("sm", [RT, 2 * ROUTED * RB])
        sel_n = sb("sel_n", [RT, 4])
        sel_c = sb("sel_c", [RT, RB * ROUTED])
        top = sb("top", [RT, RB, 8])
        xm = sb("xm", [P, HALVES, C, HI])
        lg1 = sb("lg1", [HI, HALVES, 8])
        gl = sb("gl", [HI, HALVES, EXPERTS])
        ge = sb("ge", [HI, HALVES, EXPERTS])
        top1 = sb("top1", [HI, HALVES, 8])
        wx = sb("wx", [HI, HALVES, EXPERTS, HI])
        wimg = sb("wimg", [P, HALVES, EXPERTS, HI])

        with nc.sbuf_tensor("gb", [P, 2, NT], F32) as gb, \
                nc.sbuf_tensor("gth", [ROUTED, HALVES, NT], F32R) as gth, \
                nc.sbuf_tensor("gtl", [ROUTED, HALVES, NT], F32R) as gtl:
            pass
        qks = sb("qks", [P, C, 3, NT], F32R)
        with nc.sbuf_tensor("patch_raw", [P, HALVES, KP, NT], F32) as patch_raw, \
                nc.sbuf_tensor("patch_h", [P, HALVES, KP, NT], F32R) as patch_h, \
                nc.sbuf_tensor("patch_l", [P, HALVES, KP, NT], F32R) as patch_l:
            pass
        with nc.sbuf_tensor("head_products", [PITCH, 2, HD ** 3], F32) as head_products:
            pass
        qkx = sb("qkx", [P, HC, C, 3, NT], F32R)
        with nc.sbuf_tensor("av", [P, C, HC, NT], F32) as av:
            pass
        hid = sb("hid", [P, HID, 2, NT], F32R)

        k_dma = sem("k_dma")
        patch_dma = [sem(f"patch_dma{hv}") for hv in range(HALVES)]
        stage_dma = [sem(f"stage_dma{i}") for i in range(STAGES)]
        aid_dma = [sem(f"aid_dma{i}") for i in range(STAGES)]
        w_high = sem("w_high")
        w_ready = sem("w_ready")
        w_used = sem("w_used")
        k_ready = sem("k_ready")
        zeroed = sem("zeroed")
        patch_split = sem("patch_split")
        u_full, u_taken = sem("u_full"), sem("u_taken")
        d_full, d_taken = sem("d_full"), sem("d_taken")
        a_split = sem("a_split")
        norm_in = sem("norm_in")
        squared = sem("squared")
        act_out = sem("act_out")
        dve_in = sem("dve_in")
        dve_step = sem("dve_step")
        qk_split = sem("qk_split")
        pads_ready = sem("pads_ready")
        hb_dma = sem("hb_dma")
        ho_ready = sem("ho_ready")
        h_soft = sem("h_soft")
        h_mixed = sem("h_mixed")
        mixed_dma = sem("mixed_dma")
        back_dma = [sem(f"back_dma{i}") for i in range(2)]
        vb_dma = sem("vb_dma")
        qk_dma = [sem(f"qk_dma{c}") for c in range(C)]
        v_split = sem("v_split")
        v_dma = [sem(f"v_dma{c}") for c in range(C)]
        mx_ready = sem("mx_ready")
        r_ready = sem("r_ready")
        ps_ready = sem("ps_ready")
        av_dma = [[sem(f"av_dma{hv}_{c}") for c in range(C)] for hv in range(HALVES)]
        hid_ready = sem("hid_ready")
        hid_used = sem("hid_used")
        gate_ready = sem("gate_ready")
        xm_ready = sem("xm_ready")
        wx_ready = sem("wx_ready")
        out_ready = sem("out_ready")
        out_dma = sem("out_dma")

        flat = "p h c n -> p (h c n)"
        hb = xr[:].rearrange(flat)[:, 0:3 * D]
        hq = t2[0:PITCH].rearrange(flat)[:, 0:4 * D]
        hp = av[0:PITCH].rearrange("p c s n -> p (c s n)")[:, 0:HD ** 3]
        hv_p = head_products
        units = [(hv, g) for hv in range(HALVES) for g in range(len(GROUPS))]
        cube = [HD, HD, HD]

        SHARE = 4

        def value_products(u, heads):
            m, na = GROUPS[units[u][1]][1] * TOK, heads.stop - heads.start
            val = hq[0:m, D * (2 + u % 2):D * (3 + u % 2)].rearrange("p (b d) -> p d b", d=HD)
            shape = [m, na, HD, HD]
            return (hv_p[0:m, u % 2].rearrange("p (a d b) -> p a d b", a=HD, b=HD)[:, heads],
                    (h_s(u).rearrange("p (a b) -> p a b", b=HD)[:, heads].unsqueeze(2).to_broadcast(shape),
                     val.unsqueeze(1).to_broadcast(shape)))

        def h_s(u):
            return e_t[0:GROUPS[units[u][1]][1] * TOK, u % 2, 0:D]

        block = ctx.enter_context(nc.Block())

        def bc(name, i):
            return bias[:, bcol[name][0] + i:bcol[name][0] + i + 1]

        class Tally:

            def __init__(self, eng):
                self.eng, self.n = eng, Counter()

            def up(self, s, by=1):
                self.n[s.name] += by
                return s, by

            def more(self, s, by=1):
                self.n[s.name] += by
                self.eng.wait_ge(s, self.n[s.name])

            def own(self, s):
                self.eng.wait_ge(s, self.n[s.name])

            def room(self, s, used, size):
                if used >= size:
                    self.eng.wait_ge(s, used - size + 1)

        steps = [(hv, c, g) for hv in range(HALVES) for c in range(C) for g in range(len(GROUPS))]
        J, G = len(steps), len(GROUPS)
        ROUNDS = range(-2, J + 1)
        STAGE = {G - 3 + G * c: c for c in range(C)}
        PREPARE = {G - 2 + G * c: c for c in range(C)}
        N2_VAR = -1
        GATE_LOGITS = -2
        OUT_P = 2 * J // 3 + 1
        N1_VAR = OUT_P + 2

        FF_TILES = [("up", 0), ("up", 1), ("down", 0), ("up", 2), ("down", 1), ("down", 2), ("up", 3), ("down", 3)]
        LEAD, BETWEEN = 5, 3
        FF_REST = ([(1, i) for i in range(LEAD)]
                   + [(hv, i) for i in range(LEAD, len(FF_TILES)) for hv in range(HALVES)])
        FF_ORDER = [(0, i) for i in range(LEAD)] + FF_REST
        LATE = 2 * sum(way == "up" for way, _ in FF_TILES[BETWEEN:LEAD])
        made = [(hv, FF_TILES[i][1]) for hv, i in FF_ORDER if FF_TILES[i][0] == "up"]
        eaten = [(hv, FF_TILES[i][1]) for hv, i in FF_ORDER if FF_TILES[i][0] == "down"]

        aided = {blk: [i for i in range(ATT_TILES[blk] + ATT_ALONE + RING, ATT_TILES[blk] + BLOCK_TILES + RING - 1)
                       if i < tiles] for blk in range(1 + EXPERTS)}
        MOE_AHEAD, moe_tile = RING - 2, ATT_TILES[0] + BLOCK_TILES
        moe_aided = {e: moe_tile + e + MOE_AHEAD for e in range(1, MOE_TILES)}
        all_aided = list(range(STAGES)) + [i for blk in aided for i in aided[blk]] + list(moe_aided.values())

        EARLY = range(2, 1 + EXPERTS)

        def u_rounds(softmax, before, base):
            u, out = base + 2 * C, {}
            for j in ROUNDS:
                if 0 <= j + 1 < J:
                    u += 1
                    out["scores", steps[j + 1][:2]] = u
                u += softmax and 0 <= j < J
                if 0 <= j - 1 < J:
                    hv, c, g = steps[j - 1]
                    u += GROUPS[g][1]
                    out[hv, c] = u
                u += 2 * (j in STAGE) + HALVES * (before and j == N2_VAR) + (j == N1_VAR)
            return out, u + 2

        norm_u, ff_u = HALVES, HALVES * FF // P
        av_full = []
        banks_u = HALVES * C + 2 * norm_u
        for blk in range(1 + EXPERTS):
            products_at, banks_u = u_rounds(blk > 0, blk > 1, banks_u)
            av_full.append(products_at)
            banks_u += ff_u
            if blk == 0:
                banks_u += norm_u + HALVES * (SHARED + 2 * ROUTED) + 2 * norm_u

        @block.gpsimd
        def _(pool):
            def load(i):
                pool.dma_start(stage[:, i % STAGES], weights[:, TILE * i:TILE * (i + 1)]
                               ).then_inc(stage_dma[i % STAGES], 16)

            t = Tally(pool)

            def expand_v(c):
                for s in range(SLOTS):
                    r = slice(TOK * s, TOK * (s + 1))
                    g = sum(ni > s for _, ni in GROUPS)
                    to, come = (ap[:, 0:g].bitcast(F32).rearrange("p g (l d) -> p (g l) d", l=2)[:, :, P * c:P * (c + 1)]
                                for ap in (vm[r, s], vs[r]))
                    pool.dma_start(to, come).then_inc(v_dma[c], 16)

            first_tile = {}
            for blk in range(1 + EXPERTS):
                first_tile[ATT_TILES[blk] + RING] = (blk, 0)
                first_tile[ATT_TILES[blk] + RING + C + 1] = (blk, 1)

            for z in (qpad, kpad):
                nc.gpsimd.memset(z[:].bitcast(F32), 0.0).then_inc(zeroed, 1)
            for i in range(tiles):
                if i == ATT_TILES[0] + 3:
                    pool.wait_ge(u_full, HALVES * C)
                    nc.gpsimd.memset(qkx[:].bitcast(F32), 0.0).then_inc(zeroed, 1)
                if i == ATT_TILES[1] - ATT_ALONE + RING:
                    for u, (hv, g) in enumerate(units):
                        m = GROUPS[g][1] * TOK
                        pool.wait_ge(h_soft, u + 1)
                        mine = HD if u < len(units) - 1 else SHARE
                        p4, args = value_products(u, slice(0, mine))
                        nc.gpsimd.tensor_tensor(p4, *args, ALU.mult).then_inc(h_mixed, 1)
                        if mine == HD:
                            pool.wait_ge(h_mixed, 2 * u + 1)
                            nc.gpsimd.tensor_tensor(p4[..., 0:HD // 2], p4[..., 0:HD // 2], p4[..., HD // 2:],
                                                    ALU.add).then_inc(h_mixed, 1)
                    pool.wait_ge(ho_ready, len(units))
                    nc.gpsimd.memset(qkx[:].bitcast(F32).rearrange("p s c i n -> p (s c i n)")[:, 0:2 * HD ** 3], 0.0
                                     ).then_inc(zeroed, 1)
                if i in first_tile:
                    blk, part = first_tile[i]
                    if part == 0:
                        t.more(v_split)
                        for c in range(C):
                            expand_v(c)
                        t.more(v_split)
                        pool.wait_ge(u_taken, av_full[blk][0, 0])
                        expand_v(0)
                    else:
                        pool.wait_ge(u_taken, av_full[blk][0, 1])
                        expand_v(1)
                raw = stage[:, i % STAGES]
                if i in all_aided:
                    t.more(w_high)
                else:
                    t.more(stage_dma[i % STAGES], 16)
                    if i >= RING:
                        pool.wait_ge(w_used, i - RING + 1)
                    nc.gpsimd.tensor_copy(wh[:, i % RING], raw).then_inc(w_ready, 1)
                    pool.wait_ge(w_ready, 2 * i + 1)
                nc.gpsimd.tensor_tensor(wl[:, i % RING], raw, wh[:, i % RING].bitcast(F32),
                                        ALU.subtract).then_inc(w_ready, 1 + (i in all_aided))
                if i + STAGES < tiles and i + STAGES not in all_aided:
                    pool.wait_ge(w_ready, 2 * (i + 1))
                    load(i + STAGES)

        @block.sync
        def _(sp):
            t = Tally(sp)
            for i in range(STAGES):
                sp.dma_start(stage[:, i], weights[:, TILE * i:TILE * (i + 1)]).then_inc(aid_dma[i], 16)
            sp.dma_start(patch_raw[:, 0], patches[0]).then_inc(patch_dma[0], 16)
            for dst, src in ((kshape, constants), (bias, biases), (rt_raw, router), (gt, gate)):
                sp.dma_start(dst[:], src).then_inc(k_dma, 16)
            sp.dma_start(gtb[:], gate_b.partition_broadcast(P)).then_inc(k_dma, 16)
            sp.dma_start(patch_raw[:, 1], patches[1]).then_inc(patch_dma[1], 16)

            sp.dma_start(vb[:, 0], vbias[0].partition_broadcast(P)).then_inc(vb_dma, 16)
            for n in range(1 + EXPERTS):
                if n == 1:
                    sp.wait_ge(gate_ready, 1)
                    sp.dma_start(hb[:], hbias.partition_broadcast(P)).then_inc(hb_dma, 16)
                    for u, (hv, g) in enumerate(units):
                        i0, ni = GROUPS[g]
                        t.more(ho_ready)
                        for i in range(ni):
                            sp.dma_start(mixed[HI * hv + i0 + i].rearrange("a t d -> t a d"),
                                         vf[TOK * i:TOK * (i + 1)].rearrange("t (a d) -> t a d", d=HD)
                                         ).then_inc(mixed_dma, 16)
                        t.more(mixed_dma, 16 * ni)
                        sp.dma_start(rs[0:ni * TOK, u % 2, 0:D],
                                     mixed[HI * hv + i0:HI * hv + i0 + ni].rearrange("i a t d -> (i a t d)")
                                     .rearrange("(r f) -> r f", f=D)
                                     ).then_inc(back_dma[u % 2], 16)

                def extract(blk, hv, c):
                    sp.wait_ge(u_taken, av_full[blk][hv, c])
                    for s in range(HC):
                        r = slice(HD * s, HD * (s + 1))
                        sp.dma_start(t1[r, hv, c], av[r, c, s]).then_inc(av_dma[hv][c], 16)

                if n == 1:
                    sp.wait_ge(zeroed, 4)

                def expand(c, scored=None):
                    t.more(qk_split)
                    if scored:
                        sp.wait_ge(u_taken, scored)
                    for s in range(HC):
                        r = slice(HD * s, HD * (s + 1))
                        sp.dma_start(qkx[r, s, c].bitcast(F32), qks[r, c].bitcast(F32)).then_inc(qk_dma[c], 16)

                for c in range(C):
                    if c or n not in EARLY:
                        expand(c)
                for c in range(C):
                    expand(c, av_full[n]["scores", (0, c)])
                    extract(n, 0, c)
                for c in range(C):
                    extract(n, 1, c)
                if n < EXPERTS:
                    sp.wait_ge(v_split, HALVES * n)
                    sp.dma_start(vb[:, (n + 1) % 2], vbias[n + 1].partition_broadcast(P)).then_inc(vb_dma, 16)
                for i in aided[n] + (list(moe_aided.values()) if n == 0 else []):
                    if n + 1 in EARLY and i == aided[n][-1]:
                        expand(0)
                    sp.wait_ge(w_ready, 2 * (i - STAGES + 1))
                    sp.dma_start(stage[:, i % STAGES], weights[:, TILE * i:TILE * (i + 1)]
                                 ).then_inc(aid_dma[i % STAGES], 16)
            for hv in range(HALVES):
                t.more(out_ready)
                sp.dma_start(out[hv], h[:, hv]).then_inc(out_dma, 16)
            sp.wait_ge(out_dma, 16 * HALVES)

        @block.tensor
        def _(pe):
            t = Tally(pe)
            n = Counter()

            def u_bank():
                t.room(u_taken, n["u"], UB)
                n["u"] += 1
                return u_ring[(n["u"] - 1) % UB]

            def d_bank():
                t.room(d_taken, n["d"], WB)
                n["d"] += 1
                return w_ring[(n["d"] - 1) % WB]

            def product(o, lhs, rhs, start, stop):
                first = nc.tensor.matmul(o, lhs[0], rhs[0], start=start, stop=False)
                second = nc.tensor.matmul(o, lhs[0], rhs[1], start=False, stop=False)
                if n["tiles_done"]:
                    first.then_inc(w_used, n["tiles_done"])
                    n["tiles_done"] = 0
                if n["hid_done"]:
                    second.then_inc(hid_used, n["hid_done"])
                    n["hid_done"] = 0
                return nc.tensor.matmul(o, lhs[1], rhs[0], start=False, stop=stop)

            def tile(i):
                pe.wait_ge(w_ready, 2 * (n["tile"] + i + 1))
                return (n["tile"] + i) % RING

            def done(k):
                n["tile"] += k
                n["tiles_done"] += k

            def w(s, col, width=P):
                return wh[:, s, col:col + width], wl[:, s, col:col + width]

            def a(hv, k, cols=slice(0, NT)):
                return ah[:, hv, k, cols], al[:, hv, k, cols]

            def feature_mean(o, src, full):
                for k in range(C):
                    last = nc.tensor.matmul(o[:, 0:NT], kshape[:, K_MEAN:K_MEAN + P], src[:, k],
                                            start=(k == 0), stop=(k == C - 1))
                last.then_inc(full, 1)

            def mean(src, hv, added=None):
                if added:
                    pe.wait_ge(d_taken, added)
                else:
                    t.more(norm_in)
                feature_mean(d_bank(), src[:, hv], d_full)

            def variance(hv):
                t.more(squared)
                feature_mean(u_bank(), t2[:, hv], u_full)

            def norms(src, residual):
                ends = [n["d"] - C * (HALVES - 1 - hv) if residual else None for hv in range(HALVES)]
                for hv in range(HALVES):
                    mean(src, hv, ends[hv])
                for hv in range(HALVES):
                    variance(hv)

            def linear2(hv, s, bank, full):
                for m in range(2):
                    o = bank()[:, 0:NT]
                    for k in range(C):
                        last = product(o, w(s, P * (2 * m + k)), a(hv, k), k == 0, k == C - 1)
                    last.then_inc(full, 1)
                return last

            def prepare(hv, c, with_v=True, with_qk=True, ahead=0):
                if with_qk:
                    if c == 0:
                        t.more(a_split)
                    for i in range(2):
                        s, o = tile(ahead + i), u_bank()[:, 0:NT]
                        for k in range(C):
                            last = product(o, w(s, P * (C * c + k)), a(hv, k), k == 0, k == C - 1)
                        last.then_inc(u_full, 1)
                if c == 0 and with_v:
                    s = tile(2)
                    for i0, ni in GROUPS:
                        o = d_bank()[0:ni * TOK, 0:D]
                        for k in range(C):
                            last = product(o, a(hv, k, slice(TOK * i0, TOK * (i0 + ni))),
                                           w(s, D * k, D), k == 0, k == C - 1)
                        last.then_inc(d_full, 1)

            def image_logits():
                t.more(xm_ready)
                for hv in range(HALVES):
                    o = d_bank()[0:HI, 0:EXPERTS]
                    for k in range(C):
                        last = nc.tensor.matmul(o, xm[:, hv, k], gt[:, EXPERTS * k:EXPERTS * (k + 1)],
                                                start=(k == 0), stop=(k == C - 1))
                    last.then_inc(d_full, 1)

            def spread_gates():
                t.more(wx_ready)
                for hv in range(HALVES):
                    nc.tensor.matmul(d_bank()[:, 0:EXPERTS * HI], kshape[0:HI, K_ONES:K_ONES + P],
                                     wx[:, hv].rearrange("i e j -> i (e j)"), start=True, stop=True).then_inc(d_full, 1)

            def attention(blk):
                softmax, before = blk > 0, blk > 1
                first, xr_before = n["tile"], n["d"]
                scores = {}

                def out_proj(hv):
                    t.more(a_split)
                    n["tile"] = first + 3
                    linear2(hv, tile(0), d_bank, d_full)
                    n["tile"] = first
                    return n["d"]

                def images(step):
                    hv, c, g = step
                    i0, ni = GROUPS[g]
                    for i in range(ni):
                        at = PITCH * (i0 + i) + MARGIN - TOK * i
                        yield (slice(at, at + ni * TOK), slice(TOK * (i0 + i), TOK * (i0 + i + 1)),
                               i == 0, i == ni - 1)

                for c in range(C):
                    prepare(0, c, with_qk=c > 0 or blk not in EARLY)
                if before:
                    for hv in range(HALVES):
                        mean(xr, hv, xr_before - C * (HALVES - 1 - hv))
                for j in ROUNDS:
                    if j + 2 < J:
                        hv, c, g = steps[j + 2]
                        r = slice(0, GROUPS[g][1] * TOK)
                        if g == 0 and softmax:
                            t.more(pads_ready)
                            t.more(qk_dma[c], 16 * HC)
                        if softmax:
                            o = d_bank()[r, 0:HC * TOK]
                            for padded, own, start, stop in images(steps[j + 2]):
                                last = nc.tensor.matmul(o, qpad[:, c, padded], qkx[:, :, c, 2, own], start=start, stop=stop)
                            last.then_inc(d_full, 1)
                    if 0 <= j + 1 < J:
                        hv, c, g = steps[j + 1]
                        r = slice(0, GROUPS[g][1] * TOK)
                        if g == 0 and not softmax:
                            t.more(pads_ready)
                            t.more(qk_dma[c], 16 * HC)
                        o = u_bank()[r, 0:HC * TOK]
                        for padded, own, start, stop in images(steps[j + 1]):
                            last = product(o, (kpad[:, 0, c, padded], kpad[:, 1, c, padded]),
                                           (qkx[:, :, c, 0, own], qkx[:, :, c, 1, own]), start, stop and not softmax)
                        if softmax:
                            t.more(mx_ready)
                            last = nc.tensor.matmul(o, block_w[r, r], mx[r, (j + 1) % 2], start=False, stop=True)
                        last.then_inc(u_full, 1)
                        scores[j + 1] = n["u"]
                    if 0 <= j < J:
                        r = slice(0, GROUPS[steps[j][2]][1] * TOK)
                        pe.wait_ge(u_taken, scores[j])
                        o = (u_bank() if softmax else d_bank())[r, 0:HC * TOK]
                        nc.tensor.matmul(o, kshape[r, K_BLOCK:K_BLOCK + r.stop], e_t[r, j % 2], start=True, stop=True
                                         ).then_inc(u_full if softmax else d_full, 1)
                    if 0 <= j - 1 < J:
                        hv, c, g = steps[j - 1]
                        i0, ni = GROUPS[g]
                        r = slice(0, ni * TOK)
                        if g == 0:
                            t.more(v_dma[c], 16 * SLOTS)
                        t.more(ps_ready)
                        for i in range(ni):
                            o = u_bank()[:, 0:HC * TOK]
                            product(o, (vm[r, i, g, P * c:P * (c + 1)], vm[r, i, g, D + P * c:D + P * (c + 1)]),
                                    (eh[r, (j - 1) % 3], el[r, (j - 1) % 3]), True, True
                                    ).then_inc(u_full, 1)
                    if j in STAGE:
                        prepare(1, STAGE[j], with_v=False)
                    if j in PREPARE:
                        prepare(1, PREPARE[j], with_qk=False)
                        if PREPARE[j] == C - 1:
                            n["tiles_done"] += 3
                    if before and j == N2_VAR:
                        for hv in range(HALVES):
                            variance(hv)
                    if blk == 1 and j == GATE_LOGITS:
                        image_logits()
                    if blk == 1 and j == GATE_LOGITS + 2:
                        spread_gates()
                    if j == OUT_P:
                        residual = out_proj(0)
                    if j == OUT_P + 1:
                        mean(xr, 0, residual)
                    if j == N1_VAR:
                        variance(0)
                n["tile"] += 4
                ff, fold, end = feed_forward()
                t.more(a_split)
                ff(0, 0)
                ff(0, 1)
                n["tile"] -= 4
                residual = out_proj(1)
                n["tile"] += 4
                n["tiles_done"] += 1
                fold(0)
                ff(0, 2)
                pe.wait_ge(d_taken, residual)
                feature_mean(u_bank(), xr[:, 1], u_full)
                if LEAD > BETWEEN:
                    ff(0, BETWEEN)
                variance(1)
                for i in range(BETWEEN + 1, LEAD):
                    ff(0, i)
                fold(1)
                t.more(a_split)
                for hv, i in FF_REST:
                    if (hv, i) == (0, len(FF_TILES) - 1) and blk + 1 in EARLY:
                        prepare(0, 0, with_v=False, ahead=len(FF_TILES))
                    ff(hv, i)
                end()

            def feed_forward():
                acc, before = {}, t.n[hid_ready.name]
                slots = {pair: 2 * k for k, pair in enumerate(made)}

                def fold(hv):
                    acc[hv] = [d_bank() for _ in range(C)]

                def tile_products(hv, i):
                    way, p = FF_TILES[i]
                    s = tile(i)
                    if way == "up":
                        linear2(hv, s, u_bank, u_full)
                    else:
                        for b in range(2):
                            block = slots[hv, p] + b
                            pe.wait_ge(hid_ready, before + block + 1)
                            for m in range(C):
                                last = product(acc[hv][m][:, 0:NT], w(s, P * (2 * b + m)),
                                               (hid[:, block % HID, 0], hid[:, block % HID, 1]),
                                               p == 0 and b == 0, p == len(FF_TILES) // 2 - 1 and b == 1)
                                if p == len(FF_TILES) // 2 - 1 and b == 1:
                                    last.then_inc(d_full, 1)
                            n["hid_done"] += 1
                    if hv == HALVES - 1:
                        n["tiles_done"] += 1

                def end():
                    n["tile"] += len(FF_TILES)
                    n["hid"] += 2 * len(made)
                    t.up(hid_ready, 2 * len(made))

                return tile_products, fold, end

            def back(u):
                if u >= 0:
                    m = GROUPS[units[u][1]][1] * TOK
                    t.more(back_dma[u % 2], 16)
                    for c in range(C):
                        nc.tensor.transpose(d_bank()[:, 0:m], rs[0:m, u % 2, P * c:P * (c + 1)],
                                            kshape[0:m, K_IDENT:K_IDENT + m]).then_inc(d_full, 1)

            for hv in range(HALVES):
                t.more(patch_split)
                for m in range(C):
                    o = u_bank()[:, 0:NT]
                    for k in range(KP):
                        b = KP * m + k
                        s = tile(b // 4)
                        last = product(o, w(s, P * (b % 4)), (patch_h[:, hv, k], patch_l[:, hv, k]),
                                       k == 0, k == KP - 1)
                    last.then_inc(u_full, 1)
            done(3)
            s = tile(0)
            pe.wait_ge(k_ready, 1)
            for hv in range(HALVES):
                t.more(a_split)
                linear2(hv, s, d_bank, d_full)
            done(1)

            norms(h, True)
            norms(x, False)
            attention(0)

            norms(h, False)
            acc = None
            for hv in range(HALVES):
                t.more(a_split)
                o = d_bank()
                for b in range(RB):
                    for k in range(C):
                        last = product(o[0:RT, ROUTED * b:ROUTED * (b + 1)], a(hv, k, slice(RT * b, RT * (b + 1))),
                                       (rt[:, 0, ROUTED * k:ROUTED * (k + 1)], rt[:, 1, ROUTED * k:ROUTED * (k + 1)]),
                                       k == 0, k == C - 1)
                last.then_inc(d_full, 1)
            for hv in range(HALVES):
                t.more(gate_ready)
                o = d_bank()
                for b in range(RB):
                    last = nc.tensor.transpose(o[0:ROUTED, RT * b:RT * (b + 1)], gw[:, hv, ROUTED * b:ROUTED * (b + 1)],
                                               kshape[0:RT, K_IDENT:K_IDENT + RT])
                last.then_inc(d_full, 1)
            gates = n["d"]
            acc = [[d_bank() for _ in range(C)] for _ in range(HALVES)]
            E = SHARED + ROUTED
            for e in range(E + 1):
                if e < E:
                    s = tile(1 if e else 0)
                    for hv in range(HALVES):
                        o = u_bank()[:, 0:NT]
                        for k in range(C):
                            last = product(o, w(s, P * k), a(hv, k), k == 0, k == C - 1)
                        last.then_inc(u_full, 1)
                        if e >= SHARED:
                            if e == SHARED and hv == 0:
                                pe.wait_ge(d_taken, gates)
                            r = e - SHARED
                            o = u_bank()[:, 0:NT]
                            pick = eye_w[:, r:r + 1].to_broadcast([ROUTED, P])
                            nc.tensor.matmul(o, pick, gth[:, hv], start=True, stop=False)
                            nc.tensor.matmul(o, pick, gtl[:, hv], start=False, stop=True
                                             ).then_inc(u_full, 1)
                if e:
                    s = tile(0)
                    for hv in range(HALVES):
                        t.more(hid_ready)
                        slot = n["hid"] % HID
                        n["hid"] += 1
                        for m in range(C):
                            last = product(acc[hv][m][:, 0:NT], w(s, P * (2 + m)), (hid[:, slot, 0], hid[:, slot, 1]),
                                           e == 1, e == E)
                            if e == E:
                                last.then_inc(d_full, 1)
                        n["hid_done"] += 1
                    done(1)

            norms(h, True)
            t.more(a_split, HALVES)
            for u in range(len(units) + 3):
                if u < len(units):
                    hv, g = units[u]
                    i0, ni = GROUPS[g]
                    for i in range(3):
                        s = tile(i)
                        o = d_bank()[0:ni * TOK, 0:D]
                        for k in range(C):
                            last = product(o, a(hv, k, slice(TOK * i0, TOK * (i0 + ni))), w(s, D * k, D),
                                           k == 0, k == C - 1)
                        last.then_inc(d_full, 1)
                back(u - 3)
            done(3)
            s = tile(0)
            for hv in range(HALVES):
                t.more(a_split)
                linear2(hv, s, d_bank, d_full)
            done(1)

            norms(h, True)
            for e in range(EXPERTS):
                attention(1 + e)
            norms(xr, True)

        @block.scalar
        def _(act):
            t = Tally(act)
            n = Counter()

            def bank():
                t.more(u_full)
                n["u"] += 1
                return u_ring[(n["u"] - 1) % UB]

            def rsqrt(hv):
                o = bank()[:, 0:NT]
                nc.scalar.activation(rstd[:, hv], o, ACT.Ln, bias=eps_t[:, 0:1]).then_inc(*t.up(u_taken))
                t.own(u_taken)
                nc.scalar.activation(rstd[:, hv], rstd[:, hv], ACT.Exp, scale=-0.5).then_inc(*t.up(r_ready))

            def squares(hv, mean_taken=d_taken):
                t.more(dve_in)
                for c, s in enumerate((mean_taken, squared)):
                    nc.scalar.activation(t2[:, hv, c], t1[:, hv, c], ACT.Square).then_inc(s, 1)

            def affine(hv, g, b):
                t.more(dve_in)
                for c in range(C):
                    last = nc.scalar.activation(ah[:, hv, c], t2[:, hv, c], ACT.Identity,
                                                scale=bc(g, c), bias=bc(b, c))
                last.then_inc(*t.up(act_out))

            def norms(g=None, b=None):
                for hv in range(HALVES):
                    squares(hv)
                for hv in range(HALVES):
                    rsqrt(hv)
                if g:
                    for hv in range(HALVES):
                        affine(hv, g, b)

            def round_tile(i):
                t.more(aid_dma[i % STAGES], 16)
                if i >= RING:
                    act.wait_ge(w_used, i - RING + 1)
                nc.scalar.activation(wh[:, i % RING], stage[:, i % STAGES], ACT.Copy).then_inc(w_high, 1)

            def attention(blk, qk_bias, norm1, before, f, b1):
                softmax = blk > 0

                def prepare(hv, c, qk_bias=qk_bias):
                    for i, dst in ((0, t1), (1, t2)):
                        o = bank()[:, 0:NT]
                        nc.scalar.activation(dst[:, hv, c], o, ACT.Identity, bias=bc(qk_bias, 2 * i + c)
                                             ).then_inc(*t.up(u_taken))
                    if not softmax:
                        for _m in range(2):
                            t.more(dve_in)
                            nc.scalar.activation(xr[:, hv, c], xr[:, hv, c], ACT.Exp).then_inc(*t.up(act_out))

                for c in range(C):
                    if c or blk not in EARLY:
                        prepare(0, c)
                if blk in EARLY:
                    round_tile(aided[blk - 1][-1])
                for j in ROUNDS:
                    if j == N1_VAR:
                        squares(0)
                    if 0 <= j + 1 < J:
                        r = slice(0, GROUPS[steps[j + 1][2]][1] * TOK)
                        o = bank()[r, 0:HC * TOK]
                        t.room(ps_ready, n["e"], 2)
                        n["e"] += 1
                        score_f, sc = (ACT.Exp, HD ** -0.5) if softmax else (ACT.Identity, 1.0)
                        nc.scalar.activation(e_t[r, (j + 1) % 2], o, score_f, scale=sc).then_inc(*t.up(u_taken))
                    if softmax and 0 <= j < J:
                        r = slice(0, GROUPS[steps[j][2]][1] * TOK)
                        o = bank()[r, 0:HC * TOK]
                        nc.scalar.activation(rs[r, j % 2], o, ACT.Ln).then_inc(*t.up(u_taken))
                        t.own(u_taken)
                        nc.scalar.activation(rs[r, j % 2], rs[r, j % 2], ACT.Exp, scale=-1.0
                                             ).then_inc(*t.up(r_ready))
                    if 0 <= j - 1 < J:
                        hv, c, g = steps[j - 1]
                        i0, ni = GROUPS[g]
                        if g == 0:
                            if n["av", c]:
                                act.wait_ge(av_dma[1 - hv][c], 16 * HC * ((n["av", c] + 1) // 2))
                            n["av", c] += 1
                        for i in range(ni):
                            o = bank()[:, 0:HC * TOK].rearrange("p (s q) -> p s q", q=TOK)
                            at = TOK * (i0 + i)
                            nc.scalar.activation(av[:, c, :, at:at + TOK], o, ACT.Copy
                                                 ).then_inc(*t.up(u_taken))
                    if before and j == N2_VAR - 1:
                        for hv in range(HALVES):
                            squares(hv)
                    if blk == 1 and j == GATE_LOGITS + 1:
                        for hv in range(HALVES):
                            t.more(dve_in)
                            nc.scalar.activation(ge[:, hv], gl[:, hv], ACT.Exp).then_inc(*t.up(act_out))
                    if j in STAGE:
                        prepare(1, STAGE[j])
                    if before and j == N2_VAR:
                        for hv in range(HALVES):
                            rsqrt(hv)
                    if j == N1_VAR:
                        rsqrt(0)
                affine(0, *norm1)
                todo = [bc(b1, 2 * p + m) for _, p in made for m in range(2)]

                def hiddens(k):
                    for _ in range(k):
                        hidden(f, todo.pop(0))

                hiddens(4)
                n["u"] += 1
                t.up(u_full)
                squares(1, t.up(u_taken)[0])
                hiddens(LATE)
                if not softmax:
                    nc.scalar.preload_act_table_set("natural_log_exp_and_others")
                rsqrt(1)
                affine(1, *norm1)
                high = aided[blk]
                for blocks_first, free in ((4, 1), (2, 2), (2, 1), (2, 1)):
                    hiddens(blocks_first)
                    for i in high[:free]:
                        round_tile(i)
                    high = high[free:]
                if blk + 1 in EARLY:
                    prepare(0, 0, f"e{blk}_qk_b")
                for i in high[:-1] if blk + 1 in EARLY else high:
                    round_tile(i)

            def hidden(f, b):
                o = bank()[:, 0:NT]
                t.room(hid_ready, n["hf"], 2)
                nc.scalar.activation(hf[:, n["hf"] % 2], o, f, **({"bias": b} if b is not None else {})
                                     ).then_inc(*t.up(u_taken))
                n["hf"] += 1

            for i in range(STAGES):
                round_tile(i)
            act.wait_ge(k_ready, 1)
            for hv in range(HALVES):
                for m in range(C):
                    o = bank()[:, 0:NT]
                    nc.scalar.activation(t1[:, hv, m], o, ACT.Silu, bias=bc("tok_b1", m)).then_inc(*t.up(u_taken))
            nc.scalar.preload_act_table_set("natural_log_exp_and_others")
            norms()
            norms("g1", "be1")
            attention(0, "l0_qk_b", ("g2", "be2"), False, ACT.Gelu, "l0_b1")
            nc.scalar.preload_act_table_set("natural_log_exp_and_others")
            norms()
            for hv in range(HALVES):
                t.more(dve_in)
                nc.scalar.activation(pr[:], lg[:], ACT.Exp).then_inc(*t.up(act_out))
            for e in range(SHARED + ROUTED):
                for hv in range(HALVES):
                    hidden(ACT.Gelu, None)
                    if e >= SHARED:
                        o = bank()[:, 0:NT]
                        nc.scalar.activation(gb[:, n["gb"] % 2], o, ACT.Copy).then_inc(*t.up(u_taken))
                        n["gb"] += 1
                if e in moe_aided:
                    round_tile(moe_aided[e])
            nc.scalar.preload_act_table_set("natural_log_exp_and_others")
            norms()
            for u in range(len(units)):
                t.more(dve_in)
                nc.scalar.activation(h_s(u), h_s(u), ACT.Exp, scale=HD ** -0.5).then_inc(*t.up(act_out))
            norms()
            for e in range(EXPERTS):
                attention(1 + e, f"e{e}_qk_b", (f"e{e}_g1", f"e{e}_be1"), e > 0, ACT.Relu, f"e{e}_b1")
            norms()

        @block.vector
        def _(dve):
            t = Tally(dve)
            n = Counter()
            v = nc.vector

            def step(ins):
                ins.then_inc(*t.up(dve_step))
                t.own(dve_step)

            def tell(ins, s):
                ins.then_inc(*t.up(s))
                t.own(s)

            def banks(k=1):
                n["u"] += k

            def taken():
                n["u"] += 1
                dve.wait_ge(u_taken, n["u"])

            def bank():
                t.more(d_full)
                n["d"] += 1
                return w_ring[(n["d"] - 1) % WB]

            def take(ins):
                ins.then_inc(*t.up(d_taken))
                t.own(d_taken)

            def split(src, hv):
                step(v.tensor_copy(ah[:, hv], src))
                tell(v.tensor_tensor(al[:, hv], src, ah[:, hv].bitcast(F32), ALU.subtract), a_split)

            def affine(dst, hv, g, b):
                for c in range(C):
                    step(v.tensor_scalar(dst[:, hv, c], t2[:, hv, c], bc(g, c), bc(b, c), ALU.mult, ALU.add))

            def low(src, hv, g, b):
                affine(src, hv, g, b)
                t.more(act_out)
                tell(v.tensor_tensor(al[:, hv], src[:, hv], ah[:, hv].bitcast(F32), ALU.subtract), a_split)

            def center(src, hv, from_u=False):
                if from_u:
                    n["u"] += 1
                    dve.wait_ge(u_full, n["u"])
                    o = u_ring[(n["u"] - 1) % UB][:, 0:NT]
                else:
                    o = bank()[:, 0:NT]
                    t.up(d_taken)
                tell(v.tensor_tensor(t1[:, hv], src[:, hv], o.unsqueeze(1).to_broadcast([P, C, NT]), ALU.subtract),
                     dve_in)

            def normal(dst, hv, s=None):
                t.more(r_ready)
                ins = v.tensor_tensor(dst[:, hv], t1[:, hv], rstd[:, hv].unsqueeze(1).to_broadcast([P, C, NT]), ALU.mult)
                if s is not None:
                    tell(ins, s)
                else:
                    step(ins)

            def norms(src, dst, g=None, b=None, last=False, then=None):
                for hv in range(HALVES):
                    center(src, hv)
                banks(HALVES)
                for hv in range(HALVES):
                    normal(t2 if g else dst, hv, then if last or not g else dve_in)
                if g:
                    for hv in range(HALVES):
                        (affine if last else low)(dst, hv, g, b)

            def residual(dst, src, b, halves=range(HALVES)):
                for hv in halves:
                    for c in range(C):
                        o = bank()[:, 0:NT]
                        if b:
                            take(v.scalar_tensor_tensor(dst[:, hv, c], o, bc(b, c), src[:, hv, c], ALU.add, ALU.add))
                        else:
                            take(v.tensor_tensor(dst[:, hv, c], o, src[:, hv, c], ALU.add))

            def gated(e, hv):
                for c in range(C):
                    step(v.tensor_tensor(by_image(rstd[:])[:, c], by_image(xr[:, hv])[:, c],
                                         wimg[:, hv, e].unsqueeze(2).to_broadcast([P, HI, TOK]), ALU.mult))
                last = v.tensor_tensor(h[:, hv], h[:, hv], rstd[:], ALU.add)
                if e == EXPERTS - 1:
                    tell(last, out_ready)
                else:
                    step(last)

            def images(ap):
                return ap[:, :, MARGIN:PADDED].rearrange("p c (i w) -> p c i w", w=PITCH)[:, :, :, 0:TOK]

            def by_image(ap):
                return ap.rearrange("p c (i q) -> p c i q", q=TOK)

            def image_gates(stage):
                for hv in range(HALVES):
                    if stage == 0:
                        step(v.tensor_reduce(xm[:, hv], by_image(x[:, hv]), AX.X, ALU.add))
                        ins = v.tensor_scalar(xm[:, hv], xm[:, hv], 1.0 / TOK, None, ALU.mult)
                        if hv:
                            tell(ins, xm_ready)
                        else:
                            step(ins)
                    if stage == 1:
                        step(v.memset(lg1[:, hv], -3e38))
                        take(v.tensor_tensor(lg1[:, hv, 0:EXPERTS], bank()[0:HI, 0:EXPERTS], gtb[0:HI], ALU.add))
                        step(v.max(top1[:, hv], lg1[:, hv]))
                        tell(v.tensor_scalar(gl[:, hv], lg1[:, hv, 0:EXPERTS], top1[:, hv, 0:1], None, ALU.subtract),
                             dve_in)
                    if stage == 2:
                        t.more(act_out)
                        ex, total = ge[:, hv], sel_n[0:HI, 0:1]
                        step(v.tensor_reduce(total, ex, AX.X, ALU.add))
                        step(v.reciprocal(total, total))
                        step(v.tensor_scalar(ex, ex, total, None, ALU.mult))
                        keep = select(lg1[:, hv, 0:EXPERTS], top1[:, hv:hv + 1, TOP2 - 1:TOP2],
                                      kshape[0:HI, K_FIRST:K_FIRST + EXPERTS], TOP2, HI, 1, EXPERTS,
                                      sm[0:HI, 0:2 * EXPERTS].rearrange("p (a n) -> p a n", a=2))
                        step(v.tensor_tensor(keep, keep, ex, ALU.mult))
                        ins = v.tensor_tensor(wx[:, hv], keep.unsqueeze(2).to_broadcast([HI, EXPERTS, HI]),
                                              kshape[0:HI, K_EYE8:K_EYE8 + HI].unsqueeze(1)
                                              .to_broadcast([HI, EXPERTS, HI]), ALU.mult)
                        if hv:
                            tell(ins, wx_ready)
                        else:
                            step(ins)
                    if stage == 3:
                        o = bank()[:, 0:EXPERTS * HI].rearrange("p (e i) -> p e i", i=HI)
                        take(v.tensor_copy(wimg[:, hv], o))

            def attention(softmax, src, blk, res, out_b, norm_dst, norm1):
                before = blk > 1

                def prepare(hv, c, with_v=True, with_qk=True):
                    if with_qk:
                        stage_qk(hv, c)
                        pad_qk(hv, c)
                    if with_v and c == 0:
                        prepare_v(hv)

                def stage_qk(hv, c):
                    banks(2)
                    dve.wait_ge(u_taken, n["u"])
                    q, k, ex = t1[:, hv, c], t2[:, hv, c], xr[:, hv, c]
                    if not softmax:
                        for m in (q, k):
                            tell(v.tensor_scalar(ex, m, 0.0, None, ALU.min), dve_in)
                            t.more(act_out)
                            step(v.scalar_tensor_tensor(m, m, 0.0, ex, ALU.max, ALU.add))
                    if n["att", c]:
                        dve.wait_ge(qk_dma[c], 16 * HC * n["att", c])
                    n["att", c] += 1
                    step(v.tensor_copy(qks[:, c, 0], q))
                    step(v.tensor_copy(qks[:, c, 2], k))
                    tell(v.tensor_tensor(qks[:, c, 1], q, qks[:, c, 0].bitcast(F32), ALU.subtract), qk_split)

                def pad_qk(hv, c):
                    q, k = t1[:, hv, c], t2[:, hv, c]
                    row = lambda ap: ap.rearrange("p (i q) -> p i q", q=TOK)
                    v.tensor_copy(images(kpad[:, 0])[:, c], row(k))
                    ins = v.tensor_tensor(images(kpad[:, 1])[:, c], row(k), row(qks[:, c, 2].bitcast(F32)), ALU.subtract)
                    if softmax:
                        ins = v.tensor_copy(images(qpad)[:, c], row(q))
                    tell(ins, pads_ready)

                def prepare_v(hv):
                    dve.wait_ge(vb_dma, 16 * (blk + 1))
                    for d in range(C):
                        if n["vs"]:
                            dve.wait_ge(v_dma[d], 16 * SLOTS * n["vs"])
                    n["vs"] += 1
                    for g, (i0, ni) in enumerate(GROUPS):
                        r = slice(0, ni * TOK)
                        o = bank()[r, 0:D]
                        take(v.tensor_tensor(vf[r], o, vb[r, blk % 2], ALU.add))
                        step(v.tensor_copy(vs[r, g, 0:D], vf[r]))
                        last = v.tensor_tensor(vs[r, g, D:2 * D], vf[r], vs[r, g, 0:D].bitcast(F32), ALU.subtract)
                        if g < len(GROUPS) - 1:
                            step(last)
                    tell(last, v_split)

                def own_products(hv):
                    for c in range(C):
                        t.more(av_dma[hv][c], 16 * HC)
                    split(t1[:, hv], hv)

                if softmax and blk not in EARLY:
                    split(src[:, 0], 0)
                for c in range(C):
                    prepare(0, c, with_qk=c > 0 or blk not in EARLY)
                for j in ROUNDS:
                    if blk == 1 and 0 <= j - GATE_LOGITS < 4:
                        image_gates(j - GATE_LOGITS)
                    if before and j == N2_VAR - 1:
                        for hv in range(HALVES):
                            center(xr, hv)
                    if before and j == N2_VAR + 1:
                        for hv in range(HALVES):
                            normal(t2, hv)
                            affine(xr, hv, f"e{blk - 2}_g2", f"e{blk - 2}_be2")
                    if before and j == N2_VAR + 2:
                        for hv in range(HALVES):
                            gated(blk - 2, hv)
                    if softmax and STAGE.get(j) == 0:
                        split(src[:, 1], 1)
                    if j == OUT_P:
                        own_products(0)
                    if j == OUT_P + 1:
                        residual(xr, res, out_b, [0])
                    if j == N1_VAR:
                        center(xr, 0)
                    if j == N1_VAR + 1:
                        normal(t2, 0, dve_in)
                    if softmax and j + 2 < J:
                        m = GROUPS[steps[j + 2][2]][1] * TOK
                        lim = shift[0:m, j % 2]
                        o = bank()[0:m, 0:HC * TOK].rearrange("p (s k) -> p s k", k=TOK)
                        v.tensor_reduce(lim, o, AX.X, ALU.max, negate=True).then_inc(*t.up(d_taken))
                    banks(0 <= j + 1 < J)
                    scores_u = n["u"]
                    if 0 <= j < J:
                        r = slice(0, GROUPS[steps[j][2]][1] * TOK)
                        i = j % 2
                        if softmax:
                            banks()
                            t.more(r_ready)
                        else:
                            o = bank()[r, 0:HC * TOK]
                            take(v.tensor_scalar(rs[r, i], o, ATTN_EPS, None, ALU.max))
                            step(v.reciprocal(rs[r, i], rs[r, i]))
                        v.tensor_tensor(e_t[r, i], e_t[r, i], rs[r, i], ALU.mult).then_inc(*t.up(dve_step))
                    if softmax and j + 2 < J:
                        t.own(d_taken)
                        v.tensor_tensor(mx[0:m, j % 2],
                                        kshape[0:m, K_DELTA:K_DELTA + TOK].unsqueeze(1).to_broadcast([m, HC, TOK]),
                                        lim.unsqueeze(2).to_broadcast([m, HC, TOK]), ALU.mult
                                        ).then_inc(*t.up(mx_ready))
                    if 0 <= j < J:
                        t.own(dve_step)
                        step(v.tensor_copy(eh[r, j % 3], e_t[r, i]))
                        tell(v.tensor_tensor(el[r, j % 3], e_t[r, i], eh[r, j % 3].bitcast(F32), ALU.subtract), ps_ready)
                    if 0 <= j - 1 < J:
                        banks(GROUPS[steps[j - 1][2]][1])
                    if j in STAGE:
                        stage_qk(1, STAGE[j])
                    if j in PREPARE:
                        dve.wait_ge(u_taken, scores_u)
                        pad_qk(1, PREPARE[j])
                        prepare(1, PREPARE[j], with_qk=False)
                    if before and j == N2_VAR:
                        banks(HALVES)
                    if j == N1_VAR:
                        banks()
                low(norm_dst, 0, *norm1)
                first, blocks = n["hid"], iter(range(2 * len(made)))

                def hiddens(k):
                    for _ in range(k):
                        b = next(blocks)
                        used = first - 1 if b < HID else first + 2 * eaten.index(made[(b - HID) // 2]) + b % 2
                        hidden(False, b % HID, used)

                dve.wait_ge(av_dma[1][0], t.n[av_dma[1][0].name] + 16 * HC)
                hiddens(4)
                own_products(1)
                residual(xr, res, out_b, [1])
                center(xr, 1, from_u=True)
                hiddens(LATE)
                banks()
                normal(t2, 1, dve_in)
                low(norm_dst, 1, *norm1)
                hiddens(2 * len(made) - 6 - LATE)
                if blk + 1 in EARLY:
                    split(src[:, 0], 0)
                hiddens(2)
                if blk + 1 in EARLY:
                    prepare(0, 0, with_v=False)

            def hidden(by_gate, slot=None, used=None):
                taken()
                i = n["hid"] % 2
                if by_gate:
                    taken()
                    step(v.tensor_tensor(hf[:, i], hf[:, i], gb[:, n["gb"] % 2], ALU.mult))
                    n["gb"] += 1
                if slot is None:
                    slot, used = n["hid"] % HID, n["hid"] - HID
                if used >= 0:
                    dve.wait_ge(hid_used, used + 1)
                n["hid"] += 1
                step(v.tensor_copy(hid[:, slot, 0], hf[:, i]))
                tell(v.tensor_tensor(hid[:, slot, 1], hf[:, i], hid[:, slot, 0].bitcast(F32), ALU.subtract), hid_ready)

            def select(values, least, first, count, m, nb, ne, work):
                view = values.rearrange("p (b e) -> p b e", e=ne)
                lim = least.to_broadcast([m, nb, ne])
                w3 = [work[:, i].rearrange("p (b e) -> p b e", e=ne) for i in range(2)]
                step(v.tensor_tensor(w3[0], view, lim, ALU.is_gt))
                step(v.tensor_tensor(w3[1], view, lim, ALU.is_equal))
                step(v.tensor_reduce(sel_n[0:m, 0:nb], w3[0], AX.X, ALU.add))
                step(v.tensor_tensor_scan(sel_c[0:m, 0:nb * ne], first, work[:, 1], 0.0, ALU.mult, ALU.add))
                c3 = sel_c[0:m, 0:nb * ne].rearrange("p (b e) -> p b e", e=ne)
                step(v.tensor_tensor(c3, c3, sel_n[0:m, 0:nb].unsqueeze(2).to_broadcast([m, nb, ne]), ALU.add))
                step(v.scalar_tensor_tensor(work[:, 1], sel_c[0:m, 0:nb * ne], float(count), work[:, 1],
                                            ALU.is_le, ALU.mult))
                step(v.tensor_tensor(work[:, 0], work[:, 0], work[:, 1], ALU.add))
                return work[:, 0]

            def mixed_out(u):
                m = GROUPS[units[u][1]][1] * TOK
                n["groups"] += 1
                if n["groups"] > 1:
                    dve.wait_ge(mixed_dma, 16 * n["images"])
                n["images"] += GROUPS[units[u][1]][1]
                left = HD // 2
                if u == len(units) - 1:
                    left = HD
                    p4, args = value_products(u, slice(SHARE, HD))
                    step(v.tensor_tensor(p4, *args, ALU.mult))
                dve.wait_ge(h_mixed, 2 * (u + 1) - (left == HD))
                tell(v.tensor_reduce(vf[0:m].rearrange("p (a d) -> p a d", d=HD),
                                     hv_p[0:m, u % 2].rearrange("p (a d b) -> p a d b", a=HD, b=HD)[..., 0:left],
                                     AX.X, ALU.add), ho_ready)

            def over_heads(u):
                m = GROUPS[units[u][1]][1] * TOK
                own = [0, D, D * (2 + u % 2)]
                if u >= 2:
                    dve.wait_ge(h_mixed, 2 * (u - 2) + 1)
                for i, at in enumerate(own):
                    take(v.tensor_tensor(hq[0:m, at:at + D], bank()[0:m, 0:D], hb[0:m, D * i:D * (i + 1)], ALU.add))
                q, k = (hq[0:m, D * i:D * (i + 1)].rearrange("p (a d) -> p a d", d=HD) for i in range(2))
                p4 = hp[0:m].rearrange("p (a b d) -> p a b d", a=HD, b=HD)
                s3 = h_s(u).rearrange("p (a b) -> p a b", b=HD)
                lim = shift[0:m].rearrange("p i s -> p (i s)")
                step(v.tensor_tensor(p4, q.unsqueeze(2).to_broadcast([m] + cube),
                                     k.unsqueeze(1).to_broadcast([m] + cube), ALU.mult))
                step(v.tensor_reduce(s3, p4, AX.X, ALU.add))
                step(v.tensor_reduce(lim, s3, AX.X, ALU.max))
                tell(v.tensor_tensor(s3, s3, lim.unsqueeze(2).to_broadcast([m, HD, HD]), ALU.subtract), dve_in)
                if u >= 2:
                    mixed_out(u - 2)
                t.more(act_out)
                step(v.tensor_reduce(lim, s3, AX.X, ALU.add))
                step(v.reciprocal(lim, lim))
                tell(v.tensor_tensor(s3, s3, lim.unsqueeze(2).to_broadcast([m, HD, HD]), ALU.mult), h_soft)

            def heads_back(u):
                if u >= 0:
                    hv, g = units[u]
                    i0, ni = GROUPS[g]
                    for c in range(C):
                        take(v.tensor_copy(t1[:, hv, c, TOK * i0:TOK * (i0 + ni)], bank()[:, 0:ni * TOK]))

            def split_patches(hv):
                dve.wait_ge(patch_dma[hv], 16)
                step(v.tensor_copy(patch_h[:, hv], patch_raw[:, hv]))
                tell(v.tensor_tensor(patch_l[:, hv], patch_raw[:, hv], patch_h[:, hv].bitcast(F32), ALU.subtract),
                     patch_split)

            step(v.memset(vm[:].bitcast(F32), 0.0))
            split_patches(0)
            dve.wait_ge(k_dma, 16 * 5)
            step(v.memset(eps_t[:], LN_EPS))
            step(v.tensor_copy(block_w[:], kshape[0:PITCH, K_BLOCK:K_BLOCK + PITCH]))
            step(v.tensor_copy(eye_w[:], kshape[0:ROUTED, K_IDENT:K_IDENT + ROUTED]))
            step(v.tensor_copy(rt[:, 0], rt_raw[:]))
            tell(v.tensor_tensor(rt[:, 1], rt_raw[:], rt[:, 0].bitcast(F32), ALU.subtract), k_ready)
            split_patches(1)
            for hv in range(HALVES):
                banks(C)
                dve.wait_ge(u_taken, n["u"])
                split(t1[:, hv], hv)
            for hv in range(HALVES):
                for c in range(C):
                    take(v.tensor_scalar(h[:, hv, c], bank()[:, 0:NT], bc("tok_b2", c), None, ALU.add))

            norms(h, x, then=norm_in)
            norms(x, t1, "g1", "be1")
            dve.wait_ge(zeroed, 3)
            attention(False, t1, 0, x, "l0_out_b", t1, ("g2", "be2"))
            residual(t2, xr, "l0_b2")
            for hv in range(HALVES):
                tell(v.tensor_tensor(h[:, hv], h[:, hv], t2[:, hv], ALU.add), norm_in)

            norms(h, x)
            for hv in range(HALVES):
                split(x[:, hv], hv)
            for hv in range(HALVES):
                o = bank()[0:RT, 0:RB * ROUTED]
                o3 = o.rearrange("p (b e) -> p b e", e=ROUTED)
                l3 = lg[:].rearrange("p (b e) -> p b e", e=ROUTED)
                p3 = pr[:].rearrange("p (b e) -> p b e", e=ROUTED)
                step(v.tensor_reduce(sel_n[:, 0:RB], o3, AX.X, ALU.max))
                tell(v.tensor_tensor(l3, o3, sel_n[:, 0:RB].unsqueeze(2).to_broadcast([RT, RB, ROUTED]), ALU.subtract), dve_in)
                t.more(act_out)
                tell(v.tensor_reduce(sel_n[:, 0:RB], p3, AX.X, ALU.add), d_taken)
                t.own(d_taken)
                step(v.reciprocal(sel_n[:, 0:RB], sel_n[:, 0:RB]))
                step(v.tensor_tensor(p3, p3, sel_n[:, 0:RB].unsqueeze(2).to_broadcast([RT, RB, ROUTED]), ALU.mult))
                for b in range(RB):
                    step(v.max(top[:, b], pr[:, ROUTED * b:ROUTED * (b + 1)]))
                keep = select(pr[:], top[:, :, TOPK - 1:TOPK], kshape[0:RT, K_FIRST:K_FIRST + RB * ROUTED],
                              TOPK, RT, RB, ROUTED, sm[:].rearrange("p (a n) -> p a n", a=2))
                tell(v.tensor_tensor(gw[:, hv], keep, pr[:], ALU.mult), gate_ready)
            for hv in range(HALVES):
                o = bank()[0:ROUTED, 0:NT]
                step(v.tensor_copy(gth[:, hv], o))
                take(v.tensor_tensor(gtl[:, hv], o, gth[:, hv].bitcast(F32), ALU.subtract))
            for e in range(SHARED + ROUTED):
                for hv in range(HALVES):
                    hidden(e >= SHARED)
            residual(h, h, None)

            norms(h, x)
            for hv in range(HALVES):
                split(x[:, hv], hv)
            dve.wait_ge(hb_dma, 16)
            for u in range(len(units)):
                over_heads(u)
                heads_back(u - 3)
            for u in range(len(units) - 2, len(units)):
                mixed_out(u)
                heads_back(u - 1)
            heads_back(len(units) - 1)
            for hv in range(HALVES):
                split(t1[:, hv], hv)
            residual(h, h, "l1_out_b")

            norms(h, x)
            for e in range(EXPERTS):
                attention(True, x, 1 + e, x, f"e{e}_out_b", xr, (f"e{e}_g1", f"e{e}_be1"))
                residual(xr, xr, f"e{e}_b2")
            e = EXPERTS - 1
            norms(xr, xr, f"e{e}_g2", f"e{e}_be2", last=True)
            for hv in range(HALVES):
                gated(e, hv)


def blocks(w, order):
    k, m = w.shape[0] // P, w.shape[1] // P
    b = w.reshape(k, P, m, P)
    return b.transpose((1, 2, 0, 3) if order == "mk" else (1, 0, 2, 3)).reshape(P, -1)


def expert_pairs(w1, w2):
    a, b = blocks(w1, "mk"), blocks(w2, "km")
    order = [(a, 0), (a, 1), (b, 0), (a, 2), (b, 1), (b, 2), (a, 3), (b, 3)]
    return [m[:, TILE * p:TILE * (p + 1)] for m, p in order]


def attention_weights(wq, wk, wv, wo):
    return [blocks(wq, "mk"), blocks(wk, "mk"), blocks(wv, "km"), blocks(wo, "mk")]


def kernel(**inputs):
    import concourse.bacc as bacc
    from concourse.bass_utils import run_bass_kernel_spmd

    a = {k: np.asarray(v) for k, v in inputs.items()}
    patches = a["x"].reshape(HALVES, HI, 3, 6, 16, 6, 16).transpose(0, 2, 4, 6, 1, 3, 5)
    patches = patches.reshape(HALVES, KP, P, NT).transpose(0, 2, 1, 3)

    parts = [blocks(a["L0_tok_W1"], "mk"), blocks(a["L0_tok_W2"], "mk")]
    qkv = a["L0_attn_qkv_w"]
    parts += attention_weights(qkv[:, 0:D], qkv[:, D:2 * D], qkv[:, 2 * D:], a["L0_attn_out_w"])
    parts += expert_pairs(a["L0_attn_w1"], a["L0_attn_w2"])
    ups = list(a["L0_ffn_shared_up"]) + list(a["L0_ffn_routed_up"])
    downs = list(a["L0_ffn_shared_down"]) + list(a["L0_ffn_routed_down"])
    for up, down in zip(ups, downs):
        parts += [blocks(up.T, "mk"), blocks(down.T, "mk")]
    parts += [blocks(a[f"L1_attn_W{n}"].T, "km") for n in "qkv"] + [blocks(a["L1_attn_Wo"].T, "mk")]
    for e in range(EXPERTS):
        qkv = a["L1_ffn_in_proj_w"][e]
        parts += attention_weights(qkv[0:D].T, qkv[D:2 * D].T, qkv[2 * D:].T, a["L1_ffn_out_proj_w"][e].T)
        parts += expert_pairs(a["L1_ffn_lin1_w"][e].T, a["L1_ffn_lin2_w"][e].T)

    vectors = {"tok_b1": a["L0_tok_b1"], "tok_b2": a["L0_tok_b2"], "l0_qk_b": a["L0_attn_qkv_b"][0:2 * D],
               "l0_out_b": a["L0_attn_out_b"], "l0_b1": a["L0_attn_b1"], "l0_b2": a["L0_attn_b2"],
               "g1": a["L0_attn_g1"], "be1": a["L0_attn_be1"], "g2": a["L0_attn_g2"], "be2": a["L0_attn_be2"],
               "l1_out_b": a["L1_attn_bo"]}
    vbias = [a["L0_attn_qkv_b"][2 * D:]]
    for e in range(EXPERTS):
        f = {n: a[f"L1_ffn_{n}"][e] for n in ("in_proj_b", "out_proj_b", "lin1_b", "lin2_b", "ln1_w", "ln1_b",
                                              "ln2_w", "ln2_b")}
        vectors |= {f"e{e}_qk_b": f["in_proj_b"][0:2 * D], f"e{e}_out_b": f["out_proj_b"], f"e{e}_b1": f["lin1_b"],
                    f"e{e}_b2": f["lin2_b"], f"e{e}_g1": f["ln1_w"], f"e{e}_be1": f["ln1_b"],
                    f"e{e}_g2": f["ln2_w"], f"e{e}_be2": f["ln2_b"]}
        vbias.append(f["in_proj_b"][2 * D:])
    bcol, _ = bias_columns()
    biases = np.concatenate([vectors[n].reshape(k, P).T for n, (_, k) in bcol.items()], axis=1)

    arrays = {
        "patches": patches,
        "weights": np.concatenate(parts, axis=1),
        "biases": biases,
        "vbias": np.stack(vbias),
        "hbias": np.concatenate([a["L1_attn_bq"], a["L1_attn_bk"], a["L1_attn_bv"]]),
        "router": blocks_narrow(a["L0_ffn_router_w"].T),
        "gate": blocks_narrow(a["L1_ffn_gate_w"].T),
        "gate_b": a["L1_ffn_gate_b"],
        "constants": shape_constants(),
    }
    arrays = {f"in_{k}": np.ascontiguousarray(v) for k, v in arrays.items()}

    nc = bacc.Bacc("TRN2", target_bir_lowering=False, num_devices=1)
    args = [nc.dram_tensor(k, v.shape, mybir.dt.from_np(v.dtype), kind="ExternalInput").ap()
            for k, v in arrays.items()]
    out = nc.dram_tensor("out", (HALVES, P, C, NT), F32, kind="ExternalOutput").ap()
    mixed = nc.dram_tensor("mixed", (IMAGES, HD, TOK, HD), F32, kind="Internal").ap()
    build_tower(nc, *args, out, mixed)
    r = run_bass_kernel_spmd(nc, [arrays], core_ids=[0])
    got = r.results[0]["out"]
    return got.transpose(0, 3, 2, 1).reshape(IMAGES, TOK, D)


def blocks_narrow(w):
    return w.reshape(C, P, -1).transpose(1, 0, 2).reshape(P, -1)
```
